# Optimizing a Trainium2 kernel written in Bass

```python
import numpy as np
import jax
import jax.numpy as jnp

def _softmax(x, axis=-1):
    return jax.nn.softmax(x, axis=axis)

def _gelu(x):
    return jax.nn.gelu(x, approximate=True)

def _silu(x):
    return jax.nn.silu(x)

def _sigmoid(x):
    return jax.nn.sigmoid(x)

def _layernorm(x, axis=-1, eps=1e-05):
    m = jnp.mean(x, axis=axis, keepdims=True)
    v = jnp.var(x, axis=axis, keepdims=True)
    return (x - m) / jnp.sqrt(v + eps)

def _scatter_add(tgt, idx, src, axis=0):
    return tgt.at[idx].add(src)

def _segment_sum(src, seg, n):
    return jax.ops.segment_sum(src, seg, n)
kernel_name = 'mk_seq_preln_d2_jaxref_r8_8b1059'

def setup_inputs(seed: int=0):
    np.random.seed(seed)
    _w = jnp.asarray

    def _L0_attn_setup():
        import jax, jax.numpy as jnp
        import numpy as np
        D_MODEL = 128
        N_HEADS = 16
        HEAD_DIM = D_MODEL // N_HEADS
        WINDOW = 128
        LOCAL_BLOCK = 32
        LATENT_TOKENS = 64
        LATENT_D = 32
        LATENT_HEADS = 4
        LATENT_HD = LATENT_D // LATENT_HEADS
        NEG = -1000000000.0

        def _local_attention(q, k, v):
            B, H, S, hd = q.shape
            bs = min(S, max(WINDOW, LOCAL_BLOCK))
            nb = S // bs
            w = WINDOW
            L = bs + w - 1
            k_pad = jnp.pad(k, ((0, 0), (0, 0), (w - 1, 0), (0, 0)))
            v_pad = jnp.pad(v, ((0, 0), (0, 0), (w - 1, 0), (0, 0)))
            starts = jnp.arange(nb) * bs
            idx = starts[:, None] + jnp.arange(L)[None, :]
            kb = k_pad[:, :, idx]
            vb = v_pad[:, :, idx]
            qb = q.reshape(B, H, nb, bs, hd)
            q_pos = starts[:, None] + jnp.arange(bs)[None, :]
            k_gpos = starts[:, None] + jnp.arange(L)[None, :] - (w - 1)
            dist = q_pos[:, :, None] - k_gpos[:, None, :]
            allowed = (dist > 0) & (dist <= w) & (k_gpos[:, None, :] >= 0)
            scale = 1.0 / np.sqrt(hd)
            scores = jnp.einsum('bhnqd,bhnkd->bhnqk', qb, kb) * scale
            scores = jnp.where(allowed, scores, NEG)
            attn = jax.nn.softmax(scores, axis=-1)
            attn = jnp.where(allowed.any(-1)[None, None, :, :, None], attn, 0.0)
            out = jnp.einsum('bhnqk,bhnkd->bhnqd', attn, vb)
            return out.reshape(B, H, S, hd)
        key = jax.random.key(seed)
        ks = jax.random.split(key, 14)
        B, S = (2, 512)
        s = 0.02
        f32 = jnp.float32
        return {'x': jax.random.normal(ks[0], (B, S, D_MODEL), f32), 'qkv_w': jax.random.normal(ks[1], (D_MODEL, 3 * D_MODEL), f32) * s, 'qkv_b': jnp.zeros((3 * D_MODEL,), f32), 'rq_w': jax.random.normal(ks[2], (D_MODEL, LATENT_D), f32) * s, 'rq_b': jnp.zeros((LATENT_D,), f32), 'rkv_w': jax.random.normal(ks[3], (D_MODEL, 2 * LATENT_D), f32) * s, 'rkv_b': jnp.zeros((2 * LATENT_D,), f32), 'rout_w': jax.random.normal(ks[4], (LATENT_D, D_MODEL), f32) * s, 'rout_b': jnp.zeros((D_MODEL,), f32), 'out_w': jax.random.normal(ks[5], (D_MODEL, D_MODEL), f32) * s, 'out_b': jnp.zeros((D_MODEL,), f32), 'gl_w': jax.random.normal(ks[6], (HEAD_DIM, 1), f32) * s, 'gr_w': jax.random.normal(ks[7], (HEAD_DIM, 1), f32) * s}
    _L0_attn_in = _L0_attn_setup()

    def _L0_ffn_setup():
        import jax, jax.numpy as jnp
        import numpy as np
        H = 128
        I = 352
        E = 8
        TOP_K = 2

        def _moe(hidden_states, router_w, gate_w, up_w, down_w):
            B, S, Hd = hidden_states.shape
            x = hidden_states.reshape(-1, Hd)
            logits = x @ router_w.T
            probs = jax.nn.softmax(logits.astype(jnp.float32), axis=-1)
            top_w, top_idx = jax.lax.top_k(probs, TOP_K)
            top_w = top_w.astype(x.dtype)
            onehot = jax.nn.one_hot(top_idx, E, dtype=x.dtype)
            w_te = jnp.einsum('tk,tke->te', top_w, onehot)
            g = jnp.einsum('th,eih->tei', x, gate_w)
            u = jnp.einsum('th,eih->tei', x, up_w)
            h = jax.nn.silu(g) * u
            y = jnp.einsum('tei,ehi,te->th', h, down_w, w_te)
            return y.reshape(B, S, Hd)
        key = jax.random.key(seed)
        ks = jax.random.split(key, 5)
        s = 0.02
        return {'hidden_states': jax.random.normal(ks[0], (2, 128, H), dtype=jnp.float32), 'router_w': jax.random.normal(ks[1], (E, H), dtype=jnp.float32) * s, 'gate_w': jax.random.normal(ks[2], (E, I, H), dtype=jnp.float32) * s, 'up_w': jax.random.normal(ks[3], (E, I, H), dtype=jnp.float32) * s, 'down_w': jax.random.normal(ks[4], (E, H, I), dtype=jnp.float32) * s}
    _L0_ffn_in = _L0_ffn_setup()

    def _L1_attn_setup():
        import jax, jax.numpy as jnp
        import numpy as np
        from jax import lax
        D_MODEL = 128
        STATE_DIM = 64
        BATCH = 4
        SEQ_LEN = 1024

        def _cayley_eigenvalues(a_params, n):
            half = n // 2
            a_full = jnp.zeros((n,), dtype=a_params.dtype)
            a_full = a_full.at[1:half + 1].set(a_params)
            a_full = a_full.at[half + 1:].set(-a_params[::-1][:n - half - 1])
            a_hat = jnp.fft.fft(a_full)
            omega = jnp.imag(a_hat)
            ones = jnp.ones_like(omega)
            num = lax.complex(ones, -omega)
            den = lax.complex(ones, omega)
            return num / den
        key = jax.random.key(seed)
        k1, k2, k3, k4 = jax.random.split(key, 4)
        u = jax.random.normal(k1, (BATCH, SEQ_LEN, D_MODEL), dtype=jnp.float32)
        a_params = jax.random.normal(k2, (STATE_DIM // 2,), dtype=jnp.float32) * 0.1
        B_w = jax.random.normal(k3, (STATE_DIM, D_MODEL), dtype=jnp.float32) / np.sqrt(D_MODEL)
        C_w = jax.random.normal(k4, (D_MODEL, STATE_DIM), dtype=jnp.float32) / np.sqrt(STATE_DIM)
        D = jnp.ones((D_MODEL,), dtype=jnp.float32)
        return {'u': u, 'a_params': a_params, 'B_w': B_w, 'C_w': C_w, 'D': D}
    _L1_attn_in = _L1_attn_setup()

    def _L1_ffn_setup():
        import jax, jax.numpy as jnp
        import numpy as np
        DIM = 128
        DEPTH = 2
        HEADS = 8
        DIM_HEAD = 64
        WINDOW = 64
        INNER = HEADS * DIM_HEAD
        HID = int(DIM * 4 * 2 / 3)
        B, N = (2, 1024)
        QK_SCALE = 8.0

        def shift_token(t):
            t1, t2 = jnp.split(t, 2, axis=-1)
            t2 = jnp.pad(t2, ((0, 0), (1, 0), (0, 0)))[:, :-1]
            return jnp.concatenate([t1, t2], axis=-1)

        def l2norm(t):
            return t / jnp.clip(jnp.linalg.norm(t, axis=-1, keepdims=True), 1e-12)

        def rotate_half(x):
            x1, x2 = jnp.split(x, 2, axis=-1)
            return jnp.concatenate([-x2, x1], axis=-1)

        def rotary_xpos(q, k):
            n = q.shape[-2]
            half_idx = jnp.arange(0, DIM_HEAD, 2, dtype=jnp.float32)
            inv_freq = 1.0 / 10000.0 ** (half_idx / DIM_HEAD)
            t = jnp.arange(n, dtype=jnp.float32)
            freqs = t[:, None] * inv_freq[None, :]
            freqs = jnp.concatenate([freqs, freqs], axis=-1)
            base = (half_idx + 0.4 * DIM_HEAD) / (1.4 * DIM_HEAD)
            power = (t - n // 2) / float(WINDOW // 2)
            scale = base[None, :] ** power[:, None]
            scale = jnp.concatenate([scale, scale], axis=-1)
            cos, sin = (jnp.cos(freqs), jnp.sin(freqs))
            q = q * cos * scale + rotate_half(q) * sin * scale
            k = k * cos / scale + rotate_half(k) * sin / scale
            return (q, k)

        def local_attention(q, k, v):
            b, h, n, d = q.shape
            w = n // WINDOW
            bq = q.reshape(b, h, w, WINDOW, d) * QK_SCALE
            bk = k.reshape(b, h, w, WINDOW, d)
            bv = v.reshape(b, h, w, WINDOW, d)

            def look_around(t):
                p = jnp.pad(t, ((0, 0), (0, 0), (1, 0), (0, 0), (0, 0)))
                return jnp.concatenate([p[:, :, :w], p[:, :, 1:]], axis=3)
            bk, bv = (look_around(bk), look_around(bv))
            bt = jnp.arange(n).reshape(w, WINDOW)
            btp = jnp.pad(bt, ((1, 0), (0, 0)), constant_values=-1)
            btk = jnp.concatenate([btp[:w], btp[1:]], axis=1)
            sim = jnp.einsum('bhwid,bhwjd->bhwij', bq, bk)
            i = bt[:, :, None]
            j = btk[:, None, :]
            mask = (i < j) | (i > j + WINDOW) | (j == -1)
            sim = jnp.where(mask, -jnp.finfo(sim.dtype).max, sim)
            attn = jax.nn.softmax(sim, axis=-1)
            out = jnp.einsum('bhwij,bhwjd->bhwid', attn, bv)
            return out.reshape(b, h, n, d)

        def _layer(x, wqkv, qs, ksc, wo, lg, lb, w1, b1, w2, b2):
            b, n, _ = x.shape
            h = shift_token(x)
            qkv = h @ wqkv
            q, k, v = jnp.split(qkv, 3, axis=-1)
            to_heads = lambda t: t.reshape(b, n, HEADS, DIM_HEAD).transpose(0, 2, 1, 3)
            q, k, v = (to_heads(q), to_heads(k), to_heads(v))
            q = l2norm(q) * qs
            k = l2norm(k) * ksc
            q, k = rotary_xpos(q, k)
            o = local_attention(q, k, v)
            o = o.transpose(0, 2, 1, 3).reshape(b, n, INNER)
            x = x + o @ wo
            h = shift_token(x)
            mu = h.mean(-1, keepdims=True)
            var = h.var(-1, keepdims=True)
            h = (h - mu) / jnp.sqrt(var + 1e-05) * lg + lb
            h = h @ w1 + b1
            a, g = jnp.split(h, 2, axis=-1)
            h = a * jax.nn.gelu(g, approximate=False)
            x = x + h @ w2 + b2
            return x
        key = jax.random.key(seed)
        ks = jax.random.split(key, 6)
        return {'x': jax.random.normal(ks[0], (B, N, DIM), jnp.float32), 'wqkv': jax.random.normal(ks[1], (DEPTH, DIM, 3 * INNER), jnp.float32) * 0.02, 'q_scale': jnp.ones((DEPTH, DIM_HEAD), jnp.float32), 'k_scale': jnp.ones((DEPTH, DIM_HEAD), jnp.float32), 'wo': jax.random.normal(ks[2], (DEPTH, INNER, DIM), jnp.float32) * 0.02, 'ln_g': jnp.ones((DEPTH, DIM), jnp.float32), 'ln_b': jnp.zeros((DEPTH, DIM), jnp.float32), 'w1': jax.random.normal(ks[3], (DEPTH, DIM, 2 * HID), jnp.float32) * 0.02, 'b1': jnp.zeros((DEPTH, 2 * HID), jnp.float32), 'w2': jax.random.normal(ks[4], (DEPTH, HID, DIM), jnp.float32) * 0.02, 'b2': jnp.zeros((DEPTH, DIM), jnp.float32)}
    _L1_ffn_in = _L1_ffn_setup()
    _d = {'L0_attn_x': _L0_attn_in['x'], 'L0_attn_qkv_w': _L0_attn_in['qkv_w'], 'L0_attn_qkv_b': _L0_attn_in['qkv_b'], 'L0_attn_rq_w': _L0_attn_in['rq_w'], 'L0_attn_rq_b': _L0_attn_in['rq_b'], 'L0_attn_rkv_w': _L0_attn_in['rkv_w'], 'L0_attn_rkv_b': _L0_attn_in['rkv_b'], 'L0_attn_rout_w': _L0_attn_in['rout_w'], 'L0_attn_rout_b': _L0_attn_in['rout_b'], 'L0_attn_out_w': _L0_attn_in['out_w'], 'L0_attn_out_b': _L0_attn_in['out_b'], 'L0_attn_gl_w': _L0_attn_in['gl_w'], 'L0_attn_gr_w': _L0_attn_in['gr_w'], 'L0_ffn_router_w': _L0_ffn_in['router_w'], 'L0_ffn_gate_w': _L0_ffn_in['gate_w'], 'L0_ffn_up_w': _L0_ffn_in['up_w'], 'L0_ffn_down_w': _L0_ffn_in['down_w'], 'L1_attn_a_params': _L1_attn_in['a_params'], 'L1_attn_B_w': _L1_attn_in['B_w'], 'L1_attn_C_w': _L1_attn_in['C_w'], 'L1_attn_D': _L1_attn_in['D'], 'L1_ffn_wqkv': _L1_ffn_in['wqkv'], 'L1_ffn_q_scale': _L1_ffn_in['q_scale'], 'L1_ffn_k_scale': _L1_ffn_in['k_scale'], 'L1_ffn_wo': _L1_ffn_in['wo'], 'L1_ffn_ln_g': _L1_ffn_in['ln_g'], 'L1_ffn_ln_b': _L1_ffn_in['ln_b'], 'L1_ffn_w1': _L1_ffn_in['w1'], 'L1_ffn_b1': _L1_ffn_in['b1'], 'L1_ffn_w2': _L1_ffn_in['w2'], 'L1_ffn_b2': _L1_ffn_in['b2']}
    _x0 = _d['L0_attn_x']
    _d['L0_attn_x'] = jax.random.normal(jax.random.fold_in(jax.random.key(seed), 1), (8, 512, 128), dtype=_x0.dtype)
    del _x0
    return _d

def reference(L0_attn_x, L0_attn_qkv_w, L0_attn_qkv_b, L0_attn_rq_w, L0_attn_rq_b, L0_attn_rkv_w, L0_attn_rkv_b, L0_attn_rout_w, L0_attn_rout_b, L0_attn_out_w, L0_attn_out_b, L0_attn_gl_w, L0_attn_gr_w, L0_ffn_router_w, L0_ffn_gate_w, L0_ffn_up_w, L0_ffn_down_w, L1_attn_a_params, L1_attn_B_w, L1_attn_C_w, L1_attn_D, L1_ffn_wqkv, L1_ffn_q_scale, L1_ffn_k_scale, L1_ffn_wo, L1_ffn_ln_g, L1_ffn_ln_b, L1_ffn_w1, L1_ffn_b1, L1_ffn_w2, L1_ffn_b2):

    def _L0_attn_ref(x, qkv_w, qkv_b, rq_w, rq_b, rkv_w, rkv_b, rout_w, rout_b, out_w, out_b, gl_w, gr_w):
        import jax, jax.numpy as jnp
        import numpy as np
        D_MODEL = 128
        N_HEADS = 16
        HEAD_DIM = D_MODEL // N_HEADS
        WINDOW = 128
        LOCAL_BLOCK = 32
        LATENT_TOKENS = 64
        LATENT_D = 32
        LATENT_HEADS = 4
        LATENT_HD = LATENT_D // LATENT_HEADS
        NEG = -1000000000.0

        def _local_attention(q, k, v):
            B, H, S, hd = q.shape
            bs = min(S, max(WINDOW, LOCAL_BLOCK))
            nb = S // bs
            w = WINDOW
            L = bs + w - 1
            k_pad = jnp.pad(k, ((0, 0), (0, 0), (w - 1, 0), (0, 0)))
            v_pad = jnp.pad(v, ((0, 0), (0, 0), (w - 1, 0), (0, 0)))
            starts = jnp.arange(nb) * bs
            idx = starts[:, None] + jnp.arange(L)[None, :]
            kb = k_pad[:, :, idx]
            vb = v_pad[:, :, idx]
            qb = q.reshape(B, H, nb, bs, hd)
            q_pos = starts[:, None] + jnp.arange(bs)[None, :]
            k_gpos = starts[:, None] + jnp.arange(L)[None, :] - (w - 1)
            dist = q_pos[:, :, None] - k_gpos[:, None, :]
            allowed = (dist > 0) & (dist <= w) & (k_gpos[:, None, :] >= 0)
            scale = 1.0 / np.sqrt(hd)
            scores = jnp.einsum('bhnqd,bhnkd->bhnqk', qb, kb) * scale
            scores = jnp.where(allowed, scores, NEG)
            attn = jax.nn.softmax(scores, axis=-1)
            attn = jnp.where(allowed.any(-1)[None, None, :, :, None], attn, 0.0)
            out = jnp.einsum('bhnqk,bhnkd->bhnqd', attn, vb)
            return out.reshape(B, H, S, hd)
        B, S, D = x.shape
        qkv = x @ qkv_w + qkv_b
        q, k, v = jnp.split(qkv, 3, axis=-1)

        def heads(t):
            return t.reshape(B, S, N_HEADS, HEAD_DIM).transpose(0, 2, 1, 3)
        local = _local_attention(heads(q), heads(k), heads(v))
        chunk = -(-S // min(LATENT_TOKENS, S))
        nlat = S // chunk
        pooled = x.reshape(B, nlat, chunk, D).mean(axis=2)
        chunk_ids = jnp.arange(S) // chunk
        rq = (x @ rq_w + rq_b).reshape(B, S, LATENT_HEADS, LATENT_HD).transpose(0, 2, 1, 3)
        rkv = pooled @ rkv_w + rkv_b
        rk, rv = jnp.split(rkv, 2, axis=-1)
        rk = rk.reshape(B, nlat, LATENT_HEADS, LATENT_HD).transpose(0, 2, 1, 3)
        rv = rv.reshape(B, nlat, LATENT_HEADS, LATENT_HD).transpose(0, 2, 1, 3)
        lscale = 1.0 / np.sqrt(LATENT_HD)
        lscores = jnp.einsum('bhsd,bhld->bhsl', rq, rk) * lscale
        lat_allowed = jnp.arange(nlat)[None, :] < chunk_ids[:, None]
        lscores = jnp.where(lat_allowed[None, None], lscores, NEG)
        lattn = jax.nn.softmax(lscores, axis=-1)
        lattn = jnp.where(lat_allowed.any(-1)[None, None, :, None], lattn, 0.0)
        lat_out = jnp.einsum('bhsl,bhld->bhsd', lattn, rv)
        lat_out = lat_out.transpose(0, 2, 1, 3).reshape(B, S, LATENT_D)
        remote = lat_out @ rout_w + rout_b
        remote_h = remote.reshape(B, S, N_HEADS, HEAD_DIM).transpose(0, 2, 1, 3)
        gate = jax.nn.sigmoid(local @ gl_w + remote_h @ gr_w)
        mixed = gate * local + (1.0 - gate) * remote_h
        mixed = mixed.transpose(0, 2, 1, 3).reshape(B, S, D)
        return mixed @ out_w + out_b

    def _L0_ffn_ref(hidden_states, router_w, gate_w, up_w, down_w):
        import jax, jax.numpy as jnp
        import numpy as np
        H = 128
        I = 352
        E = 8
        TOP_K = 2

        def _moe(hidden_states, router_w, gate_w, up_w, down_w):
            B, S, Hd = hidden_states.shape
            x = hidden_states.reshape(-1, Hd)
            logits = x @ router_w.T
            probs = jax.nn.softmax(logits.astype(jnp.float32), axis=-1)
            top_w, top_idx = jax.lax.top_k(probs, TOP_K)
            top_w = top_w.astype(x.dtype)
            onehot = jax.nn.one_hot(top_idx, E, dtype=x.dtype)
            w_te = jnp.einsum('tk,tke->te', top_w, onehot)
            g = jnp.einsum('th,eih->tei', x, gate_w)
            u = jnp.einsum('th,eih->tei', x, up_w)
            h = jax.nn.silu(g) * u
            y = jnp.einsum('tei,ehi,te->th', h, down_w, w_te)
            return y.reshape(B, S, Hd)
        return _moe(hidden_states, router_w, gate_w, up_w, down_w)

    def _L1_attn_ref(u, a_params, B_w, C_w, D):
        import jax, jax.numpy as jnp
        import numpy as np
        from jax import lax
        D_MODEL = 128
        STATE_DIM = 64
        BATCH = 4
        SEQ_LEN = 1024

        def _cayley_eigenvalues(a_params, n):
            half = n // 2
            a_full = jnp.zeros((n,), dtype=a_params.dtype)
            a_full = a_full.at[1:half + 1].set(a_params)
            a_full = a_full.at[half + 1:].set(-a_params[::-1][:n - half - 1])
            a_hat = jnp.fft.fft(a_full)
            omega = jnp.imag(a_hat)
            ones = jnp.ones_like(omega)
            num = lax.complex(ones, -omega)
            den = lax.complex(ones, omega)
            return num / den
        batch, seq_len, d = u.shape
        n = B_w.shape[0]
        Bu = jnp.einsum('btd,nd->btn', u, B_w)
        eig = _cayley_eigenvalues(a_params, n)
        t = jnp.arange(seq_len, dtype=jnp.float32)
        kernel = jnp.exp(t[:, None] * jnp.log(eig)[None, :])
        fft_len = 1
        while fft_len < 2 * seq_len:
            fft_len *= 2
        pad = fft_len - seq_len
        kernel_padded = jnp.pad(kernel, ((0, pad), (0, 0)))
        K_hat = jnp.fft.fft(kernel_padded, axis=0)
        Bu_padded = jnp.pad(Bu, ((0, 0), (0, pad), (0, 0))).astype(jnp.complex64)
        Bu_hat = jnp.fft.fft(Bu_padded, axis=1)
        h = jnp.fft.ifft(K_hat[None] * Bu_hat, axis=1).real[:, :seq_len, :]
        y = jnp.einsum('btn,dn->btd', h, C_w) + D * u
        return y

    def _L1_ffn_ref(x, wqkv, q_scale, k_scale, wo, ln_g, ln_b, w1, b1, w2, b2):
        import jax, jax.numpy as jnp
        import numpy as np
        DIM = 128
        DEPTH = 2
        HEADS = 8
        DIM_HEAD = 64
        WINDOW = 64
        INNER = HEADS * DIM_HEAD
        HID = int(DIM * 4 * 2 / 3)
        B, N = (2, 1024)
        QK_SCALE = 8.0

        def shift_token(t):
            t1, t2 = jnp.split(t, 2, axis=-1)
            t2 = jnp.pad(t2, ((0, 0), (1, 0), (0, 0)))[:, :-1]
            return jnp.concatenate([t1, t2], axis=-1)

        def l2norm(t):
            return t / jnp.clip(jnp.linalg.norm(t, axis=-1, keepdims=True), 1e-12)

        def rotate_half(x):
            x1, x2 = jnp.split(x, 2, axis=-1)
            return jnp.concatenate([-x2, x1], axis=-1)

        def rotary_xpos(q, k):
            n = q.shape[-2]
            half_idx = jnp.arange(0, DIM_HEAD, 2, dtype=jnp.float32)
            inv_freq = 1.0 / 10000.0 ** (half_idx / DIM_HEAD)
            t = jnp.arange(n, dtype=jnp.float32)
            freqs = t[:, None] * inv_freq[None, :]
            freqs = jnp.concatenate([freqs, freqs], axis=-1)
            base = (half_idx + 0.4 * DIM_HEAD) / (1.4 * DIM_HEAD)
            power = (t - n // 2) / float(WINDOW // 2)
            scale = base[None, :] ** power[:, None]
            scale = jnp.concatenate([scale, scale], axis=-1)
            cos, sin = (jnp.cos(freqs), jnp.sin(freqs))
            q = q * cos * scale + rotate_half(q) * sin * scale
            k = k * cos / scale + rotate_half(k) * sin / scale
            return (q, k)

        def local_attention(q, k, v):
            b, h, n, d = q.shape
            w = n // WINDOW
            bq = q.reshape(b, h, w, WINDOW, d) * QK_SCALE
            bk = k.reshape(b, h, w, WINDOW, d)
            bv = v.reshape(b, h, w, WINDOW, d)

            def look_around(t):
                p = jnp.pad(t, ((0, 0), (0, 0), (1, 0), (0, 0), (0, 0)))
                return jnp.concatenate([p[:, :, :w], p[:, :, 1:]], axis=3)
            bk, bv = (look_around(bk), look_around(bv))
            bt = jnp.arange(n).reshape(w, WINDOW)
            btp = jnp.pad(bt, ((1, 0), (0, 0)), constant_values=-1)
            btk = jnp.concatenate([btp[:w], btp[1:]], axis=1)
            sim = jnp.einsum('bhwid,bhwjd->bhwij', bq, bk)
            i = bt[:, :, None]
            j = btk[:, None, :]
            mask = (i < j) | (i > j + WINDOW) | (j == -1)
            sim = jnp.where(mask, -jnp.finfo(sim.dtype).max, sim)
            attn = jax.nn.softmax(sim, axis=-1)
            out = jnp.einsum('bhwij,bhwjd->bhwid', attn, bv)
            return out.reshape(b, h, n, d)

        def _layer(x, wqkv, qs, ksc, wo, lg, lb, w1, b1, w2, b2):
            b, n, _ = x.shape
            h = shift_token(x)
            qkv = h @ wqkv
            q, k, v = jnp.split(qkv, 3, axis=-1)
            to_heads = lambda t: t.reshape(b, n, HEADS, DIM_HEAD).transpose(0, 2, 1, 3)
            q, k, v = (to_heads(q), to_heads(k), to_heads(v))
            q = l2norm(q) * qs
            k = l2norm(k) * ksc
            q, k = rotary_xpos(q, k)
            o = local_attention(q, k, v)
            o = o.transpose(0, 2, 1, 3).reshape(b, n, INNER)
            x = x + o @ wo
            h = shift_token(x)
            mu = h.mean(-1, keepdims=True)
            var = h.var(-1, keepdims=True)
            h = (h - mu) / jnp.sqrt(var + 1e-05) * lg + lb
            h = h @ w1 + b1
            a, g = jnp.split(h, 2, axis=-1)
            h = a * jax.nn.gelu(g, approximate=False)
            x = x + h @ w2 + b2
            return x
        for l in range(DEPTH):
            x = _layer(x, wqkv[l], q_scale[l], k_scale[l], wo[l], ln_g[l], ln_b[l], w1[l], b1[l], w2[l], b2[l])
        return x
    x = L0_attn_x
    x = x + _L0_attn_ref(_layernorm(x, axis=-1), L0_attn_qkv_w, L0_attn_qkv_b, L0_attn_rq_w, L0_attn_rq_b, L0_attn_rkv_w, L0_attn_rkv_b, L0_attn_rout_w, L0_attn_rout_b, L0_attn_out_w, L0_attn_out_b, L0_attn_gl_w, L0_attn_gr_w)
    x = x + _L0_ffn_ref(_layernorm(x, axis=-1), L0_ffn_router_w, L0_ffn_gate_w, L0_ffn_up_w, L0_ffn_down_w)
    x = x + _L1_attn_ref(_layernorm(x, axis=-1), L1_attn_a_params, L1_attn_B_w, L1_attn_C_w, L1_attn_D)
    x = x + _L1_ffn_ref(_layernorm(x, axis=-1), L1_ffn_wqkv, L1_ffn_q_scale, L1_ffn_k_scale, L1_ffn_wo, L1_ffn_ln_g, L1_ffn_ln_b, L1_ffn_w1, L1_ffn_b1, L1_ffn_w2, L1_ffn_b2)
    return x

_drawn_inputs = setup_inputs


def setup_inputs(seed=0):
    import zlib

    import numpy as np

    out = dict(_drawn_inputs(seed))
    spreads = {'L0_attn_qkv_b': (0.0, 0.287),
     'L0_attn_rq_b': (0.0, 0.8),
     'L0_attn_rkv_b': (0.0, 0.8),
     'L0_attn_rout_b': (0.0, 0.1),
     'L0_attn_out_b': (0.0, 0.1),
     'L1_attn_D': (1.0, 0.6),
     'L1_ffn_q_scale': (1.0, 0.6),
     'L1_ffn_k_scale': (1.0, 0.6),
     'L1_ffn_ln_g': (1.0, 0.6),
     'L1_ffn_ln_b': (0.0, 0.8),
     'L1_ffn_b1': (0.0, 0.8),
     'L1_ffn_b2': (0.0, 0.698)}
    factors = {'L0_attn_qkv_w': 5.232,
     'L0_attn_rq_w': 8.0,
     'L0_attn_rkv_w': 8.0,
     'L0_attn_rout_w': 8.0,
     'L0_attn_gl_w': 8.0,
     'L0_attn_gr_w': 8.0,
     'L0_ffn_router_w': 8.0,
     'L0_ffn_gate_w': 8.0,
     'L0_ffn_up_w': 8.0,
     'L0_ffn_down_w': 8.0,
     'L1_ffn_wqkv': 8.0,
     'L1_ffn_wo': 8.0,
     'L1_ffn_w1': 8.0,
     'L1_ffn_w2': 8.0}
    for name, (base, spread) in spreads.items():
        noise = np.random.default_rng([zlib.crc32(name.encode()), seed]).standard_normal(out[name].shape)
        drawn = base * np.exp(spread * noise) if base else spread * noise
        out[name] = jnp.asarray(drawn.astype(out[name].dtype))
    for name, factor in factors.items():
        out[name] = (out[name] * factor).astype(out[name].dtype)
    return out
```

```python
from contextlib import ExitStack

import numpy as np

import concourse.bass as bass
from concourse import mybir

F32 = mybir.dt.float32
F32R = mybir.dt.float32r
I32 = mybir.dt.int32
ALU = mybir.AluOpType
ACT = mybir.ActivationFunctionType
AX_X = mybir.AxisListType.X

P = 128
NT = 4
S = NT * P
EPS = 1e-5
NEG = -1e30
SLOT = 32
HD0 = 8
NH0 = 16
NG0 = NH0 // 4
NLAT = 64
LH = 4
NE = 8
FI = 352
E_CHUNKS = [(0, 128), (128, 128), (256, 96)]
NCH = NE * len(E_CHUNKS)
NW = 8
W = 64
NP = 4
INNER = 512
HID = 341
H_CHUNKS = [(0, 128), (128, 128), (256, 85)]
QK_SCALE = 8.0


def build(nc, io, n_batch, out):
    with ExitStack() as ctx:
        def sb(name, shape, dt=F32):
            return ctx.enter_context(nc.sbuf_tensor(name, shape, dt))

        def sem(name):
            return ctx.enter_context(nc.semaphore(name))

        resident = {}

        def keep(name, shape, dt=F32):
            resident[name] = sb(name, shape, dt)
            return resident[name]

        ident = keep("ident", [P, P])
        wqk = keep("wqk", [P, 8, P])
        bqk = keep("bqk", [P, 8])
        low_rows = keep("low_rows", [P, 8])
        wv0 = keep("wv0", [P, P])
        rq_w = keep("rq_w", [P, 32])
        rq_b = keep("rq_b", [32, 1])
        rk_w = keep("rk_w", [P, 32])
        rk_b = keep("rk_b", [32, 1])
        rv_w = keep("rv_w", [P, 32])
        rout_w = keep("rout_w", [32, P])
        out_w = keep("out_w", [P, P])
        take_prev = keep("take_prev", [P, 4, P], I32)
        key_before = keep("key_before", [P, P])
        key_after = keep("key_after", [P, P])
        lat_mask = keep("lat_mask", [P, NT, NLAT])
        lat_valid = keep("lat_valid", [P, NT])
        own_head = keep("own_head", [32, LH])
        own_half = keep("own_half", [P, 2])
        router = keep("router", [P, NE])
        gate_w = keep("gate_w", [P, NE * FI])
        up_w = keep("up_w", [P, NE * FI])
        down_w = keep("down_w", [P, NCH, P])
        lower_index = keep("lower_index", [P, NE * NE])
        bw2 = keep("bw2", [P, P])
        cw2 = keep("cw2", [P, P])
        omega_w = keep("omega_w", [32, P])
        a_col = keep("a_col", [32, 1])
        up_to = keep("up_to", [P, S])
        wqkv = [keep(f"wqkv{l}", [P, 3, INNER]) for l in range(2)]
        wo = [keep(f"wo{l}", [P, NP, P]) for l in range(2)]
        w1 = [keep(f"w1_{l}", [P, 2 * HID]) for l in range(2)]
        w2 = [keep(f"w2_{l}", [P, 3, P]) for l in range(2)]
        b1a = [keep(f"b1a{l}", [P, 3]) for l in range(2)]
        b1g = [keep(f"b1g{l}", [P, 3]) for l in range(2)]
        ln_g = [keep(f"ln_g{l}", [P, 1]) for l in range(2)]
        ln_b = [keep(f"ln_b{l}", [P, 1]) for l in range(2)]
        win_mask = keep("win_mask", [P, 3, P])
        rows = {}

        def keep_row(name, n):
            rows[name] = sb("row_" + name, [P, n])
            return rows[name]

        v_b = keep_row("v_b", P)
        rv_b = keep_row("rv_b", 32)
        rout_b = keep_row("rout_b", P)
        out_b = keep_row("out_b", P)
        gl = keep_row("gl", HD0)
        gr = keep_row("gr", HD0)
        d_row = keep_row("d_row", P)
        qk_s = [[keep_row(f"qk_s{l}{i}", W) for i in range(2)] for l in range(2)]
        b2 = [keep_row(f"b2_{l}", P) for l in range(2)]

        never = sb("never", [P, 4, P])
        eps4 = sb("eps4", [P, NT])
        minus_half = sb("minus_half", [P, NT])
        low_bias = sb("low_bias", [P, 8])
        omega = sb("omega", [P, 1])
        pw = sb("pw", [P, 12])
        turn_t = sb("turn_t", [P, S])
        turn = sb("turn", [P, NT, P])
        rope_c = [[sb(f"rope_c{l}{i}", [P, NT, W]) for i in range(2)] for l in range(2)]
        rope_s = [[sb(f"rope_s{l}{i}", [P, NT, W]) for i in range(2)] for l in range(2)]

        x = sb("x", [P, NT, P])
        y = sb("y", [P, NT, P])
        stats = sb("stats", [P, NT, 6])
        mv = sb("mv", [P, NT, 2])
        veps = sb("veps", [P, NT])
        rstd = sb("rstd", [P, NT])
        xn = sb("xn", [P, NT, P])
        xt = sb("xt", [P, S])
        shifted = sb("shifted", [P, NT, P])
        v0 = sb("v0", [P, NT, NH0, SLOT])
        tmp = [sb(f"tmp{i}", [P, S]) for i in range(6)]
        small = sb("small", [P, 8, 64])

        early = ExitStack()

        def sb(name, shape, dt=F32):
            return early.enter_context(nc.sbuf_tensor(name, shape, dt))

        cos_t = sb("cos_t", [P, S])
        sin_t = sb("sin_t", [P, S])
        rope = [sb(f"rope{i}", [P, NT, W]) for i in range(4)]
        for i in range(4):
            resident[f"rope{i}"] = rope[i]
        qk = sb("qk", [P, 8, S])
        low = sb("low", [P, 2, S])
        pool_t = sb("pool_t", [P, 2, NLAT])
        rqt = sb("rqt", [32, S])
        rk_row = sb("rk_row", [32, NLAT])
        rk_bd = sb("rk_bd", [32, LH, NLAT])
        rv_row = sb("rv_row", [P, 32])
        rv_bd = sb("rv_bd", [P, 2, 2, HD0])
        prob = sb("prob", [P, 3, 4, P])
        pt = sb("pt", [P, 2, 4, P])
        p_cur = sb("p_cur", [P, 2, 4, P])
        p_prev = sb("p_prev", [P, 2, 4, P])
        negmax = sb("negmax", [P, 2, 4])
        o_t = sb("o_t", [P, 2, P])
        loc = sb("loc", [P, NT, NH0, HD0 + 1])
        loc_r = sb("loc_r", [P, NT * NH0])
        lat_p = sb("lat_p", [P, NT * LH * NLAT])
        lat_t = sb("lat_t", [P, 8, P])
        lat_o = sb("lat_o", [P, NT, 32])
        lat_ot = sb("lat_ot", [32, S])
        remote = sb("remote", [P, S])

        w_te = sb("w_te", [P, NT, NE])
        hid = sb("hid", [P, 2, S])
        sil = sb("sil", [P, 2, S])

        early.close()

        def sb(name, shape, dt=F32):
            return ctx.enter_context(nc.sbuf_tensor(name, shape, dt))

        qr = sb("qr", [P, 8, S])
        qt = sb("qt", [P, 2, NP, S])
        vt = sb("vt", [P, NT, INNER])
        vte = sb("vte", [P, NT, INNER])
        ss = sb("ss", [P, 64])
        nw = sb("nw", [P, 5, 64])
        quad = sb("quad", [P, 4, S])
        sc, pn = quad[:, 0:2, :], quad[:, 2:4, :]
        mlp = quad[:, 0:3, :]
        wmax = sb("wmax", [P, 2, 12])
        ptw = sb("ptw", [P, 2, NP, P])
        ot = sb("ot", [P, NP, S])
        hn = sb("hn", [P, S])
        gel = sb("gel", [P, 3, S])

        ps = ctx.enter_context(nc.psum_tensor("ps", [P, 8, 512], F32))

        def b4(i):
            return ps[:, i, :].rearrange("p (t d) -> p t d", t=NT)

        loaded = sem("loaded")
        setup_dve = sem("setup_dve")
        setup_pe = sem("setup_pe")
        setup_done = sem("setup_done")
        next_turn = sem("next_turn")

        turn_sems = []

        def tsem(name):
            turn_sems.append(sem(name))
            return turn_sems[-1]

        turn_over = tsem("turn_over")
        x_loaded = tsem("x_loaded")
        x_stored = tsem("x_stored")
        dve_step = tsem("dve_step")
        act_step = tsem("act_step")
        pool_step = tsem("pool_step")
        NLN = 6
        var_ready = [tsem(f"var_ready{k}") for k in range(NLN)]
        rstd_ready = [tsem(f"rstd_ready{k}") for k in range(NLN)]
        xn_ready = [tsem(f"xn_ready{k}") for k in range(NLN)]
        xt_made = [tsem(f"xt_made{k}") for k in range(NLN)]
        xt_ready = [tsem(f"xt_ready{k}") for k in range(NLN)]
        qk_made, low_ready, qk_split, v0_made, v0_ready = (tsem(n) for n in (
            "qk_made", "low_ready", "qk_split", "v0_made", "v0_ready"))
        pooled, lat_made, rqt_ready, lat_split = (tsem(n) for n in ("pooled", "lat_made", "rqt_ready", "lat_split"))
        a_scores, a_shifted, a_probs, a_turned, a_pt, a_prev, a_cur, a_pv, a_ot, a_back, a_loc = (tsem(n) for n in (
            "a_scores", "a_shifted", "a_probs", "a_turned", "a_pt", "a_prev", "a_cur", "a_pv", "a_ot", "a_back",
            "a_loc"))
        l_scores, l_shifted, l_probs, l_turned, l_pt, l_out, l_norm, l_back, l_ot, l_remote = (tsem(n) for n in (
            "l_scores", "l_shifted", "l_probs", "l_turned", "l_pt", "l_out", "l_norm", "l_back", "l_ot", "l_remote"))
        rem_ready, g_rem, g_sum, g_gate, mixed_ready, mixed_made, mixed_t, a_proj, x1_ready = (tsem(n) for n in (
            "rem_ready", "g_rem", "g_sum", "g_gate", "mixed_ready", "mixed_made", "mixed_t", "a_proj", "x1_ready"))
        m_logits, m_shifted, m_exp, m_gate, m_silu, m_up, m_hid, m_down, m_added = (tsem(n) for n in (
            "m_logits", "m_shifted", "m_exp", "m_gate", "m_silu", "m_up", "m_hid", "m_down", "m_added"))
        s_in, s_turned, s_sum, s_state, s_skip, s_out, x3_ready = (tsem(n) for n in (
            "s_in", "s_turned", "s_sum", "s_state", "s_skip", "s_out", "x3_ready"))
        x4_ready = tsem("x4_ready")
        PER_LAYER = {"shift": 32, "shift2": 32, "left": 1, "left2": 1, "h_made": 1, "h_ready": 1, "v_made": NT,
                     "v_ready": NT, "vte": 32, "qk_made": 8, "sq": 8, "parts": 8, "rot": 8, "normed": 8,
                     "turned": 8, "qt_ready": 8, "scores": NW, "shifted": NW, "probs": NW, "wsum": NW,
                     "pnorm": NW, "pturn": NW, "ptw": NW, "pv": NW, "ot": NW, "wo": 1, "y_mid": 1, "ga": 3,
                     "gelu": 3, "mlp": 3, "w2": 1, "y_out": 1}
        d = {n: tsem(n if n != "qk_made" else "qk_made_d") for n in PER_LAYER}

        def at(l, name, n):
            return l * PER_LAYER[name] + n

        block = ctx.enter_context(nc.Block())
        n_loads = len(resident) + len(rows)

        @block.sync
        def _(sp):
            for name, t in resident.items():
                sp.dma_start(t[:], io[name]).then_inc(loaded, 16)
            for name, t in rows.items():
                sp.dma_start(t[:], io[name].partition_broadcast(P)).then_inc(loaded, 16)

            def shift_tokens(which, source_ready, n):
                sp.wait_ge(source_ready, n)
                sem_ = d[which]
                sp.dma_start(shifted[1:P, :, 64:P], y[0:P - 1, :, 64:P]).then_inc(sem_, 16)
                sp.dma_start(shifted[0:1, 1:NT, 64:P], y[P - 1:P, 0:NT - 1, 64:P]).then_inc(sem_, 16)

            def even_values(l):
                sp.wait_ge(d["v_ready"], at(l, "v_ready", NT))
                sp.dma_start(vte[0:W], vt[0:W]).then_inc(d["vte"], 16)
                sp.dma_start(vte[W:P, 1:NT], vt[W:P, 0:NT - 1]).then_inc(d["vte"], 16)

            with sp.Fori(0, n_batch) as b:
                sp.dma_start(x[:], io["x"][b].rearrange("(t p) d -> p t d", p=P)).then_inc(x_loaded, 16)
                shift_tokens("shift", xn_ready[5], 1)
                even_values(0)
                shift_tokens("shift2", d["y_mid"], 1)
                shift_tokens("shift", d["y_out"], 1)
                even_values(1)
                shift_tokens("shift2", d["y_mid"], 2)
                sp.wait_ge(x4_ready, 1)
                sp.dma_start(out[b].rearrange("(t p) d -> p t d", p=P), x[:]).then_inc(x_stored, 16)
                sp.wait_ge(x_stored, 16)
                sp.wait_ge(turn_over, 4)
                nums = [s.num for s in turn_sems]
                sp.sem_clear(range(min(nums), max(nums) + 1))
                sp.sem_inc(next_turn, 1)

        def end_turn(eng, b):
            eng.drain().then_inc(turn_over, 1)
            eng.wait_ge(next_turn, b + 1)

        @block.gpsimd
        def _(pool):
            nc.gpsimd.memset(never[:], NEG)
            nc.gpsimd.memset(eps4[:], EPS)
            nc.gpsimd.memset(minus_half[:], -0.5)
            nc.gpsimd.memset(v0[:], 0.0)
            nc.gpsimd.memset(shifted[0:1, 0, 64:P], 0.0).then_inc(setup_done, 1)
            pool.wait_ge(setup_done, 1)
            nc.gpsimd.memset(v0[:, :, :, HD0:HD0 + 1], 1.0).then_inc(setup_done, 1)
            pool.wait_ge(loaded, 16 * n_loads)
            steps = [0]

            def mark(ins):
                steps[0] += 1
                ins.then_inc(pool_step, 1)
                return steps[0]

            def need(n):
                pool.wait_ge(pool_step, n)

            def inverse_deviation(k):
                pool.wait_ge(var_ready[k], 1)
                need(mark(nc.gpsimd.tensor_tensor(veps[:], mv[:, :, 1], eps4[:], ALU.add)))
                nc.gpsimd.tensor_tensor(rstd[:], veps[:], minus_half[:], ALU.pow).then_inc(rstd_ready[k], 1)

            def attention():
                inverse_deviation(0)
                for u in range(NG0 * NT):
                    pool.wait_ge(a_pt, u + 1)
                    if u < NG0:
                        continue
                    if u >= 2:
                        pool.wait_ge(a_pv, u - 1)
                    nc.gpsimd.tensor_tensor(p_prev[:, u % 2], pt[:, u % 2],
                                            key_after[:].unsqueeze(1).to_broadcast([P, 4, P]),
                                            ALU.mult).then_inc(a_prev, 1)
                pool.wait_ge(rem_ready, 1)
                nc.gpsimd.tensor_tensor(tmp[1][:].rearrange("p (n d) -> p n d", d=HD0),
                                        remote[:].rearrange("p (n d) -> p n d", d=HD0),
                                        gr[:].unsqueeze(1).to_broadcast([P, NT * NH0, HD0]),
                                        ALU.mult).then_inc(g_rem, 1)
                nc.gpsimd.tensor_tensor(tmp[2][:].rearrange("p (t d) -> p t d", t=NT), x[:],
                                        out_b[:].unsqueeze(1).to_broadcast([P, NT, P]), ALU.add).then_inc(g_rem, 1)

            def skip_path():
                pool.wait_ge(xn_ready[2], 1)
                need(mark(nc.gpsimd.tensor_tensor(tmp[3][:].rearrange("p (t d) -> p t d", t=NT), xn[:],
                                                  d_row[:].unsqueeze(1).to_broadcast([P, NT, P]), ALU.mult)))
                nc.gpsimd.tensor_tensor(tmp[4][:].rearrange("p (t d) -> p t d", t=NT),
                                        tmp[3][:].rearrange("p (t d) -> p t d", t=NT), x[:],
                                        ALU.add).then_inc(s_skip, 1)

            def left_half(which, source_ready, n):
                pool.wait_ge(source_ready, n)
                nc.gpsimd.tensor_copy(shifted[:, :, 0:64], y[:, :, 0:64]).then_inc(d[which], 1)

            def layer(l, source_ready):
                left_half("left", source_ready, 1)
                for u in range(8):
                    pool.wait_ge(d["parts"], at(l, "parts", u + 1))
                    nc.gpsimd.tensor_tensor(qr[:, u, :], tmp[2 * (u % 2)][:], tmp[2 * (u % 2) + 1][:],
                                            ALU.add).then_inc(d["rot"], 1)
                for w in range(NW):
                    pool.wait_ge(d["wsum"], at(l, "wsum", w + 1))
                    if w >= 2:
                        pool.wait_ge(d["pturn"], at(l, "pturn", w - 1))
                    nc.gpsimd.tensor_tensor(pn[:, w % 2, :].rearrange("p (n k) -> p n k", n=NP),
                                            sc[:, w % 2, :].rearrange("p (n k) -> p n k", n=NP),
                                            wmax[:, w % 2, 8:12].unsqueeze(2).to_broadcast([P, NP, P]),
                                            ALU.mult).then_inc(d["pnorm"], 1)
                left_half("left2", d["y_mid"], l + 1)
                inverse_deviation(3 + l)

            with pool.Fori(0, n_batch) as b:
                steps[0] = 0
                attention()
                inverse_deviation(1)
                inverse_deviation(2)
                skip_path()
                inverse_deviation(5)
                layer(0, xn_ready[5])
                layer(1, d["y_out"])
                end_turn(pool, b)

        @block.scalar
        def _(act):
            act.wait_ge(setup_dve, 1)
            act.wait_ge(setup_done, 2)
            act.wait_ge(loaded, 16 * n_loads)

            def xt_copy(k):
                act.wait_ge(xt_made[k], 1)
                nc.scalar.copy(xt[:], ps[:, 0, :]).then_inc(xt_ready[k], 1)

            def attention():
                xt_copy(0)
                for u in range(8):
                    act.wait_ge(qk_made, u + 1)
                    if u >= 2:
                        act.wait_ge(qk_split, u - 1)
                    nc.scalar.activation(low[:, u % 2, :].bitcast(F32R), ps[:, 1 + u % 4, :], ACT.Identity,
                                         scale=low_rows[:, u:u + 1], bias=low_bias[:, u:u + 1]).then_inc(low_ready, 1)
                act.wait_ge(lat_made, 1)
                nc.scalar.activation(rqt[:], ps[0:32, 6, :], ACT.Identity, bias=rq_b[:]).then_inc(rqt_ready, 1)

                def values_out(u):
                    act.wait_ge(a_pv, u + 1)
                    if u >= 2:
                        act.wait_ge(a_back, u - 1)
                    nc.scalar.copy(o_t[:, u % 2, :], ps[:, 6, 0:P]).then_inc(a_ot, 1)

                n_units = NG0 * NT
                for u in range(n_units + 4):
                    if u >= 4:
                        values_out(u - 4)
                    if u < n_units:
                        act.wait_ge(a_shifted, u + 1)
                        nc.scalar.activation(prob[:, u % 3], prob[:, u % 3], ACT.Exp,
                                             scale=HD0 ** -0.5).then_inc(a_probs, 1)
                    if 1 <= u <= n_units:
                        act.wait_ge(a_turned, u)
                        if u >= 3:
                            act.wait_ge(a_cur, u - 2)
                            if u - 3 >= NG0:
                                act.wait_ge(a_prev, u - 2 - NG0)
                        nc.scalar.copy(pt[:, (u - 1) % 2], ps[:, 4 + (u - 1) % 2, :]
                                       .rearrange("p (h q) -> p h q", h=4)).then_inc(a_pt, 1)
                act.wait_ge(l_shifted, 1)
                nc.scalar.activation(lat_p[:], lat_p[:], ACT.Exp, scale=HD0 ** -0.5).then_inc(l_probs, 1)
                act.wait_ge(l_turned, 1)
                nc.scalar.copy(lat_t[:].rearrange("p u q -> p (u q)"),
                               ps[:, 2:4, :].rearrange("p a b -> p (a b)")).then_inc(l_pt, 1)
                act.wait_ge(l_back, 1)
                nc.scalar.copy(lat_ot[:], ps[0:32, 5, :]).then_inc(l_ot, 1)
                act.wait_ge(g_sum, 1)
                nc.scalar.activation(small[:, 1, :], small[:, 0, :], ACT.Sigmoid).then_inc(g_gate, 1)
                act.wait_ge(mixed_made, 1)
                nc.scalar.copy(xt[:], ps[:, 1, :]).then_inc(mixed_t, 1)

            def experts():
                xt_copy(1)
                act.wait_ge(m_shifted, 1)
                nc.scalar.activation(small[:, 2, 0:32], small[:, 1, 0:32], ACT.Exp).then_inc(m_exp, 1)
                for c in range(NCH):
                    n = E_CHUNKS[c % 3][1]
                    act.wait_ge(m_gate, c + 1)
                    if c >= 2:
                        act.wait_ge(m_hid, c - 1)
                    nc.scalar.activation(sil[0:n, c % 2, :], ps[0:n, 1 + c % 2, :], ACT.Silu).then_inc(m_silu, 1)

            def state_space():
                xt_copy(2)

            def layer(l):
                act.wait_ge(d["h_made"], at(l, "h_made", 1))
                nc.scalar.copy(xt[:], ps[:, 0, :]).then_inc(d["h_ready"], 1)
                for u in range(8):
                    if u >= 4:
                        act.wait_ge(d["v_made"], at(l, "v_made", u - 3))
                        nc.scalar.copy(vt[:, u - 4, :], ps[:, u, :]).then_inc(d["v_ready"], 1)
                    act.wait_ge(d["qk_made"], at(l, "qk_made", u + 1))
                    if u >= 2:
                        act.wait_ge(d["parts"], at(l, "parts", u - 1))
                    nc.scalar.activation(gel[:, u % 2, :], ps[:, u % 4, :], ACT.Square).then_inc(d["sq"], 1)
                for u in range(8):
                    act.wait_ge(d["turned"], at(l, "turned", u + 1))
                    nc.scalar.copy(qt[:, u // 4, :, (u % 4) * P:(u % 4 + 1) * P],
                                   ps[:, 4 + u % 4, :].rearrange("p (n q) -> p n q", n=NP)).then_inc(d["qt_ready"], 1)

                def copies(w):
                    act.wait_ge(d["pturn"], at(l, "pturn", w + 1))
                    if w >= 2:
                        act.wait_ge(d["pv"], at(l, "pv", w - 1))
                    nc.scalar.copy(ptw[:, w % 2], ps[:, 2 + w % 2, :]
                                   .rearrange("p (n q) -> p n q", n=NP)).then_inc(d["ptw"], 1)

                def outputs(w):
                    act.wait_ge(d["pv"], at(l, "pv", w + 1))
                    nc.scalar.copy(ot[:, :, w * W:(w + 1) * W],
                                   ps[:, 4 + w % 2, 0:NP * W].rearrange("p (n q) -> p n q", n=NP)).then_inc(d["ot"], 1)

                for w in range(NW + 4):
                    if w >= 4:
                        outputs(w - 4)
                    if w < NW:
                        act.wait_ge(d["shifted"], at(l, "shifted", w + 1))
                        nc.scalar.activation(sc[:, w % 2, :], sc[:, w % 2, :], ACT.Exp,
                                             scale=QK_SCALE).then_inc(d["probs"], 1)
                    if 2 <= w <= NW + 1:
                        copies(w - 2)
                act.wait_ge(xt_made[3 + l], 1)
                nc.scalar.activation(hn[:], ps[:, 7, :], ACT.Identity, scale=ln_g[l][:],
                                     bias=ln_b[l][:]).then_inc(xt_ready[3 + l], 1)
                for c, (_, n) in enumerate(H_CHUNKS):
                    act.wait_ge(d["ga"], at(l, "ga", c + 1))
                    nc.scalar.activation(gel[0:n, c, :], ps[0:n, 3 + c, :], ACT.Gelu,
                                         bias=b1g[l][0:n, c:c + 1]).then_inc(d["gelu"], 1)

            with act.Fori(0, n_batch) as b:
                attention()
                experts()
                state_space()
                layer(0)
                layer(1)
                end_turn(act, b)

        @block.tensor
        def _(pe):
            pe.wait_ge(loaded, 16 * n_loads)
            nc.tensor.matmul(ps[:, 0, 0:1], omega_w[:], a_col[:], start=True, stop=True).then_inc(setup_pe, 1)
            pe.wait_ge(setup_dve, 2)
            for t in range(NT):
                last = nc.tensor.transpose(ps[:, 1, t * P:(t + 1) * P], turn_t[:, t * P:(t + 1) * P], ident[:])
            last.then_inc(setup_pe, 1)
            pe.wait_ge(setup_dve, 3)

            def turn_tiles(src, bank_):
                for t in range(NT):
                    last = nc.tensor.transpose(ps[:, bank_, t * P:(t + 1) * P], src[:, t, :], ident[:])
                return last

            def normalised(k, bank_=0):
                pe.wait_ge(xn_ready[k], 1)
                turn_tiles(xn, bank_).then_inc(xt_made[k], 1)

            def attention():
                normalised(0)
                pe.wait_ge(xt_ready[0], 1)
                for u in range(8):
                    if u >= 4:
                        pe.wait_ge(qk_split, u - 3)
                    nc.tensor.matmul(ps[:, 1 + u % 4, :], wqk[:, u, :], xt[:], start=True, stop=True)\
                        .then_inc(qk_made, 1)
                for t in range(NT):
                    last = nc.tensor.matmul(b4(5)[:, t, :], xt[:, t * P:(t + 1) * P], wv0[:], start=True, stop=True)
                last.then_inc(v0_made, 1)
                nc.tensor.matmul(ps[0:32, 6, :], rq_w[:], xt[:], start=True, stop=True)
                pe.wait_ge(pooled, 1)
                nc.tensor.matmul(ps[0:32, 7, 0:NLAT], rk_w[:], pool_t[:, 0, :], start=True, stop=True)
                nc.tensor.matmul(ps[:, 7, NLAT:NLAT + 32], pool_t[:].rearrange("p a l -> p (a l)"), rv_w[:],
                                 start=True, stop=True).then_inc(lat_made, 1)
                pe.wait_ge(qk_split, 8)
                pe.wait_ge(v0_ready, 1)
                pe.wait_ge(lat_split, 1)
                pe.wait_ge(rqt_ready, 1)

                def scores(u):
                    qb, g = u // NG0, u % NG0
                    if u >= 2:
                        pe.wait_ge(a_shifted, u - 1)
                    r = slice(SLOT * g, SLOT * (g + 1))
                    first = max(qb - 1, 0) * P
                    for h in range(4):
                        c0 = 2 * (u % 2) + h // 2
                        o = (h % 2) * 256 + (0 if qb else P)
                        last = nc.tensor.matmul(ps[:, c0, o:(h % 2 + 1) * 256],
                                                qk[r, h, qb * P:(qb + 1) * P].bitcast(F32R),
                                                qk[r, 4 + h, first:(qb + 1) * P].bitcast(F32R),
                                                start=True, stop=True)
                    last.then_inc(a_scores, 1)

                def turned(u):
                    pe.wait_ge(a_probs, u + 1)
                    if u >= 2:
                        pe.wait_ge(a_pt, u - 1)
                    for h in range(4):
                        last = nc.tensor.transpose(ps[:, 4 + u % 2, h * P:(h + 1) * P], prob[:, u % 3, h, :],
                                                   ident[:])
                    last.then_inc(a_turned, 1)

                def values(u):
                    qb, g = u // NG0, u % NG0
                    pe.wait_ge(a_cur, u + 1)
                    if qb:
                        pe.wait_ge(a_prev, u + 1 - NG0)
                    if u >= 1:
                        pe.wait_ge(a_ot, u)
                    for h in range(4):
                        o = ps[32 * h:32 * h + 32, 6, 0:P]
                        last = nc.tensor.matmul(o, v0[:, qb, 4 * g + h, :], p_cur[:, u % 2, h, :],
                                                start=True, stop=(qb == 0))
                        if qb:
                            last = nc.tensor.matmul(o, v0[:, qb - 1, 4 * g + h, :], p_prev[:, u % 2, h, :],
                                                    start=False, stop=True)
                    last.then_inc(a_pv, 1)

                def back(u):
                    pe.wait_ge(a_ot, u + 1)
                    if u >= 1:
                        pe.wait_ge(a_loc, u)
                    nc.tensor.transpose(ps[:, 7, 0:P], o_t[:, u % 2, :],
                                        ident[:]).then_inc(a_back, 1)

                n_units = NG0 * NT
                for u in range(n_units + 4):
                    if u < n_units:
                        scores(u)
                    if 1 <= u <= n_units:
                        turned(u - 1)
                    if 3 <= u <= n_units + 2:
                        values(u - 3)
                    if u >= 4:
                        back(u - 4)
                pe.wait_ge(a_shifted, n_units)
                for t in range(NT):
                    last = nc.tensor.matmul(ps[:, t // 2, (t % 2) * 256:(t % 2 + 1) * 256],
                                            rqt[:, t * P:(t + 1) * P], rk_bd[:].rearrange("p h l -> p (h l)"),
                                            start=True, stop=True)
                last.then_inc(l_scores, 1)
                pe.wait_ge(l_probs, 1)
                for t in range(NT):
                    for c in range(2):
                        i = 2 * t + c
                        last = nc.tensor.transpose(ps[:, 2 + i // 4, (i % 4) * P:(i % 4 + 1) * P],
                                                   lat_p[:, i * P:(i + 1) * P], ident[:])
                last.then_inc(l_turned, 1)
                pe.wait_ge(l_pt, 1)
                for t in range(NT):
                    for c in range(2):
                        last = nc.tensor.matmul(ps[:, 4, t * 32 + c * 16:t * 32 + c * 16 + 16], lat_t[:, 2 * t + c, :],
                                                rv_bd[:, c].rearrange("p a d -> p (a d)"), start=True, stop=True)
                last.then_inc(l_out, 1)
                pe.wait_ge(l_norm, 1)
                for t in range(NT):
                    last = nc.tensor.transpose(ps[0:32, 5, t * P:(t + 1) * P], lat_o[:, t, :], ident[:])
                last.then_inc(l_back, 1)
                pe.wait_ge(l_ot, 1)
                for t in range(NT):
                    last = nc.tensor.matmul(b4(0)[:, t, :], lat_ot[:, t * P:(t + 1) * P], rout_w[:],
                                            start=True, stop=True)
                last.then_inc(l_remote, 1)
                pe.wait_ge(mixed_ready, 1)
                turn_tiles(tmp[3][:].rearrange("p (t d) -> p t d", t=NT), 1).then_inc(mixed_made, 1)
                pe.wait_ge(mixed_t, 1)
                for t in range(NT):
                    last = nc.tensor.matmul(b4(2)[:, t, :], xt[:, t * P:(t + 1) * P], out_w[:], start=True, stop=True)
                last.then_inc(a_proj, 1)

            def experts():
                normalised(1)
                pe.wait_ge(xt_ready[1], 1)
                for t in range(NT):
                    last = nc.tensor.matmul(ps[:, 7, t * NE:(t + 1) * NE], xt[:, t * P:(t + 1) * P], router[:],
                                            start=True, stop=True)
                last.then_inc(m_logits, 1)

                def up(c):
                    lo, n = E_CHUNKS[c % 3]
                    lo += (c // 3) * FI
                    if c >= 2:
                        pe.wait_ge(m_silu, c - 1)
                    nc.tensor.matmul(ps[0:n, 1 + c % 2, :], gate_w[:, lo:lo + n], xt[:], start=True, stop=True)\
                        .then_inc(m_gate, 1)
                    if c >= 2:
                        pe.wait_ge(m_hid, c - 1)
                    nc.tensor.matmul(ps[0:n, 3 + c % 2, :], up_w[:, lo:lo + n], xt[:], start=True, stop=True)\
                        .then_inc(m_up, 1)

                def down(c):
                    e, n = c // 3, E_CHUNKS[c % 3][1]
                    pe.wait_ge(m_hid, c + 1)
                    if c % 3 == 0 and e >= 2:
                        pe.wait_ge(m_added, NT * (e - 1))
                    for t in range(NT):
                        last = nc.tensor.matmul(b4(5 + e % 2)[:, t, :], hid[0:n, c % 2, t * P:(t + 1) * P],
                                                down_w[0:n, c, :], start=(c % 3 == 0 and t == 0), stop=(c % 3 == 2),
                                                skip_group_check=True)
                    last.then_inc(m_down, 1)

                for c in range(NCH + 1):
                    if c < NCH:
                        up(c)
                    if c:
                        down(c - 1)

            def state_space():
                normalised(2)
                pe.wait_ge(xt_ready[2], 1)
                for t in range(NT):
                    last = nc.tensor.matmul(b4(1)[:, t, :], xt[:, t * P:(t + 1) * P], bw2[:], start=True, stop=True)
                last.then_inc(s_in, 1)
                pe.wait_ge(s_turned, 1)
                for t in range(NT):
                    last = nc.tensor.matmul(ps[:, 2, t * P:S], tmp[0][:, t * P:(t + 1) * P], up_to[:, 0:S - t * P],
                                            start=(t == 0), stop=(t == NT - 1), skip_group_check=True)
                last.then_inc(s_sum, 1)
                pe.wait_ge(s_state, 1)
                for t in range(NT):
                    last = nc.tensor.matmul(b4(3)[:, t, :], tmp[1][:, t * P:(t + 1) * P], cw2[:],
                                            start=True, stop=True)
                last.then_inc(s_out, 1)

            def layer(l):
                pe.wait_ge(d["shift"], at(l, "shift", 32))
                pe.wait_ge(d["left"], at(l, "left", 1))
                turn_tiles(shifted, 0).then_inc(d["h_made"], 1)
                pe.wait_ge(d["h_ready"], at(l, "h_ready", 1))
                for u in range(8):
                    if u == 4:
                        for t in range(NT):
                            nc.tensor.matmul(ps[:, 4 + t, :], xt[:, t * P:(t + 1) * P], wqkv[l][:, 2, :],
                                             start=True, stop=True).then_inc(d["v_made"], 1)
                    if u >= 4:
                        pe.wait_ge(d["parts"], at(l, "parts", u - 3))
                    nc.tensor.matmul(ps[:, u % 4, :], xt[:, (u % 4) * P:(u % 4 + 1) * P], wqkv[l][:, u // 4, :],
                                     start=True, stop=True).then_inc(d["qk_made"], 1)
                for u in range(8):
                    pe.wait_ge(d["normed"], at(l, "normed", u + 1))
                    if u < 4:
                        pe.wait_ge(d["v_ready"], at(l, "v_ready", u + 1))
                    else:
                        pe.wait_ge(d["qt_ready"], at(l, "qt_ready", u - 3))
                    for n in range(NP):
                        last = nc.tensor.transpose(ps[:, 4 + u % 4, n * P:(n + 1) * P], qr[:, u, n * P:(n + 1) * P],
                                                   ident[:])
                    last.then_inc(d["turned"], 1)
                pe.wait_ge(d["qt_ready"], at(l, "qt_ready", 8))

                def scores(w):
                    if w >= 2:
                        pe.wait_ge(d["shifted"], at(l, "shifted", w - 1))
                    qw = slice(w * W, (w + 1) * W)
                    for n in range(NP):
                        for h in range(2):
                            r = slice(W * h, W * h + W)
                            if w % 2:
                                last = nc.tensor.matmul(ps[r, w % 2, n * P:(n + 1) * P], qt[r, 0, n, qw],
                                                        qt[r, 1, n, (w - 1) * W:(w + 1) * W], start=True, stop=True)
                            else:
                                before = max(w - 1, 0)
                                nc.tensor.matmul(ps[r, w % 2, n * P:n * P + W], qt[r, 0, n, qw], qt[r, 1, n, qw],
                                                 start=True, stop=True)
                                last = nc.tensor.matmul(ps[r, w % 2, n * P + W:(n + 1) * P], qt[r, 0, n, qw],
                                                        qt[r, 1, n, before * W:(before + 1) * W],
                                                        start=True, stop=True)
                    last.then_inc(d["scores"], 1)

                def turned(w):
                    pe.wait_ge(d["pnorm"], at(l, "pnorm", w + 1))
                    if w >= 2:
                        pe.wait_ge(d["ptw"], at(l, "ptw", w - 1))
                    for n in range(NP):
                        last = nc.tensor.transpose(ps[:, 2 + w % 2, n * P:(n + 1) * P],
                                                   pn[:, w % 2, n * P:(n + 1) * P], ident[:])
                    last.then_inc(d["pturn"], 1)

                def values(w):
                    pe.wait_ge(d["ptw"], at(l, "ptw", w + 1))
                    if w == 2:
                        pe.wait_ge(d["vte"], at(l, "vte", 32))
                    if w >= 2:
                        pe.wait_ge(d["ot"], at(l, "ot", w - 1))
                    t = w // 2
                    for n in range(NP):
                        for h in range(2):
                            f = slice((2 * n + h) * W, (2 * n + h + 1) * W)
                            o = ps[W * h:W * h + W, 4 + w % 2, n * W:(n + 1) * W]
                            pcols = slice(h * W, h * W + W)
                            if w:
                                v_ = vt if w % 2 else vte
                                last = nc.tensor.matmul(o, v_[:, t, f], ptw[:, w % 2, n, pcols], start=True, stop=True)
                            else:
                                last = nc.tensor.matmul(o, vt[0:W, t, f], ptw[0:W, w % 2, n, pcols],
                                                        start=True, stop=True)
                    last.then_inc(d["pv"], 1)

                for w in range(NW + 3):
                    if w < NW:
                        scores(w)
                    if 2 <= w <= NW + 1:
                        turned(w - 2)
                    if w >= 3:
                        values(w - 3)
                pe.wait_ge(d["ot"], at(l, "ot", NW))
                for t in range(NT):
                    for n in range(NP):
                        last = nc.tensor.matmul(b4(6)[:, t, :], ot[:, n, t * P:(t + 1) * P], wo[l][:, n, :],
                                                start=(n == 0), stop=(n == NP - 1))
                last.then_inc(d["wo"], 1)
                normalised(3 + l, 7)
                pe.wait_ge(xt_ready[3 + l], 1)
                for c, (lo, n) in enumerate(H_CHUNKS):
                    nc.tensor.matmul(ps[0:n, c, :], w1[l][:, lo:lo + n], hn[:], start=True, stop=True)
                    nc.tensor.matmul(ps[0:n, 3 + c, :], w1[l][:, HID + lo:HID + lo + n], hn[:],
                                     start=True, stop=True).then_inc(d["ga"], 1)
                pe.wait_ge(d["mlp"], at(l, "mlp", 3))
                for t in range(NT):
                    for c, (lo, n) in enumerate(H_CHUNKS):
                        last = nc.tensor.matmul(b4(6)[:, t, :], mlp[0:n, c, t * P:(t + 1) * P], w2[l][0:n, c, :],
                                                start=(c == 0), stop=(c == 2))
                last.then_inc(d["w2"], 1)

            with pe.Fori(0, n_batch) as b:
                attention()
                experts()
                state_space()
                layer(0)
                layer(1)
                end_turn(pe, b)

        @block.vector
        def _(dve):
            V = nc.vector
            steps = [0]
            chain = [setup_chain := sem("setup_chain")]

            def mark(ins):
                steps[0] += 1
                ins.then_inc(chain[0], 1)
                return steps[0]

            def need(n):
                dve.wait_ge(chain[0], n)

            dve.wait_ge(loaded, 16 * n_loads)
            V.tensor_tensor(low_bias[:], low_rows[:], bqk[:], ALU.mult).then_inc(setup_dve, 1)
            for l in range(2):
                for i in range(2):
                    s = qk_s[l][i]
                    V.tensor_tensor(rope_c[l][i][:], rope[2 * i][:], s[:].unsqueeze(1).to_broadcast([P, NT, W]),
                                    ALU.mult)
                    for a, c in ((0, 32), (32, 0)):
                        V.tensor_tensor(rope_s[l][i][:, :, a:a + 32], rope[2 * i + 1][:, :, a:a + 32],
                                        s[:, c:c + 32].unsqueeze(1).to_broadcast([P, NT, 32]), ALU.mult)
            dve.wait_ge(setup_pe, 1)
            need(mark(V.tensor_copy(omega[:], ps[:, 0, 0:1])))
            need(mark(V.tensor_tensor(pw[:, 0:1], omega[:], omega[:], ALU.mult)))
            V.tensor_scalar(pw[:, 1:2], pw[:, 0:1], 1.0, None, ALU.add)
            need(mark(V.tensor_scalar(pw[:, 2:3], pw[:, 0:1], -1.0, 1.0, ALU.mult, ALU.add)))
            need(mark(V.reciprocal(pw[:, 3:4], pw[:, 1:2])))
            V.tensor_tensor(pw[:, 4:5], pw[:, 2:3], pw[:, 3:4], ALU.mult)
            need(mark(V.scalar_tensor_tensor(pw[:, 5:6], omega[:], 2.0, pw[:, 3:4], ALU.mult, ALU.mult)))
            V.memset(cos_t[:, 0:1], 1.0)
            need(mark(V.memset(sin_t[:, 0:1], 0.0)))
            c0 = 4
            m = 1
            while m < S:
                c_, s_ = pw[:, c0:c0 + 1], pw[:, c0 + 1:c0 + 2]
                V.tensor_scalar(turn_t[:, 0:m], sin_t[:, 0:m], s_, None, ALU.mult)
                need(mark(V.tensor_scalar(tmp[0][:, 0:m], sin_t[:, 0:m], c_, None, ALU.mult)))
                V.scalar_tensor_tensor(cos_t[:, m:2 * m], cos_t[:, 0:m], c_, turn_t[:, 0:m], ALU.mult, ALU.subtract)
                V.scalar_tensor_tensor(sin_t[:, m:2 * m], cos_t[:, 0:m], s_, tmp[0][:, 0:m], ALU.mult, ALU.add)
                n0 = 10 - c0
                need(mark(V.tensor_tensor(pw[:, 8:9], s_, s_, ALU.mult)))
                V.scalar_tensor_tensor(pw[:, n0:n0 + 1], c_, c_, pw[:, 8:9], ALU.mult, ALU.subtract)
                need(mark(V.scalar_tensor_tensor(pw[:, n0 + 1:n0 + 2], c_, 2.0, s_, ALU.mult, ALU.mult)))
                c0 = n0
                m *= 2
            V.tensor_copy(turn_t[0:64, :], cos_t[0:64, :])
            V.tensor_copy(turn_t[64:P, :], sin_t[64:P, :]).then_inc(setup_dve, 1)
            dve.wait_ge(setup_pe, 2)
            V.tensor_copy(turn[:], b4(1)).then_inc(setup_dve, 1)
            dve.wait_ge(setup_dve, 3)
            dve.wait_ge(setup_done, 2)
            chain[0] = dve_step

            def layernorm(k, src, dst=xn):
                for t in range(NT):
                    n = mark(V.bn_stats(stats[:, t, :], src[:, t, :]))
                need(n)
                for t in range(NT):
                    last = V.bn_aggr(mv[:, t, :], stats[:, t, :])
                last.then_inc(var_ready[k], 1)
                dve.wait_ge(rstd_ready[k], 1)
                for t in range(NT):
                    last = V.tensor_scalar(dst[:, t, :], src[:, t, :], mv[:, t, 0:1], rstd[:, t:t + 1],
                                           ALU.subtract, ALU.mult)
                last.then_inc(xn_ready[k], 1)

            def attention():
                dve.wait_ge(x_loaded, 16)
                layernorm(0, x)
                dve.wait_ge(xt_ready[0], 1)
                need(mark(V.tensor_reduce(pool_t[:, 0, :], xt[:].rearrange("p (l c) -> p l c", c=8), AX_X, ALU.add)))
                V.tensor_copy(pool_t[:, 1, :], pool_t[:, 0, :]).then_inc(pooled, 1)
                for u in range(8):
                    dve.wait_ge(low_ready, u + 1)
                    V.scalar_tensor_tensor(qk[:, u, :].bitcast(F32R), ps[:, 1 + u % 4, :], bqk[:, u:u + 1],
                                           low[:, u % 2, :], ALU.add, ALU.subtract).then_inc(qk_split, 1)
                dve.wait_ge(v0_made, 1)
                V.tensor_tensor(v0[:, :, :, 0:HD0], b4(5).rearrange("p t (h d) -> p t h d", d=HD0),
                                v_b[:].rearrange("p (h d) -> p h d", d=HD0).unsqueeze(1)
                                .to_broadcast([P, NT, NH0, HD0]), ALU.add).then_inc(v0_ready, 1)
                dve.wait_ge(lat_made, 1)
                V.tensor_scalar(rk_row[:], ps[0:32, 7, 0:NLAT], 0.125, rk_b[:], ALU.mult, ALU.add)
                need(mark(V.scalar_tensor_tensor(rv_row[:], ps[:, 7, NLAT:NLAT + 32], 0.125, rv_b[:],
                                                 ALU.mult, ALU.add)))
                V.tensor_tensor(rk_bd[:], rk_row[:].unsqueeze(1).to_broadcast([32, LH, NLAT]),
                                own_head[:].unsqueeze(2).to_broadcast([32, LH, NLAT]), ALU.mult)
                V.tensor_tensor(rv_bd[:].rearrange("p c a d -> p c a d"),
                                rv_row[:].rearrange("p (c a d) -> p c a d", c=2, a=2),
                                own_half[:].unsqueeze(1).unsqueeze(3).to_broadcast([P, 2, 2, HD0]),
                                ALU.mult).then_inc(lat_split, 1)

                def shift(u):
                    qb = u // NG0
                    dve.wait_ge(a_scores, u + 1)
                    both = ps[:, 2 * (u % 2):2 * (u % 2) + 2, :].rearrange("p a (h k) -> p (a h) k", h=2)
                    cur = both[:, :, P:2 * P]
                    prev = both[:, :, 0:P] if qb else never[:]
                    need(mark(V.copy_predicated(cur, take_prev[:], prev)))
                    if qb:
                        need(mark(V.memset(cur[0:1, :, 0:1], NEG)))
                    need(mark(V.tensor_reduce(negmax[:, u % 2, :], cur, AX_X, ALU.max)))
                    if u >= 3:
                        dve.wait_ge(a_turned, u - 2)
                    V.tensor_tensor(prob[:, u % 3], cur, negmax[:, u % 2, :].unsqueeze(2).to_broadcast([P, 4, P]),
                                    ALU.subtract).then_inc(a_shifted, 1)

                def keys_of_block(u):
                    dve.wait_ge(a_pt, u + 1)
                    if u >= 2:
                        dve.wait_ge(a_pv, u - 1)
                    V.tensor_tensor(p_cur[:, u % 2], pt[:, u % 2], key_before[:].unsqueeze(1).to_broadcast([P, 4, P]),
                                    ALU.mult).then_inc(a_cur, 1)

                def gather(u):
                    qb, g = u // NG0, u % NG0
                    dve.wait_ge(a_back, u + 1)
                    V.tensor_copy(loc[:, qb, 4 * g:4 * g + 4, :],
                                  ps[:, 7, 0:P].rearrange("p (h s) -> p h s", h=4)
                                  [:, :, 0:HD0 + 1]).then_inc(a_loc, 1)

                n_units = NG0 * NT
                for u in range(n_units + 5):
                    if u >= 5:
                        gather(u - 5)
                    if u < n_units:
                        shift(u)
                    if 2 <= u <= n_units + 1:
                        keys_of_block(u - 2)
                lat3 = lat_p[:].rearrange("p (t h l) -> p t h l", t=NT, h=LH)
                lat2 = lat_p[:].rearrange("p (n l) -> p n l", l=NLAT)
                dve.wait_ge(l_scores, 1)
                for a in range(2):
                    n = mark(V.tensor_tensor(lat3[:, 2 * a:2 * a + 2],
                                             ps[:, a, :].rearrange("p (t h l) -> p t h l", t=2, h=LH),
                                             lat_mask[:, 2 * a:2 * a + 2].unsqueeze(2).to_broadcast([P, 2, LH, NLAT]),
                                             ALU.add))
                need(n)
                need(mark(V.tensor_reduce(small[:, 2, 0:16], lat2, AX_X, ALU.max)))
                V.tensor_tensor(lat2, lat2, small[:, 2, 0:16].unsqueeze(2).to_broadcast([P, 16, NLAT]),
                                ALU.subtract).then_inc(l_shifted, 1)
                dve.wait_ge(l_probs, 1)
                need(mark(V.tensor_reduce(small[:, 3, 0:16], lat2, AX_X, ALU.add)))
                need(mark(V.reciprocal(small[:, 4, 0:16], small[:, 3, 0:16])))
                need(mark(V.tensor_tensor(small[:, 5, 0:16].rearrange("p (t h) -> p t h", t=NT),
                                          small[:, 4, 0:16].rearrange("p (t h) -> p t h", t=NT),
                                          lat_valid[:].unsqueeze(2).to_broadcast([P, NT, LH]), ALU.mult)))
                dve.wait_ge(l_out, 1)
                V.tensor_tensor(lat_o[:].rearrange("p t (h d) -> p (t h) d", h=LH),
                                ps[:, 4, 0:P].rearrange("p (n d) -> p n d", d=HD0),
                                small[:, 5, 0:16].unsqueeze(2).to_broadcast([P, 16, HD0]), ALU.mult)\
                    .then_inc(l_norm, 1)
                dve.wait_ge(l_remote, 1)
                V.tensor_tensor(remote[:].rearrange("p (t d) -> p t d", t=NT), b4(0),
                                rout_b[:].unsqueeze(1).to_broadcast([P, NT, P]), ALU.add).then_inc(rem_ready, 1)
                locf = loc[:].rearrange("p t h d -> p (t h) d")
                dve.wait_ge(a_loc, n_units)
                need(mark(V.tensor_scalar(loc_r[:], locf[:, :, HD0], 1e-30, None, ALU.max)))
                need(mark(V.reciprocal(small[:, 6, :], loc_r[:])))
                t0 = tmp[0][:].rearrange("p (n d) -> p n d", d=HD0)
                t1 = tmp[1][:].rearrange("p (n d) -> p n d", d=HD0)
                t3 = tmp[3][:].rearrange("p (n d) -> p n d", d=HD0)
                need(mark(V.tensor_tensor(t0, locf[:, :, 0:HD0], small[:, 6, :].unsqueeze(2)
                                          .to_broadcast([P, 64, HD0]), ALU.mult)))
                need(mark(V.tensor_tensor(t3, t0, gl[:].unsqueeze(1).to_broadcast([P, 64, HD0]), ALU.mult)))
                dve.wait_ge(g_rem, 2)
                need(mark(V.tensor_tensor(tmp[3][:], tmp[3][:], tmp[1][:], ALU.add)))
                V.tensor_reduce(small[:, 0, :], t3, AX_X, ALU.add).then_inc(g_sum, 1)
                dve.wait_ge(rem_ready, 1)
                need(mark(V.tensor_tensor(tmp[4][:], tmp[0][:], remote[:], ALU.subtract)))
                dve.wait_ge(g_gate, 1)
                need(mark(V.tensor_tensor(tmp[5][:].rearrange("p (n d) -> p n d", d=HD0),
                                          tmp[4][:].rearrange("p (n d) -> p n d", d=HD0),
                                          small[:, 1, :].unsqueeze(2).to_broadcast([P, 64, HD0]), ALU.mult)))
                V.tensor_tensor(tmp[3][:], tmp[5][:], remote[:], ALU.add).then_inc(mixed_ready, 1)
                dve.wait_ge(a_proj, 1)
                V.tensor_tensor(x[:], b4(2), tmp[2][:].rearrange("p (t d) -> p t d", t=NT),
                                ALU.add).then_inc(x1_ready, 1)

            def experts():
                dve.wait_ge(x1_ready, 1)
                layernorm(1, x)
                logits = small[:, 0, 0:32].rearrange("p (t e) -> p t e", e=NE)
                dve.wait_ge(m_logits, 1)
                need(mark(V.tensor_copy(small[:, 0, 0:32], ps[:, 7, 0:NT * NE])))
                need(mark(V.tensor_reduce(small[:, 3, 0:NT], logits, AX_X, ALU.max)))
                V.tensor_tensor(small[:, 1, 0:32].rearrange("p (t e) -> p t e", e=NE), logits,
                                small[:, 3, 0:NT].unsqueeze(2).to_broadcast([P, NT, NE]),
                                ALU.subtract).then_inc(m_shifted, 1)
                sh = [P, NT, NE, NE]
                pair = [t_[:, 0:256].rearrange("p (t e f) -> p t e f", t=NT, e=NE) for t_ in tmp]
                other, own = logits.unsqueeze(2).to_broadcast(sh), logits.unsqueeze(3).to_broadcast(sh)
                V.tensor_tensor(pair[0], other, own, ALU.is_gt)
                need(mark(V.tensor_tensor(pair[1], other, own, ALU.is_equal)))
                need(mark(V.tensor_tensor(tmp[2][:, 0:256].rearrange("p (t e) -> p t e", t=NT),
                                          tmp[1][:, 0:256].rearrange("p (t e) -> p t e", t=NT),
                                          lower_index[:].unsqueeze(1).to_broadcast([P, NT, 64]), ALU.mult)))
                need(mark(V.tensor_tensor(tmp[3][:, 0:256], tmp[0][:, 0:256], tmp[2][:, 0:256], ALU.add)))
                need(mark(V.tensor_reduce(small[:, 4, 0:32], tmp[3][:, 0:256].rearrange("p (n f) -> p n f", f=NE),
                                          AX_X, ALU.add)))
                need(mark(V.tensor_scalar(small[:, 5, 0:32], small[:, 4, 0:32], 2.0, None, ALU.is_lt)))
                dve.wait_ge(m_exp, 1)
                ex = small[:, 2, 0:32].rearrange("p (t e) -> p t e", e=NE)
                need(mark(V.tensor_reduce(small[:, 3, 8:8 + NT], ex, AX_X, ALU.add)))
                n = mark(V.tensor_tensor(small[:, 6, 0:32], small[:, 2, 0:32], small[:, 5, 0:32], ALU.mult))
                need(mark(V.reciprocal(small[:, 3, 16:16 + NT], small[:, 3, 8:8 + NT])))
                need(mark(V.tensor_tensor(w_te[:], small[:, 6, 0:32].rearrange("p (t e) -> p t e", e=NE),
                                          small[:, 3, 16:16 + NT].unsqueeze(2).to_broadcast([P, NT, NE]), ALU.mult)))

                def product(c):
                    n_ = E_CHUNKS[c % 3][1]
                    dve.wait_ge(m_silu, c + 1)
                    dve.wait_ge(m_up, c + 1)
                    if c >= 2:
                        dve.wait_ge(m_down, c - 1)
                    V.tensor_tensor(hid[0:n_, c % 2, :], sil[0:n_, c % 2, :], ps[0:n_, 3 + c % 2, :],
                                    ALU.mult).then_inc(m_hid, 1)

                def add_expert(e):
                    dve.wait_ge(m_down, 3 * (e + 1))
                    if e:
                        dve.wait_ge(m_added, NT * e)
                    for t in range(NT):
                        V.scalar_tensor_tensor(x[:, t, :], b4(5 + e % 2)[:, t, :], w_te[:, t, e:e + 1], x[:, t, :],
                                               ALU.mult, ALU.add).then_inc(m_added, 1)

                for c in range(NCH):
                    product(c)
                    if c % 3 == 1 and c > 3:
                        add_expert(c // 3 - 1)
                add_expert(NE - 1)

            def state_space():
                dve.wait_ge(m_added, NE * NT)
                layernorm(2, x)
                dve.wait_ge(s_in, 1)
                V.tensor_tensor(tmp[0][:].rearrange("p (t d) -> p t d", t=NT), b4(1), turn[:], ALU.mult)\
                    .then_inc(s_turned, 1)
                dve.wait_ge(s_sum, 1)
                V.tensor_tensor(tmp[1][:], ps[:, 2, :], turn_t[:], ALU.mult).then_inc(s_state, 1)
                dve.wait_ge(s_skip, 1)
                dve.wait_ge(s_out, 1)
                V.tensor_tensor(x[:], b4(3), tmp[4][:].rearrange("p (t d) -> p t d", t=NT),
                                ALU.add).then_inc(x3_ready, 1)

            def layer(l):

                def h8(ap):
                    return ap.rearrange("p (h k) -> p h k", h=8)

                def parts(u):
                    i, t = u // 4, u % 4
                    src = ps[:, u % 4, :]
                    c_part, s_part = tmp[2 * (u % 2)], tmp[2 * (u % 2) + 1]
                    dve.wait_ge(d["sq"], at(l, "sq", u + 1))
                    if u >= 2:
                        dve.wait_ge(d["rot"], at(l, "rot", u - 1))
                    V.tensor_tensor(h8(c_part[:]), h8(src), rope_c[l][i][:, t, :].unsqueeze(1)
                                    .to_broadcast([P, 8, W]), ALU.mult)
                    for a, c in ((0, 32), (32, 0)):
                        V.tensor_tensor(h8(s_part[:])[:, :, a:a + 32], h8(src)[:, :, c:c + 32],
                                        rope_s[l][i][:, t, a:a + 32].unsqueeze(1).to_broadcast([P, 8, 32]), ALU.mult)
                    V.tensor_reduce(ss[:, 8 * u:8 * u + 8], h8(gel[:, u % 2, :]), AX_X, ALU.add)\
                        .then_inc(d["parts"], 1)

                def inverse_norms(i):
                    c = slice(32 * i, 32 * i + 32)
                    dve.wait_ge(d["parts"], at(l, "parts", 4 * i + 4))
                    need(mark(V.tensor_scalar(nw[:, 0, c], ss[:, c], 1e-24, None, ALU.max)))
                    need(mark(V.tensor_scalar(nw[:, 1, c].bitcast(I32), nw[:, 0, c].bitcast(I32), 1, None,
                                              ALU.logical_shift_right)))
                    need(mark(V.tensor_scalar(nw[:, 2, c].bitcast(I32), nw[:, 1, c].bitcast(I32), -1.0,
                                              float(0x5f3759df), ALU.mult, ALU.add)))
                    for k in range(3):
                        old, new = nw[:, 2 - k % 2, c], nw[:, 1 + k % 2, c]
                        need(mark(V.tensor_tensor(nw[:, 3, c], old, old, ALU.mult)))
                        need(mark(V.scalar_tensor_tensor(nw[:, 4, c], nw[:, 3, c], -0.5, nw[:, 0, c],
                                                         ALU.mult, ALU.mult)))
                        need(mark(V.scalar_tensor_tensor(new, nw[:, 4, c], 1.5, old, ALU.add, ALU.mult)))

                def normed(u):
                    dve.wait_ge(d["rot"], at(l, "rot", u + 1))
                    V.tensor_tensor(h8(qr[:, u, :]), h8(qr[:, u, :]), nw[:, 1, 8 * u:8 * u + 8].unsqueeze(2)
                                    .to_broadcast([P, 8, W]), ALU.mult).then_inc(d["normed"], 1)

                for u in range(4):
                    parts(u)
                inverse_norms(0)
                for u in range(4, 8):
                    parts(u)
                    normed(u - 4)
                inverse_norms(1)
                for u in range(4, 8):
                    normed(u)

                def n4(ap):
                    return ap.rearrange("p (n k) -> p n k", n=NP)

                def shift(w):
                    kind = 0 if w % 2 else (1 if w else 2)
                    dve.wait_ge(d["scores"], at(l, "scores", w + 1))
                    if w >= 2:
                        dve.wait_ge(d["pnorm"], at(l, "pnorm", w - 1))
                    need(mark(V.tensor_tensor(n4(sc[:, w % 2, :]), n4(ps[:, w % 2, :]),
                                              win_mask[:, kind, :].unsqueeze(1).to_broadcast([P, NP, P]), ALU.add)))
                    need(mark(V.tensor_reduce(wmax[:, w % 2, 0:4], n4(sc[:, w % 2, :]), AX_X, ALU.max)))
                    V.tensor_tensor(n4(sc[:, w % 2, :]), n4(sc[:, w % 2, :]),
                                    wmax[:, w % 2, 0:4].unsqueeze(2).to_broadcast([P, NP, P]),
                                    ALU.subtract).then_inc(d["shifted"], 1)

                def sums(w):
                    dve.wait_ge(d["probs"], at(l, "probs", w + 1))
                    need(mark(V.tensor_reduce(wmax[:, w % 2, 4:8], n4(sc[:, w % 2, :]), AX_X, ALU.add)))
                    V.reciprocal(wmax[:, w % 2, 8:12], wmax[:, w % 2, 4:8]).then_inc(d["wsum"], 1)

                for w in range(NW + 1):
                    if w < NW:
                        shift(w)
                    if w:
                        sums(w - 1)
                dve.wait_ge(d["wo"], at(l, "wo", 1))
                V.tensor_tensor(y[:], y[:], b4(6), ALU.add).then_inc(d["y_mid"], 1)
                dve.wait_ge(d["shift2"], at(l, "shift2", 32))
                dve.wait_ge(d["left2"], at(l, "left2", 1))
                layernorm(3 + l, shifted)
                for c, (_, n) in enumerate(H_CHUNKS):
                    dve.wait_ge(d["gelu"], at(l, "gelu", c + 1))
                    V.scalar_tensor_tensor(mlp[0:n, c, :], ps[0:n, c, :], b1a[l][0:n, c:c + 1], gel[0:n, c, :],
                                           ALU.add, ALU.mult).then_inc(d["mlp"], 1)
                t4 = tmp[4][:].rearrange("p (t d) -> p t d", t=NT)
                need(mark(V.tensor_tensor(t4, y[:], b2[l][:].unsqueeze(1).to_broadcast([P, NT, P]), ALU.add)))
                dve.wait_ge(d["w2"], at(l, "w2", 1))
                V.tensor_tensor(y[:], t4, b4(6), ALU.add).then_inc(d["y_out"], 1)
                dve.wait_ge(d["y_out"], at(l, "y_out", 1))

            with dve.Fori(0, n_batch) as b:
                steps[0] = 0
                attention()
                experts()
                state_space()
                dve.wait_ge(x3_ready, 1)
                layernorm(5, x, y)
                dve.wait_ge(xn_ready[5], 1)
                layer(0)
                layer(1)
                V.tensor_tensor(x[:], x[:], y[:], ALU.add).then_inc(x4_ready, 1)
                end_turn(dve, b)


def constants():
    f = np.float32
    p = np.arange(P)
    c = {"ident": np.eye(P, dtype=f)}
    c["take_prev"] = np.ascontiguousarray(np.broadcast_to((p[None, :] >= p[:, None]).astype(np.int32)[:, None], (P, 4, P)))
    c["key_before"] = (p[:, None] < p[None, :]).astype(f)
    c["key_after"] = (p[:, None] >= p[None, :]).astype(f)
    tok = np.arange(S).reshape(NT, P)
    lat = np.where(np.arange(NLAT)[None, None, :] < (tok // 8)[:, :, None], 0.0, NEG).astype(f)
    c["lat_mask"] = np.ascontiguousarray(lat.transpose(1, 0, 2))
    c["lat_valid"] = np.ascontiguousarray((tok >= 8).astype(f).T)
    c["own_head"] = (np.arange(32)[:, None] // 8 == np.arange(LH)[None, :]).astype(f)
    c["own_half"] = (p[:, None] // 64 == np.arange(2)[None, :]).astype(f)
    low = np.zeros((P, 8), f)
    row = p % SLOT
    low[(row >= 16) & (row < 24), 0:4] = 1.0
    low[(row >= 8) & (row < 16), 4:8] = 1.0
    c["low_rows"] = low
    e = np.arange(NE)
    c["lower_index"] = np.ascontiguousarray(np.broadcast_to((e[None, :] < e[:, None]).astype(f).reshape(1, -1), (P, 64)))
    j, k = np.arange(32)[:, None].astype(np.float64), (np.arange(P) % 64)[None, :]
    c["omega_w"] = (-(np.sin(2 * np.pi * (j + 1) * k / 64) + (j >= 1) * np.sin(2 * np.pi * j * k / 64))).astype(f)
    c["up_to"] = (p[:, None] <= np.arange(S)[None, :]).astype(f)
    half = np.arange(0, W, 2, dtype=f)
    inv = f(1.0) / f(10000.0) ** (half / f(W))
    t = np.arange(S, dtype=f)
    fr = (t[:, None] * inv[None, :]).astype(f)
    fr = np.concatenate([fr, fr], -1)
    base = (half + f(0.4) * W) / f(1.4 * W)
    power = (t - S // 2) / f(32)
    scale = base[None, :].astype(f) ** power[:, None].astype(f)
    scale = np.concatenate([scale, scale], -1)
    sign = np.where(np.arange(W) < 32, -1.0, 1.0)
    tabs = [np.cos(fr) * scale, np.sin(fr) * scale * sign, np.cos(fr) / scale, np.sin(fr) / scale * sign]
    for i, a in enumerate(tabs):
        c[f"rope{i}"] = np.ascontiguousarray(a.astype(f).reshape(NT, P, W).transpose(1, 0, 2))
    q, kk = (p % W)[:, None], np.arange(W)[None, :]
    cur, prev = kk <= q, kk >= q
    no = np.zeros_like(cur)
    m = np.stack([np.concatenate([prev, cur], 1), np.concatenate([cur, prev], 1), np.concatenate([cur, no], 1)], 1)
    c["win_mask"] = np.where(m, 0.0, NEG).astype(f)
    return c


def layout(a):
    g = {n: np.asarray(v) for n, v in a.items()}
    o = {"x": g["L0_attn_x"]}
    qkv_w, qkv_b = g["L0_attn_qkv_w"], g["L0_attn_qkv_b"]
    wqk = np.zeros((P, 8, P), np.float32)
    bqk = np.zeros((P, 8), np.float32)
    for i in range(2):
        for h in range(NH0):
            grp, t = h // 4, h % 4
            for r in range(3):
                cols = slice(SLOT * grp + 8 * r, SLOT * grp + 8 * r + 8)
                src = slice(i * P + 8 * h, i * P + 8 * h + 8)
                wqk[:, 4 * i + t, cols] = qkv_w[:, src]
                bqk[cols, 4 * i + t] = qkv_b[src]
    o["wqk"], o["bqk"] = wqk, bqk
    o["wv0"], o["v_b"] = qkv_w[:, 2 * P:], qkv_b[2 * P:]
    o["rq_w"], o["rq_b"] = g["L0_attn_rq_w"], g["L0_attn_rq_b"][:, None]
    o["rk_w"], o["rv_w"] = g["L0_attn_rkv_w"][:, :32], g["L0_attn_rkv_w"][:, 32:]
    o["rk_b"], o["rv_b"] = g["L0_attn_rkv_b"][:32, None], g["L0_attn_rkv_b"][32:]
    o["rout_w"], o["rout_b"] = g["L0_attn_rout_w"], g["L0_attn_rout_b"]
    o["out_w"], o["out_b"] = g["L0_attn_out_w"], g["L0_attn_out_b"]
    o["gl"], o["gr"] = g["L0_attn_gl_w"][:, 0], g["L0_attn_gr_w"][:, 0]
    o["router"] = g["L0_ffn_router_w"].T
    o["gate_w"] = g["L0_ffn_gate_w"].reshape(NE * FI, P).T
    o["up_w"] = g["L0_ffn_up_w"].reshape(NE * FI, P).T
    down = np.zeros((P, NCH, P), np.float32)
    for e in range(NE):
        for i, (lo, n) in enumerate(E_CHUNKS):
            down[0:n, 3 * e + i, :] = g["L0_ffn_down_w"][e, :, lo:lo + n].T
    o["down_w"] = down
    o["bw2"] = np.concatenate([g["L1_attn_B_w"].T] * 2, 1)
    o["cw2"] = np.concatenate([g["L1_attn_C_w"].T] * 2, 0)
    o["a_col"], o["d_row"] = g["L1_attn_a_params"][:, None], g["L1_attn_D"]
    for l in range(2):
        o[f"wqkv{l}"] = g["L1_ffn_wqkv"][l].reshape(P, 3, INNER)
        o[f"wo{l}"] = g["L1_ffn_wo"][l].reshape(NP, P, P).transpose(1, 0, 2)
        o[f"qk_s{l}0"], o[f"qk_s{l}1"] = g["L1_ffn_q_scale"][l], g["L1_ffn_k_scale"][l]
        o[f"w1_{l}"] = g["L1_ffn_w1"][l]
        w2, b1 = np.zeros((P, 3, P), np.float32), np.zeros((2, P, 3), np.float32)
        for i, (lo, n) in enumerate(H_CHUNKS):
            w2[0:n, i, :] = g["L1_ffn_w2"][l, lo:lo + n, :]
            for j in range(2):
                b1[j, 0:n, i] = g["L1_ffn_b1"][l, j * HID + lo:j * HID + lo + n]
        o[f"w2_{l}"], o[f"b1a{l}"], o[f"b1g{l}"] = w2, b1[0], b1[1]
        o[f"ln_g{l}"], o[f"ln_b{l}"] = g["L1_ffn_ln_g"][l][:, None], g["L1_ffn_ln_b"][l][:, None]
        o[f"b2_{l}"] = g["L1_ffn_b2"][l]
    return o


def kernel(**inputs):
    import concourse.bacc as _bacc
    from concourse.bass_utils import run_bass_kernel_spmd as _run

    nc = _bacc.Bacc("TRN2", target_bir_lowering=False, num_devices=1)
    arrays = {f"in_{n}": np.ascontiguousarray(v) for n, v in {**layout(inputs), **constants()}.items()}
    io = {n[3:]: nc.dram_tensor(n, v.shape, mybir.dt.from_np(v.dtype), kind="ExternalInput").ap()
          for n, v in arrays.items()}
    shape = arrays["in_x"].shape
    out = nc.dram_tensor("out", shape, F32, kind="ExternalOutput").ap()
    build(nc, io, shape[0], out)
    r = _run(nc, [arrays], core_ids=[0])
    return r.results[0]["out"]
```

```python
from contextlib import ExitStack

import numpy as np

import concourse.bass as bass
from concourse import mybir

F32 = mybir.dt.float32
F32R = mybir.dt.float32r
I32 = mybir.dt.int32
ALU = mybir.AluOpType
ACT = mybir.ActivationFunctionType
AX_X = mybir.AxisListType.X

P = 128
NT = 4
S = NT * P
EPS = 1e-5
NEG = -1e30
SLOT = 32
HD0 = 8
NH0 = 16
NG0 = NH0 // 4
NLAT = 64
LH = 4
NE = 8
FI = 352
E_CHUNKS = [(0, 128), (128, 128), (256, 96)]
NCH = NE * len(E_CHUNKS)
NW = 8
W = 64
NP = 4
INNER = 512
HID = 341
H_CHUNKS = [(0, 128), (128, 128), (256, 85)]
GA_BANKS = [(6, 7), (4, 5), (6, 7)]
QK_SCALE = 8.0


def build(nc, io, n_batch, out):
    with ExitStack() as ctx:
        def sb(name, shape, dt=F32):
            return ctx.enter_context(nc.sbuf_tensor(name, shape, dt))

        def sem(name):
            return ctx.enter_context(nc.semaphore(name))

        resident = {}

        def keep(name, shape, dt=F32):
            resident[name] = sb(name, shape, dt)
            return resident[name]

        ident = keep("ident", [P, P])
        wqk = keep("wqk", [P, 8, P])
        bqk = keep("bqk", [P, 8])
        low_rows = keep("low_rows", [P, 8])
        wv0 = keep("wv0", [P, P])
        rq_w = keep("rq_w", [P, 32])
        rq_b = keep("rq_b", [32, 1])
        rk_w = keep("rk_w", [P, 32])
        rk_b = keep("rk_b", [32, 1])
        rv_w = keep("rv_w", [P, 32])
        rout_w = keep("rout_w", [32, P])
        out_w = keep("out_w", [P, P])
        take_prev = keep("take_prev", [P, P], I32)
        key_before = keep("key_before", [P, P])
        key_after = keep("key_after", [P, P])
        lat_mask = keep("lat_mask", [P, NT, NLAT])
        lat_valid = keep("lat_valid", [P, NT])
        own_head = keep("own_head", [32, LH])
        own_half = keep("own_half", [P, 2])
        router = keep("router", [P, NE])
        gate_w = keep("gate_w", [P, NE * FI])
        up_w = keep("up_w", [P, NE * FI])
        down_w = keep("down_w", [P, NCH, P])
        lower_index = keep("lower_index", [P, NE * NE])
        bw2 = keep("bw2", [P, P])
        cw2 = keep("cw2", [P, P])
        omega_w = keep("omega_w", [32, P])
        a_col = keep("a_col", [32, 1])
        up_to = keep("up_to", [P, S])
        wqkv = [keep(f"wqkv{l}", [P, 3, INNER]) for l in range(2)]
        wo = [keep(f"wo{l}", [P, NP, P]) for l in range(2)]
        w1 = [keep(f"w1_{l}", [P, 2 * HID]) for l in range(2)]
        w2 = [keep(f"w2_{l}", [P, 3, P]) for l in range(2)]
        b1a = [keep(f"b1a{l}", [P, 3]) for l in range(2)]
        b1g = [keep(f"b1g{l}", [P, 3]) for l in range(2)]
        ln_g = [keep(f"ln_g{l}", [P, 1]) for l in range(2)]
        ln_b = [keep(f"ln_b{l}", [P, 1]) for l in range(2)]
        win_mask = keep("win_mask", [P, 3, P])
        rows = {}

        def keep_row(name, n):
            rows[name] = sb("row_" + name, [P, n])
            return rows[name]

        v_b = keep_row("v_b", P)
        rv_b = keep_row("rv_b", 32)
        rout_b = keep_row("rout_b", P)
        out_b = keep_row("out_b", P)
        gl = keep_row("gl", HD0)
        gr = keep_row("gr", HD0)
        d_row = keep_row("d_row", P)
        qk_s = [[keep_row(f"qk_s{l}{i}", W) for i in range(2)] for l in range(2)]
        b2 = [keep_row(f"b2_{l}", P) for l in range(2)]

        never = sb("never", [P, P])
        eps4 = sb("eps4", [P, NT])
        minus_half = sb("minus_half", [P, NT])
        low_bias = sb("low_bias", [P, 8])
        omega = sb("omega", [P, 1])
        pw = sb("pw", [P, 12])
        turn_t = sb("turn_t", [P, S])
        turn = sb("turn", [P, NT, P])
        rope_c = [[sb(f"rope_c{l}{i}", [P, NT, W]) for i in range(2)] for l in range(2)]
        rope_s = [[sb(f"rope_s{l}{i}", [P, NT, W]) for i in range(2)] for l in range(2)]

        stats = [sb(f"stats{i}", [P, NT, 6]) for i in range(2)]
        mv = [sb(f"mv{i}", [P, NT, 2]) for i in range(2)]
        veps = [sb(f"veps{i}", [P, NT]) for i in range(2)]
        rstd = [sb(f"rstd{i}", [P, NT]) for i in range(2)]

        def tiles(ap):
            return ap.rearrange("p (t d) -> p t d", t=NT)

        x = sb("x", [P, NT, P])
        xt = sb("xt", [P, S])
        v0 = sb("v0", [P, NT, NH0, HD0 + 1])
        small = sb("small", [P, 8, 64])
        with nc.sbuf_tensor("qk", [P, 8, S], F32) as qk:
            pass
        room = sb("room", [P, 8, S])
        low = sb("low", [P, 2, S])
        pool_t = sb("pool_t", [P, 2, NLAT])
        rk_row = sb("rk_row", [32, NLAT])
        rk_bd = sb("rk_bd", [32, LH, NLAT])
        rv_row = sb("rv_row", [P, 32])
        rv_bd = sb("rv_bd", [P, 2, 2, HD0])
        prob = sb("prob", [P, 3, 4, P])
        pt = sb("pt", [P, 2, 4, P])
        p_cur = sb("p_cur", [P, 2, 4, P])
        p_prev = sb("p_prev", [P, 2, 4, P])
        negmax = sb("negmax", [P, 2, 4])
        o_mid = sb("o_mid", [P, 2, P])
        loc = sb("loc", [P, NT, NH0, HD0 + 1])
        loc_r = sb("loc_r", [P, NT * NH0])
        lat_o = sb("lat_o", [P, NT, 32])
        w_te = sb("w_te", [P, NT, NE])

        def o_t(u):
            if u < 8:
                return low[:, u // 4, (u % 4) * P:(u % 4 + 1) * P]
            if u < 10:
                return o_mid[:, u - 8]
            return room[:, (u - 10) // 4, ((u - 10) % 4) * P:((u - 10) % 4 + 1) * P]

        rqt = prob[0:32, 2].rearrange("p h q -> p (h q)")
        lat_p = p_cur[:].rearrange("p a h q -> p (a h q)")
        lat_t = p_prev[:].rearrange("p a h q -> p (a h) q")
        lat_ot = prob[0:32, 0].rearrange("p h q -> p (h q)")
        remote = prob[:, 1].rearrange("p h q -> p (h q)")
        hid = room[:, 0:2]
        sil = room[:, 2:4]
        tmp = [room[:, 4 + i] for i in range(4)] + [low[:, i] for i in range(2)]
        xn = tiles(tmp[2])

        xr = sb("xr", [P, NT, P])
        y = sb("y", [P, NT, P])
        ht = sb("ht", [P, S])
        shifted = sb("shifted", [P, NT, P])
        rtmp = [sb(f"rtmp{i}", [P, S]) for i in range(2)]
        qr = sb("qr", [P, 4, S])
        qt = sb("qt", [P, 2, NP, S])
        vt = sb("vt", [P, NT, INNER])
        vte = sb("vte", [P, NT - 1, INNER])
        ss = sb("ss", [P, 64])
        nw = sb("nw", [P, 5, 64])
        quad = sb("quad", [P, 4, S])
        wmax = sb("wmax", [P, 4, 12])
        ptw = sb("ptw", [P, 2, NP, P])
        ot = qr
        gel = qt[:, 0, 0:3]
        hn = rtmp[1]
        cos_t, sin_t = quad[:, 0], quad[:, 1]
        rope = [quad[:, 2 + i // 2, 256 * (i % 2):256 * (i % 2) + 256].rearrange("p (t k) -> p t k", t=NT)
                for i in range(4)]
        for i in range(4):
            resident[f"rope{i}"] = rope[i]

        ps = ctx.enter_context(nc.psum_tensor("ps", [P, 8, 512], F32))

        def b4(i):
            return ps[:, i, :].rearrange("p (t d) -> p t d", t=NT)

        loaded = sem("loaded")
        setup_dve = sem("setup_dve")
        setup_pe = sem("setup_pe")
        setup_done = sem("setup_done")
        next_turn = sem("next_turn")

        turn_sems = []

        def tsem(name):
            turn_sems.append(sem(name))
            return turn_sems[-1]

        turn_over = tsem("turn_over")
        x_loaded = tsem("x_loaded")
        x_stored = tsem("x_stored")
        xr_saved = tsem("xr_saved")
        dve_step = tsem("dve_step")
        pool_step = tsem("pool_step")
        NLN = 6
        var_ready = [tsem(f"var_ready{k}") for k in range(NLN)]
        rstd_ready = [tsem(f"rstd_ready{k}") for k in range(NLN)]
        xn_ready = [tsem(f"xn_ready{k}") for k in range(NLN)]
        xt_made = [tsem(f"xt_made{k}") for k in range(NLN - 1)]
        xt_ready = [tsem(f"xt_ready{k}") for k in range(NLN - 1)]
        qk_made, low_ready, qk_split, v0_made, v0_ready = (tsem(n) for n in (
            "qk_made", "low_ready", "qk_split", "v0_made", "v0_ready"))
        pooled, lat_made, lat_split, rq_made, rqt_ready = (tsem(n) for n in (
            "pooled", "lat_made", "lat_split", "rq_made", "rqt_ready"))
        a_scores, a_shifted, a_probs, a_turned, a_pt, a_prev, a_cur, a_pv, a_ot, a_back, a_loc = (tsem(n) for n in (
            "a_scores", "a_shifted", "a_probs", "a_turned", "a_pt", "a_prev", "a_cur", "a_pv", "a_ot", "a_back",
            "a_loc"))
        l_scores, l_shifted, l_probs, l_turned, l_pt, l_out, l_norm, l_back, l_ot, l_remote = (tsem(n) for n in (
            "l_scores", "l_shifted", "l_probs", "l_turned", "l_pt", "l_out", "l_norm", "l_back", "l_ot", "l_remote"))
        rem_ready, g_rem, g_sum, g_gate, mixed_ready, mixed_made, mixed_t, a_proj, x1_ready = (tsem(n) for n in (
            "rem_ready", "g_rem", "g_sum", "g_gate", "mixed_ready", "mixed_made", "mixed_t", "a_proj", "x1_ready"))
        m_logits, m_shifted, m_exp, m_gate, m_silu, m_up, m_hid, m_down, m_added = (tsem(n) for n in (
            "m_logits", "m_shifted", "m_exp", "m_gate", "m_silu", "m_up", "m_hid", "m_down", "m_added"))
        s_in, s_turned, s_sum, s_state, s_skip, s_out, x3_ready = (tsem(n) for n in (
            "s_in", "s_turned", "s_sum", "s_state", "s_skip", "s_out", "x3_ready"))
        x4_ready = tsem("x4_ready")
        PER_LAYER = {"shift": 32, "shift2": 32, "left": 1, "left2": 1, "h_made": 1, "h_ready": 1, "v_made": NT,
                     "v_ready": NT, "vte": 32, "qk_made": 8, "sq": 8, "parts": 8, "rot": 8, "normed": 8,
                     "turned": 8, "qt_ready": 8, "scores": NW, "shifted": NW, "probs": NW, "wsum": NW,
                     "pnorm": NW, "pturn": NW, "ptw": NW, "pv": NW, "ot": NW, "wo": 1, "y_mid": 1, "ga": 3,
                     "gelu": 3, "mlp": 3, "w2": 1, "y_out": 1}
        d = {n: tsem(n if n != "qk_made" else "qk_made_d") for n in PER_LAYER}

        def at(l, name, n):
            return l * PER_LAYER[name] + n

        NORM0 = 2
        QK = NORM0 + 3
        LOCAL = QK + 10
        POOLED = LOCAL + 17
        MOE = LOCAL + 36
        SSM = MOE + 27
        LAYER = [2, 44]
        PROJ, WINDOWS, FF = 3, 17, 31
        LAYER_STEPS = 42
        STEPS = LAYER[1] + LAYER_STEPS + 1
        N_UNITS = NG0 * NT

        def due(s, first, n=1):
            return range(s - first, s - first + 1) if first <= s < first + n else range(0)

        block = ctx.enter_context(nc.Block())
        n_loads = len(resident) + len(rows)

        def run_turns(eng, front, rear, start_turn):
            start_turn()
            for s in range(STEPS):
                front(s)
            eng.drain().then_inc(turn_over, 1)
            eng.wait_ge(next_turn, 1)
            with eng.Fori(0, n_batch - 1) as b:
                start_turn()
                for s in range(STEPS):
                    front(s)
                    rear(s)
                eng.drain().then_inc(turn_over, 1)
                eng.wait_ge(next_turn, b + 2)
            start_turn()
            for s in range(STEPS):
                rear(s)

        @block.sync
        def _(sp):
            for name, t in resident.items():
                sp.dma_start(t[:] if name[:4] != "rope" else t, io[name]).then_inc(loaded, 16)
            for name, t in rows.items():
                sp.dma_start(t[:], io[name].partition_broadcast(P)).then_inc(loaded, 16)

            def load(x_of_turn):
                sp.dma_start(x[:], x_of_turn.rearrange("(t p) d -> p t d", p=P)).then_inc(x_loaded, 16)

            def shift_tokens(which, source_ready, n):
                sp.wait_ge(source_ready, n)
                sem_ = d[which]
                sp.dma_start(shifted[1:P, :, 64:P], y[0:P - 1, :, 64:P]).then_inc(sem_, 16)
                sp.dma_start(shifted[0:1, 1:NT, 64:P], y[P - 1:P, 0:NT - 1, 64:P]).then_inc(sem_, 16)

            def even_values(l):
                sp.wait_ge(d["v_ready"], at(l, "v_ready", NT))
                sp.dma_start(vte[0:W], vt[0:W, 1:NT]).then_inc(d["vte"], 16)
                sp.dma_start(vte[W:P], vt[W:P, 0:NT - 1]).then_inc(d["vte"], 16)

            def rear(out_of_turn):
                shift_tokens("shift", xn_ready[5], 1)
                even_values(0)
                shift_tokens("shift2", d["y_mid"], 1)
                shift_tokens("shift", d["y_out"], 1)
                even_values(1)
                shift_tokens("shift2", d["y_mid"], 2)
                sp.wait_ge(x4_ready, 1)
                sp.dma_start(out_of_turn.rearrange("(t p) d -> p t d", p=P), y[:]).then_inc(x_stored, 16)
                sp.wait_ge(x_stored, 16)

            def end_turn():
                sp.wait_ge(turn_over, 4)
                nums = [s.num for s in turn_sems]
                sp.sem_clear(range(min(nums), max(nums) + 1))
                sp.sem_inc(next_turn, 1)

            load(io["x"][0])
            end_turn()
            x_of_turn, out_of_turn = io["x"][1:n_batch], out[0:n_batch - 1]
            with sp.Fori(0, n_batch - 1) as b:
                sp.wait_ge(xr_saved, 1)
                load(x_of_turn[b])
                rear(out_of_turn[b])
                end_turn()
            rear(out[n_batch - 1])

        @block.gpsimd
        def _(pool):
            G = nc.gpsimd
            G.memset(never[:], NEG)
            G.memset(eps4[:], EPS)
            G.memset(minus_half[:], -0.5)
            G.memset(v0[:, :, :, HD0:HD0 + 1], 1.0)
            G.memset(shifted[0:1, 0, 64:P], 0.0).then_inc(setup_done, 1)
            pool.wait_ge(loaded, 16 * n_loads)
            steps = [0]

            def start_turn():
                steps[0] = 0

            def mark(ins):
                steps[0] += 1
                ins.then_inc(pool_step, 1)
                return steps[0]

            def need(n):
                pool.wait_ge(pool_step, n)

            def inverse_deviation(k):
                i = k // 3
                pool.wait_ge(var_ready[k], 1)
                need(mark(G.tensor_tensor(veps[i][:], mv[i][:, :, 1], eps4[:], ALU.add)))
                G.tensor_tensor(rstd[i][:], veps[i][:], minus_half[:], ALU.pow).then_inc(rstd_ready[k], 1)

            def keys_of_block_before(u):
                if u < NG0:
                    return
                pool.wait_ge(a_pt, u + 1)
                if u >= 2:
                    pool.wait_ge(a_pv, u - 1)
                G.tensor_tensor(p_prev[:, u % 2], pt[:, u % 2], key_after[:].unsqueeze(1).to_broadcast([P, 4, P]),
                                ALU.mult).then_inc(a_prev, 1)

            def gate_argument():
                pool.wait_ge(rem_ready, 1)
                G.tensor_tensor(tmp[1].rearrange("p (n d) -> p n d", d=HD0),
                                remote.rearrange("p (n d) -> p n d", d=HD0),
                                gr[:].unsqueeze(1).to_broadcast([P, NT * NH0, HD0]), ALU.mult).then_inc(g_rem, 1)

            def residual_and_bias():
                pool.wait_ge(a_loc, 1)
                G.tensor_tensor(tiles(tmp[2]), x[:], out_b[:].unsqueeze(1).to_broadcast([P, NT, P]),
                                ALU.add).then_inc(g_rem, 1)

            def skip_path():
                pool.wait_ge(xn_ready[2], 1)
                need(mark(G.tensor_tensor(tiles(tmp[3]), xn[:], d_row[:].unsqueeze(1).to_broadcast([P, NT, P]),
                                          ALU.mult)))
                G.tensor_tensor(tiles(tmp[4]), tiles(tmp[3]), x[:], ALU.add).then_inc(s_skip, 1)

            def front(s):
                for _ in due(s, NORM0):
                    inverse_deviation(0)
                for u in due(s, LOCAL + 4, N_UNITS):
                    keys_of_block_before(u)
                for _ in due(s, LOCAL + 24):
                    residual_and_bias()
                for _ in due(s, LOCAL + 28):
                    gate_argument()
                for _ in due(s, LOCAL + 33):
                    inverse_deviation(1)
                for _ in due(s, SSM):
                    inverse_deviation(2)
                for _ in due(s, SSM + 2):
                    skip_path()

            def left_half(which, source_ready, n):
                pool.wait_ge(source_ready, n)
                G.tensor_copy(shifted[:, :, 0:64], y[:, :, 0:64]).then_inc(d[which], 1)

            def rotated(l, u):
                pool.wait_ge(d["parts"], at(l, "parts", u + 1))
                if u >= 4:
                    pool.wait_ge(d["turned"], at(l, "turned", u - 3))
                G.tensor_tensor(qr[:, u % 4, :], rtmp[u % 2][:], quad[:, 2 + u % 2, :],
                                ALU.add).then_inc(d["rot"], 1)

            def weights(l, w):
                pool.wait_ge(d["wsum"], at(l, "wsum", w + 1))
                q = quad[:, w % 4, :].rearrange("p (n k) -> p n k", n=NP)
                G.tensor_tensor(q, q, wmax[:, w % 4, 8:12].unsqueeze(2).to_broadcast([P, NP, P]),
                                ALU.mult).then_inc(d["pnorm"], 1)

            def rear(s):
                for _ in due(s, 0):
                    inverse_deviation(5)
                for l in range(2):
                    q = s - LAYER[l]
                    for _ in due(q, 0):
                        left_half("left", *((xn_ready[5], 1) if l == 0 else (d["y_out"], 1)))
                    for u in due(q, PROJ + 2, 8):
                        rotated(l, u)
                    for w in due(q, WINDOWS + 3, NW):
                        weights(l, w)
                    for _ in due(q, FF + 1):
                        left_half("left2", d["y_mid"], l + 1)
                    for _ in due(q, FF + 3):
                        inverse_deviation(3 + l)

            run_turns(pool, front, rear, start_turn)

        @block.scalar
        def _(act):
            A = nc.scalar
            act.wait_ge(setup_dve, 1)
            act.wait_ge(setup_done, 1)
            act.wait_ge(loaded, 16 * n_loads)

            def xt_copy(k, bank_):
                act.wait_ge(xt_made[k], 1)
                A.copy(xt[:], ps[:, bank_, :]).then_inc(xt_ready[k], 1)

            def low_rows_of(u):
                act.wait_ge(qk_made, u + 1)
                if u >= 2:
                    act.wait_ge(qk_split, u - 1)
                A.activation(low[:, u % 2, :].bitcast(F32R), ps[:, u % 3, :], ACT.Identity,
                             scale=low_rows[:, u:u + 1], bias=low_bias[:, u:u + 1]).then_inc(low_ready, 1)

            def local_exp(u):
                act.wait_ge(a_shifted, u + 1)
                A.activation(prob[:, u % 3], prob[:, u % 3], ACT.Exp, scale=HD0 ** -0.5).then_inc(a_probs, 1)

            def local_turned(u):
                act.wait_ge(a_turned, u + 1)
                if u >= 2:
                    act.wait_ge(a_cur, u - 1)
                    if u - 2 >= NG0:
                        act.wait_ge(a_prev, u - 1 - NG0)
                A.copy(pt[:, u % 2], ps[:, 2, :].rearrange("p (h q) -> p h q", h=4)).then_inc(a_pt, 1)

            def local_out(u):
                act.wait_ge(a_pv, u + 1)
                if u >= 10:
                    act.wait_ge(a_scores, N_UNITS)
                A.copy(o_t(u), ps[:, 3, 0:P]).then_inc(a_ot, 1)

            def front(s):
                for _ in due(s, NORM0 + 2):
                    xt_copy(0, 3)
                for u in due(s, QK + 1, 8):
                    low_rows_of(u)
                for u in due(s, LOCAL + 6, N_UNITS):
                    local_out(u)
                for u in due(s, LOCAL + 2, N_UNITS):
                    local_exp(u)
                for u in due(s, LOCAL + 3, N_UNITS):
                    local_turned(u)
                for _ in due(s, POOLED + 1):
                    act.wait_ge(rq_made, 1)
                    A.activation(rqt, ps[0:32, 0, :], ACT.Identity, bias=rq_b[:]).then_inc(rqt_ready, 1)
                for _ in due(s, POOLED + 5):
                    act.wait_ge(l_shifted, 1)
                    A.activation(lat_p, lat_p, ACT.Exp, scale=HD0 ** -0.5).then_inc(l_probs, 1)
                for _ in due(s, POOLED + 7):
                    act.wait_ge(l_turned, 1)
                    A.copy(lat_t.rearrange("p u q -> p (u q)"),
                           ps[:, 2:4, :].rearrange("p a b -> p (a b)")).then_inc(l_pt, 1)
                for _ in due(s, POOLED + 9):
                    act.wait_ge(l_back, 1)
                    A.copy(lat_ot, ps[0:32, 1, :]).then_inc(l_ot, 1)
                for _ in due(s, LOCAL + 29):
                    act.wait_ge(g_sum, 1)
                    A.activation(small[:, 1, :], small[:, 0, :], ACT.Sigmoid).then_inc(g_gate, 1)
                for _ in due(s, LOCAL + 31):
                    act.wait_ge(mixed_made, 1)
                    A.copy(xt[:], ps[:, 0, :]).then_inc(mixed_t, 1)
                for _ in due(s, LOCAL + 35):
                    xt_copy(1, 2)
                for _ in due(s, MOE + 2):
                    act.wait_ge(m_shifted, 1)
                    A.activation(small[:, 2, 0:32], small[:, 1, 0:32], ACT.Exp).then_inc(m_exp, 1)
                for c in due(s, MOE, NCH):
                    n = E_CHUNKS[c % 3][1]
                    act.wait_ge(m_gate, c + 1)
                    if c >= 2:
                        act.wait_ge(m_hid, c - 1)
                    A.activation(sil[0:n, c % 2, :], ps[0:n, 0, :], ACT.Silu).then_inc(m_silu, 1)
                for _ in due(s, SSM + 2):
                    xt_copy(2, 0)

            def square(l, u):
                act.wait_ge(d["qk_made"], at(l, "qk_made", u + 1))
                if u >= 2:
                    act.wait_ge(d["parts"], at(l, "parts", u - 1))
                A.activation(quad[:, u % 2, :], ps[:, 4 + u % 3, :], ACT.Square).then_inc(d["sq"], 1)

            def window_turned(l, w):
                act.wait_ge(d["pturn"], at(l, "pturn", w + 1))
                if w >= 2:
                    act.wait_ge(d["pv"], at(l, "pv", w - 1))
                A.copy(ptw[:, w % 2], ps[:, 6, :].rearrange("p (n q) -> p n q", n=NP)).then_inc(d["ptw"], 1)

            def window_out(l, w):
                act.wait_ge(d["pv"], at(l, "pv", w + 1))
                A.copy(ot[:, :, w * W:(w + 1) * W],
                       ps[:, 7, 0:NP * W].rearrange("p (n q) -> p n q", n=NP)).then_inc(d["ot"], 1)

            def rear(s):
                for _ in due(s, 0):
                    A.copy(xr[:], x[:]).then_inc(xr_saved, 1)
                for l in range(2):
                    q = s - LAYER[l]
                    for _ in due(q, PROJ - 1):
                        act.wait_ge(d["h_made"], at(l, "h_made", 1))
                        A.copy(ht[:], ps[:, 7, :]).then_inc(d["h_ready"], 1)
                    for t in due(q, PROJ, NT):
                        act.wait_ge(d["v_made"], at(l, "v_made", t + 1))
                        A.copy(vt[:, t, :], ps[:, 7, :]).then_inc(d["v_ready"], 1)
                    for u in due(q, PROJ, 8):
                        square(l, u)
                    for u in due(q, PROJ + 6, 8):
                        act.wait_ge(d["turned"], at(l, "turned", u + 1))
                        A.copy(qt[:, u // 4, :, (u % 4) * P:(u % 4 + 1) * P],
                               ps[:, 7, :].rearrange("p (n q) -> p n q", n=NP)).then_inc(d["qt_ready"], 1)
                    for w in due(q, WINDOWS + 6, NW):
                        window_out(l, w)
                    for w in due(q, WINDOWS + 2, NW):
                        act.wait_ge(d["shifted"], at(l, "shifted", w + 1))
                        A.activation(quad[:, w % 4, :], quad[:, w % 4, :], ACT.Exp,
                                     scale=QK_SCALE).then_inc(d["probs"], 1)
                    for w in due(q, WINDOWS + 4, NW):
                        window_turned(l, w)
                    for _ in due(q, FF + 5):
                        act.wait_ge(xt_made[3 + l], 1)
                        A.activation(hn[:], ps[:, 5, :], ACT.Identity, scale=ln_g[l][:],
                                     bias=ln_b[l][:]).then_inc(xt_ready[3 + l], 1)
                    for c in due(q, FF + 6, 3):
                        n = H_CHUNKS[c][1]
                        act.wait_ge(d["ga"], at(l, "ga", c + 1))
                        A.activation(gel[0:n, c, :], ps[0:n, GA_BANKS[c][1], :], ACT.Gelu,
                                     bias=b1g[l][0:n, c:c + 1]).then_inc(d["gelu"], 1)

            run_turns(act, front, rear, lambda: None)

        @block.tensor
        def _(pe):
            T = nc.tensor
            pe.wait_ge(loaded, 16 * n_loads)
            T.matmul(ps[:, 0, 0:1], omega_w[:], a_col[:], start=True, stop=True).then_inc(setup_pe, 1)
            pe.wait_ge(setup_dve, 2)
            for t in range(NT):
                last = T.transpose(ps[:, 1, t * P:(t + 1) * P], turn_t[:, t * P:(t + 1) * P], ident[:])
            last.then_inc(setup_pe, 1)
            pe.wait_ge(setup_dve, 3)

            def turn_tiles(src, bank_):
                for t in range(NT):
                    last = T.transpose(ps[:, bank_, t * P:(t + 1) * P], src[:, t, :], ident[:])
                return last

            def project(bank_, w_):
                for t in range(NT):
                    last = T.matmul(b4(bank_)[:, t, :], xt[:, t * P:(t + 1) * P], w_, start=True, stop=True)
                return last

            def scores0(u):
                qb, g = u // NG0, u % NG0
                if u == 0:
                    pe.wait_ge(qk_split, 8)
                    pe.wait_ge(v0_ready, 1)
                    pe.wait_ge(lat_split, 1)
                else:
                    pe.wait_ge(a_shifted, u)
                r = slice(SLOT * g, SLOT * (g + 1))
                first = max(qb - 1, 0) * P
                for h in range(4):
                    o = (h % 2) * 256 + (0 if qb else P)
                    last = T.matmul(ps[:, h // 2, o:(h % 2 + 1) * 256], qk[r, h, qb * P:(qb + 1) * P].bitcast(F32R),
                                    qk[r, 4 + h, first:(qb + 1) * P].bitcast(F32R), start=True, stop=True)
                last.then_inc(a_scores, 1)

            def turned0(u):
                pe.wait_ge(a_probs, u + 1)
                if u:
                    pe.wait_ge(a_pt, u)
                for h in range(4):
                    last = T.transpose(ps[:, 2, h * P:(h + 1) * P], prob[:, u % 3, h, :], ident[:])
                last.then_inc(a_turned, 1)

            def values0(u):
                qb, g = u // NG0, u % NG0
                pe.wait_ge(a_cur, u + 1)
                if qb:
                    pe.wait_ge(a_prev, u + 1 - NG0)
                if u:
                    pe.wait_ge(a_ot, u)
                for h in range(4):
                    o = ps[32 * h:32 * h + HD0 + 1, 3, 0:P]
                    last = T.matmul(o, v0[:, qb, 4 * g + h, :], p_cur[:, u % 2, h, :], start=True, stop=(qb == 0))
                    if qb:
                        last = T.matmul(o, v0[:, qb - 1, 4 * g + h, :], p_prev[:, u % 2, h, :],
                                        start=False, stop=True)
                last.then_inc(a_pv, 1)

            def front(s):
                for _ in due(s, NORM0 + 2):
                    pe.wait_ge(xn_ready[0], 1)
                    turn_tiles(xn, 3).then_inc(xt_made[0], 1)
                for u in due(s, QK, 8):
                    if u == 0:
                        pe.wait_ge(xt_ready[0], 1)
                    if u >= 3:
                        pe.wait_ge(qk_split, u - 2)
                    T.matmul(ps[:, u % 3, :], wqk[:, u, :], xt[:], start=True, stop=True).then_inc(qk_made, 1)
                for _ in due(s, QK + 8):
                    project(3, wv0[:]).then_inc(v0_made, 1)
                    pe.wait_ge(pooled, 1)
                    pe.wait_ge(qk_split, 6)
                    T.matmul(ps[0:32, 2, 0:NLAT], rk_w[:], pool_t[:, 0, :], start=True, stop=True)
                    T.matmul(ps[:, 2, NLAT:NLAT + 32], pool_t[:].rearrange("p a l -> p (a l)"), rv_w[:],
                             start=True, stop=True).then_inc(lat_made, 1)
                for u in due(s, LOCAL + 3, N_UNITS):
                    turned0(u)
                for u in due(s, LOCAL + 5, N_UNITS):
                    values0(u)
                for u in due(s, LOCAL, N_UNITS):
                    scores0(u)
                for _ in due(s, POOLED):
                    pe.wait_ge(a_shifted, N_UNITS)
                    T.matmul(ps[0:32, 0, :], rq_w[:], xt[:], start=True, stop=True).then_inc(rq_made, 1)
                for _ in due(s, POOLED + 2):
                    pe.wait_ge(rqt_ready, 1)
                    for t in range(NT):
                        last = T.matmul(ps[:, t // 2, (t % 2) * 256:(t % 2 + 1) * 256], rqt[:, t * P:(t + 1) * P],
                                        rk_bd[:].rearrange("p h l -> p (h l)"), start=True, stop=True)
                    last.then_inc(l_scores, 1)
                for _ in due(s, LOCAL + 22):
                    pe.wait_ge(a_ot, N_UNITS)
                    pe.wait_ge(l_shifted, 1)
                    for u in range(N_UNITS):
                        last = T.transpose(ps[:, u // NG0, (u % NG0) * P:(u % NG0 + 1) * P],
                                           o_t(u), ident[:])
                    last.then_inc(a_back, 1)
                for _ in due(s, POOLED + 7):
                    pe.wait_ge(l_probs, 1)
                    pe.wait_ge(a_loc, 1)
                    for i in range(8):
                        last = T.transpose(ps[:, 2 + i // 4, (i % 4) * P:(i % 4 + 1) * P],
                                           lat_p[:, i * P:(i + 1) * P], ident[:])
                    last.then_inc(l_turned, 1)
                for _ in due(s, POOLED + 8):
                    pe.wait_ge(l_pt, 1)
                    for t in range(NT):
                        for c in range(2):
                            last = T.matmul(ps[:, 0, t * 32 + c * 16:t * 32 + c * 16 + 16], lat_t[:, 2 * t + c, :],
                                            rv_bd[:, c].rearrange("p a d -> p (a d)"), start=True, stop=True)
                    last.then_inc(l_out, 1)
                for _ in due(s, POOLED + 9):
                    pe.wait_ge(l_norm, 1)
                    for t in range(NT):
                        last = T.transpose(ps[0:32, 1, t * P:(t + 1) * P], lat_o[:, t, :], ident[:])
                    last.then_inc(l_back, 1)
                for _ in due(s, POOLED + 10):
                    pe.wait_ge(l_ot, 1)
                    for t in range(NT):
                        last = T.matmul(b4(2)[:, t, :], lat_ot[:, t * P:(t + 1) * P], rout_w[:],
                                        start=True, stop=True)
                    last.then_inc(l_remote, 1)
                for _ in due(s, LOCAL + 31):
                    pe.wait_ge(mixed_ready, 1)
                    turn_tiles(tiles(tmp[3]), 0).then_inc(mixed_made, 1)
                for _ in due(s, LOCAL + 32):
                    pe.wait_ge(mixed_t, 1)
                    project(1, out_w[:]).then_inc(a_proj, 1)
                for _ in due(s, LOCAL + 35):
                    pe.wait_ge(xn_ready[1], 1)
                    turn_tiles(xn, 2).then_inc(xt_made[1], 1)
                for _ in due(s, MOE):
                    pe.wait_ge(xt_ready[1], 1)
                    for t in range(NT):
                        last = T.matmul(ps[:, 3, t * NE:(t + 1) * NE], xt[:, t * P:(t + 1) * P], router[:],
                                        start=True, stop=True)
                    last.then_inc(m_logits, 1)
                for c in due(s, MOE, NCH):
                    lo, n = E_CHUNKS[c % 3]
                    lo += (c // 3) * FI
                    if c:
                        pe.wait_ge(m_silu, c)
                    T.matmul(ps[0:n, 0, :], gate_w[:, lo:lo + n], xt[:], start=True, stop=True).then_inc(m_gate, 1)
                for c in due(s, MOE + 2, NCH):
                    e, n = c // 3, E_CHUNKS[c % 3][1]
                    pe.wait_ge(m_hid, c + 1)
                    if c == 3:
                        pe.wait_ge(m_shifted, 1)
                    if c % 3 == 0 and e >= 2:
                        pe.wait_ge(m_added, NT * (e - 1))
                    for t in range(NT):
                        last = T.matmul(b4(2 + e % 2)[:, t, :], hid[0:n, c % 2, t * P:(t + 1) * P],
                                        down_w[0:n, c, :], start=(c % 3 == 0 and t == 0), stop=(c % 3 == 2),
                                        skip_group_check=True)
                    last.then_inc(m_down, 1)
                for c in due(s, MOE, NCH):
                    lo, n = E_CHUNKS[c % 3]
                    lo += (c // 3) * FI
                    if c:
                        pe.wait_ge(m_hid, c)
                    T.matmul(ps[0:n, 1, :], up_w[:, lo:lo + n], xt[:], start=True, stop=True).then_inc(m_up, 1)
                for _ in due(s, SSM + 2):
                    pe.wait_ge(xn_ready[2], 1)
                    turn_tiles(xn, 0).then_inc(xt_made[2], 1)
                for _ in due(s, SSM + 3):
                    pe.wait_ge(xt_ready[2], 1)
                    project(1, bw2[:]).then_inc(s_in, 1)
                for _ in due(s, SSM + 5):
                    pe.wait_ge(s_turned, 1)
                    for t in range(NT):
                        last = T.matmul(ps[:, 2, t * P:S], tmp[0][:, t * P:(t + 1) * P], up_to[:, 0:S - t * P],
                                        start=(t == 0), stop=(t == NT - 1), skip_group_check=True)
                    last.then_inc(s_sum, 1)
                for _ in due(s, SSM + 7):
                    pe.wait_ge(s_state, 1)
                    for t in range(NT):
                        last = T.matmul(b4(3)[:, t, :], tmp[1][:, t * P:(t + 1) * P], cw2[:], start=True, stop=True)
                    last.then_inc(s_out, 1)

            def scores(l, w):
                if w >= 2:
                    pe.wait_ge(d["shifted"], at(l, "shifted", w - 1))
                qw = slice(w * W, (w + 1) * W)
                bank_ = 4 + w % 2
                for n in range(NP):
                    for h in range(2):
                        r = slice(W * h, W * h + W)
                        if w % 2:
                            last = T.matmul(ps[r, bank_, n * P:(n + 1) * P], qt[r, 0, n, qw],
                                            qt[r, 1, n, (w - 1) * W:(w + 1) * W], start=True, stop=True)
                        else:
                            before = max(w - 1, 0)
                            T.matmul(ps[r, bank_, n * P:n * P + W], qt[r, 0, n, qw], qt[r, 1, n, qw],
                                     start=True, stop=True)
                            last = T.matmul(ps[r, bank_, n * P + W:(n + 1) * P], qt[r, 0, n, qw],
                                            qt[r, 1, n, before * W:(before + 1) * W], start=True, stop=True)
                last.then_inc(d["scores"], 1)

            def turned(l, w):
                pe.wait_ge(d["pnorm"], at(l, "pnorm", w + 1))
                if w:
                    pe.wait_ge(d["ptw"], at(l, "ptw", w))
                for n in range(NP):
                    last = T.transpose(ps[:, 6, n * P:(n + 1) * P], quad[:, w % 4, n * P:(n + 1) * P], ident[:])
                last.then_inc(d["pturn"], 1)

            def values(l, w):
                pe.wait_ge(d["ptw"], at(l, "ptw", w + 1))
                if w == 2:
                    pe.wait_ge(d["vte"], at(l, "vte", 32))
                if w:
                    pe.wait_ge(d["ot"], at(l, "ot", w))
                t = w // 2
                for n in range(NP):
                    for h in range(2):
                        f = slice((2 * n + h) * W, (2 * n + h + 1) * W)
                        o = ps[W * h:W * h + W, 7, n * W:(n + 1) * W]
                        pcols = slice(h * W, h * W + W)
                        if w:
                            v_ = vt[:, t, f] if w % 2 else vte[:, t - 1, f]
                            last = T.matmul(o, v_, ptw[:, w % 2, n, pcols], start=True, stop=True)
                        else:
                            last = T.matmul(o, vt[0:W, t, f], ptw[0:W, w % 2, n, pcols], start=True, stop=True)
                last.then_inc(d["pv"], 1)

            def rear(s):
                for l in range(2):
                    q = s - LAYER[l]
                    for _ in due(q, PROJ - 1):
                        pe.wait_ge(d["shift"], at(l, "shift", 32))
                        pe.wait_ge(d["left"], at(l, "left", 1))
                        turn_tiles(shifted, 7).then_inc(d["h_made"], 1)
                    for t in due(q, PROJ, NT):
                        pe.wait_ge(d["h_ready"], at(l, "h_ready", 1))
                        if t:
                            pe.wait_ge(d["v_ready"], at(l, "v_ready", t))
                        T.matmul(ps[:, 7, :], ht[:, t * P:(t + 1) * P], wqkv[l][:, 2, :],
                                 start=True, stop=True).then_inc(d["v_made"], 1)
                    for u in due(q, PROJ, 8):
                        if u >= 3:
                            pe.wait_ge(d["parts"], at(l, "parts", u - 2))
                        T.matmul(ps[:, 4 + u % 3, :], ht[:, (u % 4) * P:(u % 4 + 1) * P], wqkv[l][:, u // 4, :],
                                 start=True, stop=True).then_inc(d["qk_made"], 1)
                    for u in due(q, PROJ + 6, 8):
                        pe.wait_ge(d["normed"], at(l, "normed", u + 1))
                        if u:
                            pe.wait_ge(d["qt_ready"], at(l, "qt_ready", u))
                        else:
                            pe.wait_ge(d["v_ready"], at(l, "v_ready", NT))
                        for n in range(NP):
                            last = T.transpose(ps[:, 7, n * P:(n + 1) * P], qr[:, u % 4, n * P:(n + 1) * P],
                                               ident[:])
                        last.then_inc(d["turned"], 1)
                    for w in due(q, WINDOWS + 4, NW):
                        turned(l, w)
                    for w in due(q, WINDOWS + 5, NW):
                        values(l, w)
                    for w in due(q, WINDOWS, NW):
                        if w == 0:
                            pe.wait_ge(d["qt_ready"], at(l, "qt_ready", 8))
                        scores(l, w)
                    for _ in due(q, FF):
                        pe.wait_ge(d["ot"], at(l, "ot", NW))
                        for t in range(NT):
                            for n in range(NP):
                                last = T.matmul(b4(4)[:, t, :], ot[:, n, t * P:(t + 1) * P], wo[l][:, n, :],
                                                start=(n == 0), stop=(n == NP - 1))
                        last.then_inc(d["wo"], 1)
                    for _ in due(q, FF + 5):
                        pe.wait_ge(xn_ready[3 + l], 1)
                        turn_tiles(tiles(rtmp[0][:]), 5).then_inc(xt_made[3 + l], 1)
                    for c in due(q, FF + 6, 3):
                        lo, n = H_CHUNKS[c]
                        value_bank, gate_bank = GA_BANKS[c]
                        if c == 0:
                            pe.wait_ge(xt_ready[3 + l], 1)
                        if c == 2:
                            pe.wait_ge(d["mlp"], at(l, "mlp", 1))
                        T.matmul(ps[0:n, value_bank, :], w1[l][:, lo:lo + n], hn[:], start=True, stop=True)
                        T.matmul(ps[0:n, gate_bank, :], w1[l][:, HID + lo:HID + lo + n], hn[:],
                                 start=True, stop=True).then_inc(d["ga"], 1)
                    for _ in due(q, FF + 10):
                        pe.wait_ge(d["mlp"], at(l, "mlp", 3))
                        for t in range(NT):
                            for c, (lo, n) in enumerate(H_CHUNKS):
                                last = T.matmul(b4(4)[:, t, :], quad[0:n, c, t * P:(t + 1) * P], w2[l][0:n, c, :],
                                                start=(c == 0), stop=(c == 2))
                        last.then_inc(d["w2"], 1)

            run_turns(pe, front, rear, lambda: None)

        @block.vector
        def _(dve):
            V = nc.vector
            steps = [0]
            chain = [sem("setup_chain")]

            def start_turn():
                steps[0] = 0

            def mark(ins):
                steps[0] += 1
                ins.then_inc(chain[0], 1)
                return steps[0]

            def need(n):
                dve.wait_ge(chain[0], n)

            dve.wait_ge(loaded, 16 * n_loads)
            V.tensor_tensor(low_bias[:], low_rows[:], bqk[:], ALU.mult).then_inc(setup_dve, 1)
            for l in range(2):
                for i in range(2):
                    s = qk_s[l][i]
                    V.tensor_tensor(rope_c[l][i][:], rope[2 * i], s[:].unsqueeze(1).to_broadcast([P, NT, W]),
                                    ALU.mult)
                    for a, c in ((0, 32), (32, 0)):
                        V.tensor_tensor(rope_s[l][i][:, :, a:a + 32], rope[2 * i + 1][:, :, a:a + 32],
                                        s[:, c:c + 32].unsqueeze(1).to_broadcast([P, NT, 32]), ALU.mult)
            dve.wait_ge(setup_pe, 1)
            need(mark(V.tensor_copy(omega[:], ps[:, 0, 0:1])))
            need(mark(V.tensor_tensor(pw[:, 0:1], omega[:], omega[:], ALU.mult)))
            V.tensor_scalar(pw[:, 1:2], pw[:, 0:1], 1.0, None, ALU.add)
            need(mark(V.tensor_scalar(pw[:, 2:3], pw[:, 0:1], -1.0, 1.0, ALU.mult, ALU.add)))
            need(mark(V.reciprocal(pw[:, 3:4], pw[:, 1:2])))
            V.tensor_tensor(pw[:, 4:5], pw[:, 2:3], pw[:, 3:4], ALU.mult)
            need(mark(V.scalar_tensor_tensor(pw[:, 5:6], omega[:], 2.0, pw[:, 3:4], ALU.mult, ALU.mult)))
            V.memset(cos_t[:, 0:1], 1.0)
            need(mark(V.memset(sin_t[:, 0:1], 0.0)))
            c0 = 4
            m = 1
            while m < S:
                c_, s_ = pw[:, c0:c0 + 1], pw[:, c0 + 1:c0 + 2]
                V.tensor_scalar(turn_t[:, 0:m], sin_t[:, 0:m], s_, None, ALU.mult)
                need(mark(V.tensor_scalar(tmp[0][:, 0:m], sin_t[:, 0:m], c_, None, ALU.mult)))
                V.scalar_tensor_tensor(cos_t[:, m:2 * m], cos_t[:, 0:m], c_, turn_t[:, 0:m], ALU.mult, ALU.subtract)
                V.scalar_tensor_tensor(sin_t[:, m:2 * m], cos_t[:, 0:m], s_, tmp[0][:, 0:m], ALU.mult, ALU.add)
                n0 = 10 - c0
                need(mark(V.tensor_tensor(pw[:, 8:9], s_, s_, ALU.mult)))
                V.scalar_tensor_tensor(pw[:, n0:n0 + 1], c_, c_, pw[:, 8:9], ALU.mult, ALU.subtract)
                need(mark(V.scalar_tensor_tensor(pw[:, n0 + 1:n0 + 2], c_, 2.0, s_, ALU.mult, ALU.mult)))
                c0 = n0
                m *= 2
            V.tensor_copy(turn_t[0:64, :], cos_t[0:64, :])
            V.tensor_copy(turn_t[64:P, :], sin_t[64:P, :]).then_inc(setup_dve, 1)
            dve.wait_ge(setup_pe, 2)
            V.tensor_copy(turn[:], b4(1)).then_inc(setup_dve, 1)
            dve.wait_ge(setup_dve, 3)
            dve.wait_ge(setup_done, 1)
            chain[0] = dve_step

            def moments(k, src):
                i = k // 3
                for t in range(NT):
                    n = mark(V.bn_stats(stats[i][:, t, :], src[:, t, :]))
                need(n)
                for t in range(NT):
                    last = V.bn_aggr(mv[i][:, t, :], stats[i][:, t, :])
                last.then_inc(var_ready[k], 1)

            def normalise(k, src, dst):
                i = k // 3
                dve.wait_ge(rstd_ready[k], 1)
                for t in range(NT):
                    last = V.tensor_scalar(dst[:, t, :], src[:, t, :], mv[i][:, t, 0:1], rstd[i][:, t:t + 1],
                                           ALU.subtract, ALU.mult)
                last.then_inc(xn_ready[k], 1)

            def pooled_tokens():
                dve.wait_ge(xt_ready[0], 1)
                need(mark(V.tensor_reduce(pool_t[:, 0, :], xt[:].rearrange("p (l c) -> p l c", c=8), AX_X, ALU.add)))
                V.tensor_copy(pool_t[:, 1, :], pool_t[:, 0, :]).then_inc(pooled, 1)

            def pooled_keys_values():
                dve.wait_ge(lat_made, 1)
                V.tensor_scalar(rk_row[:], ps[0:32, 2, 0:NLAT], 0.125, rk_b[:], ALU.mult, ALU.add)
                need(mark(V.scalar_tensor_tensor(rv_row[:], ps[:, 2, NLAT:NLAT + 32], 0.125, rv_b[:],
                                                 ALU.mult, ALU.add)))
                V.tensor_tensor(rk_bd[:], rk_row[:].unsqueeze(1).to_broadcast([32, LH, NLAT]),
                                own_head[:].unsqueeze(2).to_broadcast([32, LH, NLAT]), ALU.mult)
                V.tensor_tensor(rv_bd[:], rv_row[:].rearrange("p (c a d) -> p c a d", c=2, a=2),
                                own_half[:].unsqueeze(1).unsqueeze(3).to_broadcast([P, 2, 2, HD0]),
                                ALU.mult).then_inc(lat_split, 1)

            def shift0(u):
                qb = u // NG0
                dve.wait_ge(a_scores, u + 1)
                both = ps[:, 0:2, :].rearrange("p a (h k) -> p (a h) k", h=2)
                cur = both[:, :, P:2 * P]
                prev = both[:, :, 0:P] if qb else never[:].unsqueeze(1).to_broadcast([P, 4, P])
                need(mark(V.copy_predicated(cur, take_prev[:].unsqueeze(1).to_broadcast([P, 4, P]), prev)))
                if qb:
                    need(mark(V.memset(cur[0:1, :, 0:1], NEG)))
                need(mark(V.tensor_reduce(negmax[:, u % 2, :], cur, AX_X, ALU.max)))
                if u >= 3:
                    dve.wait_ge(a_turned, u - 2)
                V.tensor_tensor(prob[:, u % 3], cur, negmax[:, u % 2, :].unsqueeze(2).to_broadcast([P, 4, P]),
                                ALU.subtract).then_inc(a_shifted, 1)

            def keys_of_block(u):
                dve.wait_ge(a_pt, u + 1)
                if u >= 2:
                    dve.wait_ge(a_pv, u - 1)
                V.tensor_tensor(p_cur[:, u % 2], pt[:, u % 2], key_before[:].unsqueeze(1).to_broadcast([P, 4, P]),
                                ALU.mult).then_inc(a_cur, 1)

            lat3 = lat_p.rearrange("p (t h l) -> p t h l", t=NT, h=LH)
            lat2 = lat_p.rearrange("p (n l) -> p n l", l=NLAT)
            t0 = tmp[0].rearrange("p (n d) -> p n d", d=HD0)
            t3 = tmp[3].rearrange("p (n d) -> p n d", d=HD0)

            def pooled_shift():
                dve.wait_ge(l_scores, 1)
                dve.wait_ge(a_pv, N_UNITS)
                for a in range(2):
                    n = mark(V.tensor_tensor(lat3[:, 2 * a:2 * a + 2],
                                             ps[:, a, :].rearrange("p (t h l) -> p t h l", t=2, h=LH),
                                             lat_mask[:, 2 * a:2 * a + 2].unsqueeze(2).to_broadcast([P, 2, LH, NLAT]),
                                             ALU.add))
                need(n)
                need(mark(V.tensor_reduce(small[:, 2, 0:16], lat2, AX_X, ALU.max)))
                V.tensor_tensor(lat2, lat2, small[:, 2, 0:16].unsqueeze(2).to_broadcast([P, 16, NLAT]),
                                ALU.subtract).then_inc(l_shifted, 1)

            def pooled_sums():
                dve.wait_ge(l_probs, 1)
                need(mark(V.tensor_reduce(small[:, 3, 0:16], lat2, AX_X, ALU.add)))
                need(mark(V.reciprocal(small[:, 4, 0:16], small[:, 3, 0:16])))
                need(mark(V.tensor_tensor(small[:, 5, 0:16].rearrange("p (t h) -> p t h", t=NT),
                                          small[:, 4, 0:16].rearrange("p (t h) -> p t h", t=NT),
                                          lat_valid[:].unsqueeze(2).to_broadcast([P, NT, LH]), ALU.mult)))

            def local_normalised():
                locf = loc[:].rearrange("p t h d -> p (t h) d")
                dve.wait_ge(a_loc, 1)
                need(mark(V.tensor_scalar(loc_r[:], locf[:, :, HD0], 1e-30, None, ALU.max)))
                need(mark(V.reciprocal(small[:, 6, :], loc_r[:])))
                need(mark(V.tensor_tensor(t0, locf[:, :, 0:HD0], small[:, 6, :].unsqueeze(2)
                                          .to_broadcast([P, 64, HD0]), ALU.mult)))
                need(mark(V.tensor_tensor(t3, t0, gl[:].unsqueeze(1).to_broadcast([P, 64, HD0]), ALU.mult)))

            def gate_sum():
                dve.wait_ge(g_rem, 2)
                need(mark(V.tensor_tensor(tmp[3], tmp[3], tmp[1], ALU.add)))
                V.tensor_reduce(small[:, 0, :], t3, AX_X, ALU.add).then_inc(g_sum, 1)
                dve.wait_ge(rem_ready, 1)
                need(mark(V.tensor_tensor(tmp[4], tmp[0], remote, ALU.subtract)))

            def gated():
                dve.wait_ge(g_gate, 1)
                need(mark(V.tensor_tensor(tmp[5].rearrange("p (n d) -> p n d", d=HD0),
                                          tmp[4].rearrange("p (n d) -> p n d", d=HD0),
                                          small[:, 1, :].unsqueeze(2).to_broadcast([P, 64, HD0]), ALU.mult)))
                V.tensor_tensor(tmp[3], tmp[5], remote, ALU.add).then_inc(mixed_ready, 1)

            logits = small[:, 0, 0:32].rearrange("p (t e) -> p t e", e=NE)

            def router_shift():
                dve.wait_ge(m_logits, 1)
                need(mark(V.tensor_copy(small[:, 0, 0:32], ps[:, 3, 0:NT * NE])))
                need(mark(V.tensor_reduce(small[:, 3, 0:NT], logits, AX_X, ALU.max)))
                V.tensor_tensor(small[:, 1, 0:32].rearrange("p (t e) -> p t e", e=NE), logits,
                                small[:, 3, 0:NT].unsqueeze(2).to_broadcast([P, NT, NE]),
                                ALU.subtract).then_inc(m_shifted, 1)

            def ranks():
                sh = [P, NT, NE, NE]
                pair = [t_[:, 0:256].rearrange("p (t e f) -> p t e f", t=NT, e=NE) for t_ in tmp[0:2]]
                other, own = logits.unsqueeze(2).to_broadcast(sh), logits.unsqueeze(3).to_broadcast(sh)
                V.tensor_tensor(pair[0], other, own, ALU.is_gt)
                need(mark(V.tensor_tensor(pair[1], other, own, ALU.is_equal)))
                need(mark(V.tensor_tensor(tmp[2][:, 0:256].rearrange("p (t e) -> p t e", t=NT),
                                          tmp[1][:, 0:256].rearrange("p (t e) -> p t e", t=NT),
                                          lower_index[:].unsqueeze(1).to_broadcast([P, NT, 64]), ALU.mult)))
                need(mark(V.tensor_tensor(tmp[3][:, 0:256], tmp[0][:, 0:256], tmp[2][:, 0:256], ALU.add)))
                need(mark(V.tensor_reduce(small[:, 4, 0:32], tmp[3][:, 0:256].rearrange("p (n f) -> p n f", f=NE),
                                          AX_X, ALU.add)))
                need(mark(V.tensor_scalar(small[:, 5, 0:32], small[:, 4, 0:32], 2.0, None, ALU.is_lt)))

            def router_weights():
                dve.wait_ge(m_exp, 1)
                ex = small[:, 2, 0:32].rearrange("p (t e) -> p t e", e=NE)
                need(mark(V.tensor_reduce(small[:, 3, 8:8 + NT], ex, AX_X, ALU.add)))
                n = mark(V.tensor_tensor(small[:, 6, 0:32], small[:, 2, 0:32], small[:, 5, 0:32], ALU.mult))
                need(mark(V.reciprocal(small[:, 3, 16:16 + NT], small[:, 3, 8:8 + NT])))
                need(mark(V.tensor_tensor(w_te[:], small[:, 6, 0:32].rearrange("p (t e) -> p t e", e=NE),
                                          small[:, 3, 16:16 + NT].unsqueeze(2).to_broadcast([P, NT, NE]), ALU.mult)))

            def product(c):
                n_ = E_CHUNKS[c % 3][1]
                dve.wait_ge(m_silu, c + 1)
                dve.wait_ge(m_up, c + 1)
                if c >= 2:
                    dve.wait_ge(m_down, c - 1)
                V.tensor_tensor(hid[0:n_, c % 2, :], sil[0:n_, c % 2, :], ps[0:n_, 1, :], ALU.mult)\
                    .then_inc(m_hid, 1)

            def add_expert(e):
                dve.wait_ge(m_down, 3 * (e + 1))
                if e:
                    dve.wait_ge(m_added, NT * e)
                for t in range(NT):
                    V.scalar_tensor_tensor(x[:, t, :], b4(2 + e % 2)[:, t, :], w_te[:, t, e:e + 1], x[:, t, :],
                                           ALU.mult, ALU.add).then_inc(m_added, 1)

            def front(s):
                for _ in due(s, NORM0):
                    dve.wait_ge(x_loaded, 16)
                    moments(0, x)
                for _ in due(s, NORM0 + 1):
                    normalise(0, x, xn)
                for u in due(s, QK + 2, 8):
                    dve.wait_ge(low_ready, u + 1)
                    V.scalar_tensor_tensor(qk[:, u, :].bitcast(F32R), ps[:, u % 3, :], bqk[:, u:u + 1],
                                           low[:, u % 2, :], ALU.add, ALU.subtract).then_inc(qk_split, 1)
                for _ in due(s, QK):
                    pooled_tokens()
                for _ in due(s, QK + 9):
                    dve.wait_ge(v0_made, 1)
                    V.tensor_tensor(v0[:, :, :, 0:HD0], b4(3).rearrange("p t (h d) -> p t h d", d=HD0),
                                    v_b[:].rearrange("p (h d) -> p h d", d=HD0).unsqueeze(1)
                                    .to_broadcast([P, NT, NH0, HD0]), ALU.add).then_inc(v0_ready, 1)
                    pooled_keys_values()
                for u in due(s, LOCAL + 1, N_UNITS):
                    shift0(u)
                for u in due(s, LOCAL + 4, N_UNITS):
                    keys_of_block(u)
                for _ in due(s, POOLED + 4):
                    pooled_shift()
                for _ in due(s, LOCAL + 23):
                    dve.wait_ge(a_back, 1)
                    V.tensor_copy(loc[:], ps[:, 0:4, :].rearrange("p t (n s) -> p t n s", s=SLOT)
                                  [:, :, :, 0:HD0 + 1]).then_inc(a_loc, 1)
                for _ in due(s, POOLED + 6):
                    pooled_sums()
                for _ in due(s, LOCAL + 24):
                    local_normalised()
                for _ in due(s, POOLED + 8):
                    dve.wait_ge(l_out, 1)
                    V.tensor_tensor(lat_o[:].rearrange("p t (h d) -> p (t h) d", h=LH),
                                    ps[:, 0, 0:P].rearrange("p (n d) -> p n d", d=HD0),
                                    small[:, 5, 0:16].unsqueeze(2).to_broadcast([P, 16, HD0]), ALU.mult)\
                        .then_inc(l_norm, 1)
                for _ in due(s, LOCAL + 28):
                    dve.wait_ge(l_remote, 1)
                    V.tensor_tensor(tiles(remote), b4(2), rout_b[:].unsqueeze(1).to_broadcast([P, NT, P]),
                                    ALU.add).then_inc(rem_ready, 1)
                for _ in due(s, LOCAL + 29):
                    gate_sum()
                for _ in due(s, LOCAL + 30):
                    gated()
                for _ in due(s, LOCAL + 33):
                    dve.wait_ge(a_proj, 1)
                    V.tensor_tensor(x[:], b4(1), tiles(tmp[2]), ALU.add).then_inc(x1_ready, 1)
                    dve.wait_ge(x1_ready, 1)
                    moments(1, x)
                for _ in due(s, LOCAL + 34):
                    normalise(1, x, xn)
                for c in due(s, MOE + 1, NCH):
                    product(c)
                for _ in due(s, MOE + 1):
                    router_shift()
                for _ in due(s, MOE + 2):
                    ranks()
                for _ in due(s, MOE + 3):
                    router_weights()
                for e in range(NE):
                    for _ in due(s, MOE + 3 * e + 5):
                        add_expert(e)
                for _ in due(s, SSM):
                    dve.wait_ge(m_added, NE * NT)
                    moments(2, x)
                for _ in due(s, SSM + 1):
                    normalise(2, x, xn)
                for _ in due(s, SSM + 4):
                    dve.wait_ge(s_in, 1)
                    V.tensor_tensor(tiles(tmp[0]), b4(1), turn[:], ALU.mult).then_inc(s_turned, 1)
                for _ in due(s, SSM + 6):
                    dve.wait_ge(s_sum, 1)
                    V.tensor_tensor(tmp[1], ps[:, 2, :], turn_t[:], ALU.mult).then_inc(s_state, 1)
                for _ in due(s, SSM + 8):
                    dve.wait_ge(s_skip, 1)
                    dve.wait_ge(s_out, 1)
                    V.tensor_tensor(x[:], b4(3), tiles(tmp[4]), ALU.add).then_inc(x3_ready, 1)

            def h8(ap):
                return ap.rearrange("p (h k) -> p h k", h=8)

            def parts(l, u):
                i, t = u // 4, u % 4
                src = ps[:, 4 + u % 3, :]
                c_part, s_part = rtmp[u % 2][:], quad[:, 2 + u % 2, :]
                dve.wait_ge(d["sq"], at(l, "sq", u + 1))
                if u >= 2:
                    dve.wait_ge(d["rot"], at(l, "rot", u - 1))
                V.tensor_tensor(h8(c_part), h8(src), rope_c[l][i][:, t, :].unsqueeze(1)
                                .to_broadcast([P, 8, W]), ALU.mult)
                for a, c in ((0, 32), (32, 0)):
                    V.tensor_tensor(h8(s_part)[:, :, a:a + 32], h8(src)[:, :, c:c + 32],
                                    rope_s[l][i][:, t, a:a + 32].unsqueeze(1).to_broadcast([P, 8, 32]), ALU.mult)
                V.tensor_reduce(ss[:, 8 * u:8 * u + 8], h8(quad[:, u % 2, :]), AX_X, ALU.add)\
                    .then_inc(d["parts"], 1)

            def inverse_norms(l, i):
                c = slice(32 * i, 32 * i + 32)
                dve.wait_ge(d["parts"], at(l, "parts", 4 * i + 4))
                need(mark(V.tensor_scalar(nw[:, 0, c], ss[:, c], 1e-24, None, ALU.max)))
                need(mark(V.tensor_scalar(nw[:, 1, c].bitcast(I32), nw[:, 0, c].bitcast(I32), 1, None,
                                          ALU.logical_shift_right)))
                need(mark(V.tensor_scalar(nw[:, 2, c].bitcast(I32), nw[:, 1, c].bitcast(I32), -1.0,
                                          float(0x5f3759df), ALU.mult, ALU.add)))
                for k in range(3):
                    old, new = nw[:, 2 - k % 2, c], nw[:, 1 + k % 2, c]
                    need(mark(V.tensor_tensor(nw[:, 3, c], old, old, ALU.mult)))
                    need(mark(V.scalar_tensor_tensor(nw[:, 4, c], nw[:, 3, c], -0.5, nw[:, 0, c],
                                                     ALU.mult, ALU.mult)))
                    need(mark(V.scalar_tensor_tensor(new, nw[:, 4, c], 1.5, old, ALU.add, ALU.mult)))

            def normed(l, u):
                dve.wait_ge(d["rot"], at(l, "rot", u + 1))
                q = h8(qr[:, u % 4, :])
                V.tensor_tensor(q, q, nw[:, 1, 8 * u:8 * u + 8].unsqueeze(2).to_broadcast([P, 8, W]),
                                ALU.mult).then_inc(d["normed"], 1)

            def n4(ap):
                return ap.rearrange("p (n k) -> p n k", n=NP)

            def shift(l, w):
                kind = 0 if w % 2 else (1 if w else 2)
                dve.wait_ge(d["scores"], at(l, "scores", w + 1))
                if w >= 4:
                    dve.wait_ge(d["pturn"], at(l, "pturn", w - 3))
                need(mark(V.tensor_tensor(n4(quad[:, w % 4, :]), n4(ps[:, 4 + w % 2, :]),
                                          win_mask[:, kind, :].unsqueeze(1).to_broadcast([P, NP, P]), ALU.add)))
                need(mark(V.tensor_reduce(wmax[:, w % 4, 0:4], n4(quad[:, w % 4, :]), AX_X, ALU.max)))
                V.tensor_tensor(n4(quad[:, w % 4, :]), n4(quad[:, w % 4, :]),
                                wmax[:, w % 4, 0:4].unsqueeze(2).to_broadcast([P, NP, P]),
                                ALU.subtract).then_inc(d["shifted"], 1)

            def sums(l, w):
                dve.wait_ge(d["probs"], at(l, "probs", w + 1))
                need(mark(V.tensor_reduce(wmax[:, w % 4, 4:8], n4(quad[:, w % 4, :]), AX_X, ALU.add)))
                V.reciprocal(wmax[:, w % 4, 8:12], wmax[:, w % 4, 4:8]).then_inc(d["wsum"], 1)

            def rear(s):
                for _ in due(s, 0):
                    dve.wait_ge(xr_saved, 1)
                    moments(5, xr)
                for _ in due(s, 1):
                    normalise(5, xr, y)
                for l in range(2):
                    q = s - LAYER[l]
                    for i in due(q, PROJ + 5) or due(q, PROJ + 9):
                        inverse_norms(l, int(q == PROJ + 9))
                    for u in due(q, PROJ + 5, 8):
                        normed(l, u)
                    for u in due(q, PROJ + 1, 8):
                        parts(l, u)
                    for w in due(q, WINDOWS + 1, NW):
                        shift(l, w)
                    for w in due(q, WINDOWS + 3, NW):
                        sums(l, w)
                    for _ in due(q, FF + 1):
                        dve.wait_ge(d["wo"], at(l, "wo", 1))
                        if l == 0:
                            dve.wait_ge(xn_ready[5], 1)
                        else:
                            dve.wait_ge(d["y_out"], 1)
                        V.tensor_tensor(y[:], y[:], b4(4), ALU.add).then_inc(d["y_mid"], 1)
                    for _ in due(q, FF + 3):
                        dve.wait_ge(d["shift2"], at(l, "shift2", 32))
                        dve.wait_ge(d["left2"], at(l, "left2", 1))
                        moments(3 + l, shifted)
                    for _ in due(q, FF + 4):
                        normalise(3 + l, shifted, tiles(rtmp[0][:]))
                    for c in due(q, FF + 7, 3):
                        n = H_CHUNKS[c][1]
                        dve.wait_ge(d["gelu"], at(l, "gelu", c + 1))
                        V.scalar_tensor_tensor(quad[0:n, c, :], ps[0:n, GA_BANKS[c][0], :], b1a[l][0:n, c:c + 1],
                                               gel[0:n, c, :], ALU.add, ALU.mult).then_inc(d["mlp"], 1)
                    for _ in due(q, FF + 10):
                        need(mark(V.tensor_tensor(tiles(ht[:]), y[:],
                                                  b2[l][:].unsqueeze(1).to_broadcast([P, NT, P]), ALU.add)))
                    for _ in due(q, LAYER_STEPS):
                        dve.wait_ge(d["w2"], at(l, "w2", 1))
                        V.tensor_tensor(y[:], tiles(ht[:]), b4(4), ALU.add).then_inc(d["y_out"], 1)
                        if l == 1:
                            dve.wait_ge(d["y_out"], 2)
                            V.tensor_tensor(y[:], xr[:], y[:], ALU.add).then_inc(x4_ready, 1)

            run_turns(dve, front, rear, start_turn)


def constants():
    f = np.float32
    p = np.arange(P)
    c = {"ident": np.eye(P, dtype=f)}
    c["take_prev"] = (p[None, :] >= p[:, None]).astype(np.int32)
    c["key_before"] = (p[:, None] < p[None, :]).astype(f)
    c["key_after"] = (p[:, None] >= p[None, :]).astype(f)
    tok = np.arange(S).reshape(NT, P)
    lat = np.where(np.arange(NLAT)[None, None, :] < (tok // 8)[:, :, None], 0.0, NEG).astype(f)
    c["lat_mask"] = np.ascontiguousarray(lat.transpose(1, 0, 2))
    c["lat_valid"] = np.ascontiguousarray((tok >= 8).astype(f).T)
    c["own_head"] = (np.arange(32)[:, None] // 8 == np.arange(LH)[None, :]).astype(f)
    c["own_half"] = (p[:, None] // 64 == np.arange(2)[None, :]).astype(f)
    low = np.zeros((P, 8), f)
    row = p % SLOT
    low[(row >= 16) & (row < 24), 0:4] = 1.0
    low[(row >= 8) & (row < 16), 4:8] = 1.0
    c["low_rows"] = low
    e = np.arange(NE)
    c["lower_index"] = np.ascontiguousarray(np.broadcast_to((e[None, :] < e[:, None]).astype(f).reshape(1, -1), (P, 64)))
    j, k = np.arange(32)[:, None].astype(np.float64), (np.arange(P) % 64)[None, :]
    c["omega_w"] = (-(np.sin(2 * np.pi * (j + 1) * k / 64) + (j >= 1) * np.sin(2 * np.pi * j * k / 64))).astype(f)
    c["up_to"] = (p[:, None] <= np.arange(S)[None, :]).astype(f)
    half = np.arange(0, W, 2, dtype=f)
    inv = f(1.0) / f(10000.0) ** (half / f(W))
    t = np.arange(S, dtype=f)
    fr = (t[:, None] * inv[None, :]).astype(f)
    fr = np.concatenate([fr, fr], -1)
    base = (half + f(0.4) * W) / f(1.4 * W)
    power = (t - S // 2) / f(32)
    scale = base[None, :].astype(f) ** power[:, None].astype(f)
    scale = np.concatenate([scale, scale], -1)
    sign = np.where(np.arange(W) < 32, -1.0, 1.0)
    tabs = [np.cos(fr) * scale, np.sin(fr) * scale * sign, np.cos(fr) / scale, np.sin(fr) / scale * sign]
    for i, a in enumerate(tabs):
        c[f"rope{i}"] = np.ascontiguousarray(a.astype(f).reshape(NT, P, W).transpose(1, 0, 2))
    q, kk = (p % W)[:, None], np.arange(W)[None, :]
    cur, prev = kk <= q, kk >= q
    no = np.zeros_like(cur)
    m = np.stack([np.concatenate([prev, cur], 1), np.concatenate([cur, prev], 1), np.concatenate([cur, no], 1)], 1)
    c["win_mask"] = np.where(m, 0.0, NEG).astype(f)
    return c


def layout(a):
    g = {n: np.asarray(v) for n, v in a.items()}
    o = {"x": g["L0_attn_x"]}
    qkv_w, qkv_b = g["L0_attn_qkv_w"], g["L0_attn_qkv_b"]
    wqk = np.zeros((P, 8, P), np.float32)
    bqk = np.zeros((P, 8), np.float32)
    for i in range(2):
        for h in range(NH0):
            grp, t = h // 4, h % 4
            for r in range(3):
                cols = slice(SLOT * grp + 8 * r, SLOT * grp + 8 * r + 8)
                src = slice(i * P + 8 * h, i * P + 8 * h + 8)
                wqk[:, 4 * i + t, cols] = qkv_w[:, src]
                bqk[cols, 4 * i + t] = qkv_b[src]
    o["wqk"], o["bqk"] = wqk, bqk
    o["wv0"], o["v_b"] = qkv_w[:, 2 * P:], qkv_b[2 * P:]
    o["rq_w"], o["rq_b"] = g["L0_attn_rq_w"], g["L0_attn_rq_b"][:, None]
    o["rk_w"], o["rv_w"] = g["L0_attn_rkv_w"][:, :32], g["L0_attn_rkv_w"][:, 32:]
    o["rk_b"], o["rv_b"] = g["L0_attn_rkv_b"][:32, None], g["L0_attn_rkv_b"][32:]
    o["rout_w"], o["rout_b"] = g["L0_attn_rout_w"], g["L0_attn_rout_b"]
    o["out_w"], o["out_b"] = g["L0_attn_out_w"], g["L0_attn_out_b"]
    o["gl"], o["gr"] = g["L0_attn_gl_w"][:, 0], g["L0_attn_gr_w"][:, 0]
    o["router"] = g["L0_ffn_router_w"].T
    o["gate_w"] = g["L0_ffn_gate_w"].reshape(NE * FI, P).T
    o["up_w"] = g["L0_ffn_up_w"].reshape(NE * FI, P).T
    down = np.zeros((P, NCH, P), np.float32)
    for e in range(NE):
        for i, (lo, n) in enumerate(E_CHUNKS):
            down[0:n, 3 * e + i, :] = g["L0_ffn_down_w"][e, :, lo:lo + n].T
    o["down_w"] = down
    o["bw2"] = np.concatenate([g["L1_attn_B_w"].T] * 2, 1)
    o["cw2"] = np.concatenate([g["L1_attn_C_w"].T] * 2, 0)
    o["a_col"], o["d_row"] = g["L1_attn_a_params"][:, None], g["L1_attn_D"]
    for l in range(2):
        o[f"wqkv{l}"] = g["L1_ffn_wqkv"][l].reshape(P, 3, INNER)
        o[f"wo{l}"] = g["L1_ffn_wo"][l].reshape(NP, P, P).transpose(1, 0, 2)
        o[f"qk_s{l}0"], o[f"qk_s{l}1"] = g["L1_ffn_q_scale"][l], g["L1_ffn_k_scale"][l]
        o[f"w1_{l}"] = g["L1_ffn_w1"][l]
        w2, b1 = np.zeros((P, 3, P), np.float32), np.zeros((2, P, 3), np.float32)
        for i, (lo, n) in enumerate(H_CHUNKS):
            w2[0:n, i, :] = g["L1_ffn_w2"][l, lo:lo + n, :]
            for j in range(2):
                b1[j, 0:n, i] = g["L1_ffn_b1"][l, j * HID + lo:j * HID + lo + n]
        o[f"w2_{l}"], o[f"b1a{l}"], o[f"b1g{l}"] = w2, b1[0], b1[1]
        o[f"ln_g{l}"], o[f"ln_b{l}"] = g["L1_ffn_ln_g"][l][:, None], g["L1_ffn_ln_b"][l][:, None]
        o[f"b2_{l}"] = g["L1_ffn_b2"][l]
    return o


def kernel(**inputs):
    import concourse.bacc as _bacc
    from concourse.bass_utils import run_bass_kernel_spmd as _run

    nc = _bacc.Bacc("TRN2", target_bir_lowering=False, num_devices=1)
    arrays = {f"in_{n}": np.ascontiguousarray(v) for n, v in {**layout(inputs), **constants()}.items()}
    io = {n[3:]: nc.dram_tensor(n, v.shape, mybir.dt.from_np(v.dtype), kind="ExternalInput").ap()
          for n, v in arrays.items()}
    shape = arrays["in_x"].shape
    out = nc.dram_tensor("out", shape, F32, kind="ExternalOutput").ap()
    build(nc, io, shape[0], out)
    r = _run(nc, [arrays], core_ids=[0])
    return r.results[0]["out"]
```

```python
from contextlib import ExitStack

import numpy as np

import concourse.bass as bass
from concourse import mybir

F32 = mybir.dt.float32
F32R = mybir.dt.float32r
I32 = mybir.dt.int32
ALU = mybir.AluOpType
ACT = mybir.ActivationFunctionType
AX_X = mybir.AxisListType.X

P = 128
NT = 4
S = NT * P
EPS = 1e-5
NEG = -1e30
SLOT = 32
HD0 = 8
NH0 = 16
NG0 = NH0 // 4
NLAT = 64
LH = 4
NE = 8
FI = 352
E_CHUNKS = [(0, 128), (128, 128), (256, 96)]
NCH = NE * len(E_CHUNKS)
NW = 8
W = 64
NP = 4
INNER = 512
HID = 341
H_CHUNKS = [(0, 128), (128, 128), (256, 85)]
GA_BANKS = [(6, 7), (4, 5), (6, 7)]
QK_SCALE = 8.0


def build(nc, io, n_batch, out):
    with ExitStack() as ctx:
        def sb(name, shape, dt=F32):
            return ctx.enter_context(nc.sbuf_tensor(name, shape, dt))

        def sem(name):
            return ctx.enter_context(nc.semaphore(name))

        resident = {}

        def keep(name, shape, dt=F32):
            resident[name] = sb(name, shape, dt)
            return resident[name]

        ident = keep("ident", [P, P])
        wqk = keep("wqk", [P, 8, P])
        bqk = keep("bqk", [P, 8])
        low_rows = keep("low_rows", [P, 8])
        wv0 = keep("wv0", [P, P])
        rq_w = keep("rq_w", [P, 32])
        rq_b = keep("rq_b", [32, 1])
        rk_w = keep("rk_w", [P, 32])
        rk_b = keep("rk_b", [32, 1])
        rv_w = keep("rv_w", [P, 32])
        rout_w = keep("rout_w", [32, P])
        out_w = keep("out_w", [P, P])
        take_prev = keep("take_prev", [P, P], I32)
        key_before = keep("key_before", [P, P])
        key_after = keep("key_after", [P, P])
        lat_mask = keep("lat_mask", [P, NT, NLAT])
        lat_valid = keep("lat_valid", [P, NT])
        own_head = keep("own_head", [32, LH])
        own_half = keep("own_half", [P, 2])
        router = keep("router", [P, NE])
        gate_w = keep("gate_w", [P, NE * FI])
        up_w = keep("up_w", [P, NE * FI])
        down_w = keep("down_w", [P, NCH, P])
        lower_index = keep("lower_index", [P, NE * NE])
        bw2 = keep("bw2", [P, P])
        cw2 = keep("cw2", [P, P])
        omega_w = keep("omega_w", [32, P])
        a_col = keep("a_col", [32, 1])
        up_to = keep("up_to", [P, S])
        wqkv = [keep(f"wqkv{l}", [P, 3, INNER]) for l in range(2)]
        wo = [keep(f"wo{l}", [P, NP, P]) for l in range(2)]
        w1 = [keep(f"w1_{l}", [P, 2 * HID]) for l in range(2)]
        w2 = [keep(f"w2_{l}", [P, 3, P]) for l in range(2)]
        b1a = [keep(f"b1a{l}", [P, 3]) for l in range(2)]
        b1g = [keep(f"b1g{l}", [P, 3]) for l in range(2)]
        ln_g = [keep(f"ln_g{l}", [P, 1]) for l in range(2)]
        ln_b = [keep(f"ln_b{l}", [P, 1]) for l in range(2)]
        win_mask = keep("win_mask", [P, 3, P])
        rows = {}

        def keep_row(name, n):
            rows[name] = sb("row_" + name, [P, n])
            return rows[name]

        v_b = keep_row("v_b", P)
        rv_b = keep_row("rv_b", 32)
        rout_b = keep_row("rout_b", P)
        out_b = keep_row("out_b", P)
        gl = keep_row("gl", HD0)
        gr = keep_row("gr", HD0)
        d_row = keep_row("d_row", P)
        qk_s = [[keep_row(f"qk_s{l}{i}", W) for i in range(2)] for l in range(2)]
        b2 = [keep_row(f"b2_{l}", P) for l in range(2)]

        never = sb("never", [P, P])
        eps4 = sb("eps4", [P, NT])
        minus_half = sb("minus_half", [P, NT])
        low_bias = sb("low_bias", [P, 8])
        omega = sb("omega", [P, 1])
        pw = sb("pw", [P, 12])
        turn_t = sb("turn_t", [P, S])
        turn = sb("turn", [P, NT, P])
        rope_c = [[sb(f"rope_c{l}{i}", [P, NT, W]) for i in range(2)] for l in range(2)]
        rope_s = [[sb(f"rope_s{l}{i}", [P, NT, W]) for i in range(2)] for l in range(2)]

        stats = [sb(f"stats{i}", [P, NT, 6]) for i in range(2)]
        mv = [sb(f"mv{i}", [P, NT, 2]) for i in range(2)]
        veps = [sb(f"veps{i}", [P, NT]) for i in range(2)]
        rstd = [sb(f"rstd{i}", [P, NT]) for i in range(2)]

        def tiles(ap):
            return ap.rearrange("p (t d) -> p t d", t=NT)

        x_in = sb("x_in", [P, NT, P])
        x = sb("x", [P, NT, P])
        xt = sb("xt", [P, S])
        v0 = sb("v0", [P, NT, NH0, HD0 + 1])
        small = sb("small", [P, 8, 64])
        with nc.sbuf_tensor("qk", [P, 8, S], F32) as qk:
            pass
        room = sb("room", [P, 8, S])
        low = sb("low", [P, 2, S])
        pool_t = sb("pool_t", [P, 2, NLAT])
        rk_row = sb("rk_row", [32, NLAT])
        rk_bd = sb("rk_bd", [32, LH, NLAT])
        rv_row = sb("rv_row", [P, 32])
        rv_bd = sb("rv_bd", [P, 2, 2, HD0])
        prob = sb("prob", [P, 3, 4, P])
        pt = sb("pt", [P, 2, 4, P])
        p_cur = sb("p_cur", [P, 2, 4, P])
        p_prev = sb("p_prev", [P, 2, 4, P])
        negmax = sb("negmax", [P, 2, 4])
        loc = sb("loc", [P, NT, NH0, HD0 + 1])
        loc_r = sb("loc_r", [P, NT * NH0])
        lat_o = sb("lat_o", [P, NT, 32])
        w_te = sb("w_te", [P, NT, NE])

        def o_t(u):
            if u < 8:
                return low[:, u // 4, (u % 4) * P:(u % 4 + 1) * P]
            if u == 8:
                return lat_o[:].rearrange("p t d -> p (t d)")
            if u == 9:
                return pool_t[:].rearrange("p a l -> p (a l)")
            return room[:, (u - 10) // 4, ((u - 10) % 4) * P:((u - 10) % 4 + 1) * P]

        rqt = prob[0:32, 2].rearrange("p h q -> p (h q)")
        lat_p = p_cur[:].rearrange("p a h q -> p (a h q)")
        lat_t = p_prev[:].rearrange("p a h q -> p (a h) q")
        lat_ot = prob[0:32, 0].rearrange("p h q -> p (h q)")
        remote = prob[:, 1].rearrange("p h q -> p (h q)")
        hid = room[:, 0:2]
        sil = room[:, 2:4]
        tmp = [room[:, 4 + i] for i in range(4)] + [low[:, i] for i in range(2)]
        xn = tiles(tmp[2])

        xr = sb("xr", [P, NT, P])
        y = sb("y", [P, NT, P])
        ht = sb("ht", [P, S])
        shifted = sb("shifted", [P, NT, P])
        rtmp = [sb(f"rtmp{i}", [P, S]) for i in range(2)]
        qr = sb("qr", [P, 4, S])
        qt = sb("qt", [P, 2, NP, S])
        vt = sb("vt", [P, NT, INNER])
        vte = sb("vte", [P, NT - 1, INNER])
        ss = sb("ss", [P, 64])
        nw = sb("nw", [P, 5, 64])
        quad = sb("quad", [P, 4, S])
        wmax = sb("wmax", [P, 4, 4 * NP])
        ptw = sb("ptw", [P, 2, NP, P])
        ot = qr
        gel = qt[:, 0, 0:3]
        hn = rtmp[1]
        cos_t, sin_t = quad[:, 0], quad[:, 1]
        rope = [quad[:, 2 + i // 2, 256 * (i % 2):256 * (i % 2) + 256].rearrange("p (t k) -> p t k", t=NT)
                for i in range(4)]
        for i in range(4):
            resident[f"rope{i}"] = rope[i]

        ps = ctx.enter_context(nc.psum_tensor("ps", [P, 8, 512], F32))

        def b4(i):
            return ps[:, i, :].rearrange("p (t d) -> p t d", t=NT)

        loaded = {g: sem("loaded_" + g) for g in ("first", "attention", "experts", "rear")}
        setup_dve = sem("setup_dve")
        setup_pe = sem("setup_pe")
        setup_done = sem("setup_done")
        next_turn = sem("next_turn")
        x_stored = sem("x_stored")

        turn_sems = []

        def tsem(name):
            turn_sems.append(sem(name))
            return turn_sems[-1]

        turn_over = tsem("turn_over")
        x_loaded = tsem("x_loaded")
        y_free = tsem("y_free")
        dve_step = tsem("dve_step")
        pool_step = tsem("pool_step")
        NLN = 6
        var_ready = [tsem(f"var_ready{k}") for k in range(NLN)]
        rstd_ready = [tsem(f"rstd_ready{k}") for k in range(NLN)]
        xn_ready = [tsem(f"xn_ready{k}") for k in range(NLN)]
        xt_made = [tsem(f"xt_made{k}") for k in range(NLN - 1)]
        xt_ready = [tsem(f"xt_ready{k}") for k in range(NLN - 1)]
        qk_made, low_ready, qk_split, v0_made, v0_ready = (tsem(n) for n in (
            "qk_made", "low_ready", "qk_split", "v0_made", "v0_ready"))
        pooled, lat_made, lat_split, rq_made, rqt_ready = (tsem(n) for n in (
            "pooled", "lat_made", "lat_split", "rq_made", "rqt_ready"))
        a_scores, a_shifted, a_probs, a_turned, a_pt, a_prev, a_cur, a_pv, a_ot, a_back, a_loc = (tsem(n) for n in (
            "a_scores", "a_shifted", "a_probs", "a_turned", "a_pt", "a_prev", "a_cur", "a_pv", "a_ot", "a_back",
            "a_loc"))
        l_scores, l_shifted, l_probs, l_turned, l_pt, l_out, l_norm, l_back, l_ot, l_remote = (tsem(n) for n in (
            "l_scores", "l_shifted", "l_probs", "l_turned", "l_pt", "l_out", "l_norm", "l_back", "l_ot", "l_remote"))
        rem_ready, g_rem, g_sum, g_gate, mixed_ready, mixed_made, mixed_t, a_proj, x1_ready = (tsem(n) for n in (
            "rem_ready", "g_rem", "g_sum", "g_gate", "mixed_ready", "mixed_made", "mixed_t", "a_proj", "x1_ready"))
        m_logits, m_shifted, m_exp, m_gate, m_silu, m_up, m_hid, m_down, m_added = (tsem(n) for n in (
            "m_logits", "m_shifted", "m_exp", "m_gate", "m_silu", "m_up", "m_hid", "m_down", "m_added"))
        s_in, s_turned, s_sum, s_state, s_skip, s_out, x3_ready = (tsem(n) for n in (
            "s_in", "s_turned", "s_sum", "s_state", "s_skip", "s_out", "x3_ready"))
        x4_ready = tsem("x4_ready")
        a_cur_odd = tsem("a_cur_odd")
        PER_LAYER = {"shift": 32, "shift2": 32, "left": 1, "left2": 1, "h_made": 1, "h_ready": 1, "v_made": NT,
                     "v_ready": NT, "vte": 32, "qk_made": 8, "sq": 8, "parts": 8, "rot": 8, "normed": 8,
                     "turned": 8, "qt_ready": 8, "scores": NW, "shifted": NW, "probs": NW, "wsum": NW,
                     "pnorm": NW, "pturn": NW, "ptw": NW, "pv": NW, "ot": NW, "wo": 1, "y_mid": 1, "ga": 3,
                     "gelu": 3, "mlp": 3, "w2": 1, "y_out": 1}
        d = {n: tsem(n if n != "qk_made" else "qk_made_d") for n in PER_LAYER}

        def at(l, name, n):
            return l * PER_LAYER[name] + n

        NORM0 = 0
        QK = NORM0 + 3
        LOCAL = QK + 10
        POOLED = LOCAL + 17
        MOE = LOCAL + 36
        FRONT_STEPS = MOE + 27
        SSM = 0
        LAYER = [10, 52]
        PROJ, WINDOWS, FF = 3, 17, 31
        LAYER_STEPS = 42
        STEPS = LAYER[1] + LAYER_STEPS + 1

        BESIDE = [(0, 0), (MOE, MOE), (MOE + 26, MOE + 13), (STEPS - 1, FRONT_STEPS)]

        def front_steps(s):
            def before(s):
                for (r0, f0), (r1, f1) in zip(BESIDE, BESIDE[1:]):
                    if s < r1:
                        return f0 + (s - r0) * (f1 - f0) // (r1 - r0)
                return FRONT_STEPS
            return range(before(s), before(s + 1))

        N_UNITS = NG0 * NT

        def due(s, first, n=1):
            return range(s - first, s - first + 1) if first <= s < first + n else range(0)

        def wait_cur(eng, u):
            eng.wait_ge(a_cur_odd if u % 2 else a_cur, u // 2 + 1)

        block = ctx.enter_context(nc.Block())

        group = {n: "rear" for n in list(resident) + list(rows)}
        group.update({n: "first" for n in ("ident", "wqk", "bqk", "low_rows", "wv0")})
        group.update({n: "attention" for n in (
            "v_b", "rk_w", "rk_b", "rv_w", "rv_b", "own_head", "own_half", "take_prev", "key_before", "key_after",
            "rq_w", "rq_b", "lat_mask", "lat_valid", "rout_w", "rout_b", "gl", "gr", "out_w", "out_b")})
        group.update({n: "experts" for n in ("router", "gate_w", "up_w", "down_w", "lower_index")})

        def wait_loaded(eng, g):
            n = sum(v == g for v in group.values()) + (g == "first")
            eng.wait_ge(loaded[g], 16 * n)

        def run_turns(eng, front, rear, prepare, start_turn):
            start_turn()
            for s in range(FRONT_STEPS):
                if s == QK + 8:
                    wait_loaded(eng, "attention")
                if s == MOE:
                    wait_loaded(eng, "experts")
                    wait_loaded(eng, "rear")
                front(s)
                prepare(s)
            eng.drain().then_inc(turn_over, 1)
            eng.wait_ge(next_turn, 1)
            with eng.Fori(0, n_batch - 1) as b:
                start_turn()
                for s in range(STEPS):
                    for f in front_steps(s):
                        front(f)
                    rear(s)
                eng.drain().then_inc(turn_over, 1)
                eng.wait_ge(next_turn, b + 2)
            start_turn()
            for s in range(STEPS):
                rear(s)

        @block.sync
        def _(sp):
            def load(x_of_turn, sem_):
                sp.dma_start(x_in[:], x_of_turn.rearrange("(t p) d -> p t d", p=P)).then_inc(sem_, 16)

            load(io["x"][0], loaded["first"])
            for g in loaded:
                for name, of in group.items():
                    if of == g and name in resident:
                        t = resident[name]
                        sp.dma_start(t if name[:4] == "rope" else t[:], io[name]).then_inc(loaded[g], 16)
                    elif of == g:
                        sp.dma_start(rows[name][:], io[name].partition_broadcast(P)).then_inc(loaded[g], 16)

            def prefetch(x_of_next_turn):
                sp.wait_ge(g_rem, 1)
                load(x_of_next_turn, x_loaded)

            def shift_tokens(which, source_ready, n):
                sp.wait_ge(source_ready, n)
                sem_ = d[which]
                sp.dma_start(shifted[1:P, :, 64:P], y[0:P - 1, :, 64:P]).then_inc(sem_, 16)
                sp.dma_start(shifted[0:1, 1:NT, 64:P], y[P - 1:P, 0:NT - 1, 64:P]).then_inc(sem_, 16)

            def even_values(l):
                sp.wait_ge(d["v_ready"], at(l, "v_ready", NT))
                sp.dma_start(vte[0:W], vt[0:W, 1:NT]).then_inc(d["vte"], 16)
                sp.dma_start(vte[W:P], vt[W:P, 0:NT - 1]).then_inc(d["vte"], 16)

            def rear(out_of_turn, stored_before, x_of_next_turn=None):
                sp.wait_ge(x_stored, stored_before)
                sp.sem_inc(y_free, 1)
                shift_tokens("shift", xn_ready[5], 1)
                even_values(0)
                shift_tokens("shift2", d["y_mid"], 1)
                shift_tokens("shift", d["y_out"], 1)
                even_values(1)
                if x_of_next_turn is not None:
                    prefetch(x_of_next_turn)
                shift_tokens("shift2", d["y_mid"], 2)
                sp.wait_ge(x4_ready, 1)
                sp.dma_start(out_of_turn.rearrange("(t p) d -> p t d", p=P), y[:]).then_inc(x_stored, 16)

            def end_turn():
                sp.wait_ge(x_loaded, 16)
                sp.wait_ge(turn_over, 4)
                nums = [s.num for s in turn_sems]
                sp.sem_clear(range(min(nums), max(nums) + 1))
                sp.sem_inc(next_turn, 1)

            prefetch(io["x"][1])
            sp.sem_inc(x_stored, 16)
            end_turn()
            x_of_next_turn, out_of_turn = io["x"][2:n_batch + 1], out[0:n_batch - 1]
            with sp.Fori(0, n_batch - 1) as b:
                rear(out_of_turn[b], 16 * b + 16, x_of_next_turn[b])
                end_turn()
            rear(out[n_batch - 1], 16 * n_batch)
            sp.wait_ge(x_stored, 16 * n_batch + 16)

        @block.gpsimd
        def _(pool):
            G = nc.gpsimd
            G.memset(never[:], NEG)
            G.memset(eps4[:], EPS)
            G.memset(minus_half[:], -0.5)
            G.memset(v0[:, :, :, HD0:HD0 + 1], 1.0)
            G.memset(shifted[0:1, 0, 64:P], 0.0).then_inc(setup_done, 1)
            steps = [0]

            def start_turn():
                steps[0] = 0

            def mark(ins):
                steps[0] += 1
                ins.then_inc(pool_step, 1)
                return steps[0]

            def need(n):
                pool.wait_ge(pool_step, n)

            def inverse_deviation(k):
                i = int(k >= 2)
                pool.wait_ge(var_ready[k], 1)
                need(mark(G.tensor_tensor(veps[i][:], mv[i][:, :, 1], eps4[:], ALU.add)))
                G.tensor_tensor(rstd[i][:], veps[i][:], minus_half[:], ALU.pow).then_inc(rstd_ready[k], 1)

            def keys_of_block_before(u):
                if u < NG0 and u % 2 == 0:
                    return
                pool.wait_ge(a_pt, u + 1)
                if u >= 2:
                    pool.wait_ge(a_pv, u - 1)
                if u % 2:
                    G.tensor_tensor(p_cur[:, u % 2], pt[:, u % 2], key_before[:].unsqueeze(1).to_broadcast([P, 4, P]),
                                    ALU.mult).then_inc(a_cur_odd, 1)
                if u < NG0:
                    return
                G.tensor_tensor(p_prev[:, u % 2], pt[:, u % 2], key_after[:].unsqueeze(1).to_broadcast([P, 4, P]),
                                ALU.mult).then_inc(a_prev, 1)

            def gate_argument():
                pool.wait_ge(rem_ready, 1)
                G.tensor_tensor(tmp[1].rearrange("p (n d) -> p n d", d=HD0),
                                remote.rearrange("p (n d) -> p n d", d=HD0),
                                gr[:].unsqueeze(1).to_broadcast([P, NT * NH0, HD0]), ALU.mult).then_inc(g_rem, 1)

            def residual_and_bias():
                pool.wait_ge(a_loc, 1)
                G.tensor_tensor(tiles(tmp[2]), x_in[:], out_b[:].unsqueeze(1).to_broadcast([P, NT, P]),
                                ALU.add).then_inc(g_rem, 1)

            def skip_path():
                pool.wait_ge(xn_ready[2], 1)
                need(mark(G.tensor_tensor(tiles(quad[:, 2]), tiles(rtmp[0][:]),
                                          d_row[:].unsqueeze(1).to_broadcast([P, NT, P]), ALU.mult)))
                G.tensor_tensor(tiles(quad[:, 3]), tiles(quad[:, 2]), x[:], ALU.add).then_inc(s_skip, 1)

            def front(s):
                for _ in due(s, NORM0):
                    inverse_deviation(0)
                for u in due(s, LOCAL + 4, N_UNITS):
                    keys_of_block_before(u)
                for _ in due(s, LOCAL + 24):
                    residual_and_bias()
                for _ in due(s, LOCAL + 28):
                    gate_argument()
                for _ in due(s, LOCAL + 33):
                    inverse_deviation(1)

            def left_half(which, source_ready, n):
                pool.wait_ge(source_ready, n)
                G.tensor_copy(shifted[:, :, 0:64], y[:, :, 0:64]).then_inc(d[which], 1)

            def rotated(l, u):
                pool.wait_ge(d["parts"], at(l, "parts", u + 1))
                if u >= 4:
                    pool.wait_ge(d["turned"], at(l, "turned", u - 3))
                G.tensor_tensor(qr[:, u % 4, :], rtmp[u % 2][:], quad[:, 2 + u % 2, :],
                                ALU.add).then_inc(d["rot"], 1)

            def weights(l, w):
                pool.wait_ge(d["wsum"], at(l, "wsum", w + 1))
                q = quad[:, w % 4, :].rearrange("p (n k) -> p n k", n=NP)
                G.tensor_tensor(q, q, wmax[:, w % 4, 12:16].unsqueeze(2).to_broadcast([P, NP, P]),
                                ALU.mult).then_inc(d["pnorm"], 1)

            def rear(s):
                for _ in due(s, SSM):
                    inverse_deviation(2)
                for _ in due(s, SSM + 2):
                    skip_path()
                for _ in due(s, SSM + 8):
                    inverse_deviation(5)
                for l in range(2):
                    q = s - LAYER[l]
                    for _ in due(q, 0):
                        left_half("left", *((xn_ready[5], 1) if l == 0 else (d["y_out"], 1)))
                    for u in due(q, PROJ + 2, 8):
                        rotated(l, u)
                    for w in due(q, WINDOWS + 3, NW):
                        weights(l, w)
                    for _ in due(q, FF + 1):
                        left_half("left2", d["y_mid"], l + 1)
                    for _ in due(q, FF + 3):
                        inverse_deviation(3 + l)

            run_turns(pool, front, rear, lambda s: None, start_turn)

        @block.scalar
        def _(act):
            A = nc.scalar
            act.wait_ge(setup_dve, 1)
            wait_loaded(act, "first")

            def xt_copy(k, bank_):
                act.wait_ge(xt_made[k], 1)
                A.copy(xt[:], ps[:, bank_, :]).then_inc(xt_ready[k], 1)

            def low_rows_of(u):
                act.wait_ge(qk_made, u + 1)
                if u >= 2:
                    act.wait_ge(qk_split, u - 1)
                A.activation(low[:, u % 2, :].bitcast(F32R), ps[:, u % 3, :], ACT.Identity,
                             scale=low_rows[:, u:u + 1], bias=low_bias[:, u:u + 1]).then_inc(low_ready, 1)

            def local_exp(u):
                act.wait_ge(a_shifted, u + 1)
                A.activation(prob[:, u % 3], prob[:, u % 3], ACT.Exp, scale=HD0 ** -0.5).then_inc(a_probs, 1)

            def local_turned(u):
                act.wait_ge(a_turned, u + 1)
                if u >= 2:
                    wait_cur(act, u - 2)
                    if u - 2 >= NG0:
                        act.wait_ge(a_prev, u - 1 - NG0)
                A.copy(pt[:, u % 2], ps[:, 2, :].rearrange("p (h q) -> p h q", h=4)).then_inc(a_pt, 1)

            def local_out(u):
                act.wait_ge(a_pv, u + 1)
                if u >= 10:
                    act.wait_ge(a_scores, N_UNITS)
                A.copy(o_t(u), ps[:, 3, 0:P]).then_inc(a_ot, 1)

            def front(s):
                for _ in due(s, NORM0 + 2):
                    xt_copy(0, 3)
                for u in due(s, QK + 1, 8):
                    low_rows_of(u)
                for u in due(s, LOCAL + 2, N_UNITS):
                    local_exp(u)
                for u in due(s, LOCAL + 3, N_UNITS):
                    local_turned(u)
                for u in due(s, LOCAL + 5, N_UNITS):
                    local_out(u)
                for _ in due(s, POOLED + 1):
                    act.wait_ge(rq_made, 1)
                    A.activation(rqt, ps[0:32, 0, :], ACT.Identity, bias=rq_b[:]).then_inc(rqt_ready, 1)
                for _ in due(s, POOLED + 5):
                    act.wait_ge(l_shifted, 1)
                    A.activation(lat_p, lat_p, ACT.Exp, scale=HD0 ** -0.5).then_inc(l_probs, 1)
                for _ in due(s, POOLED + 7):
                    act.wait_ge(l_turned, 1)
                    A.copy(lat_t.rearrange("p u q -> p (u q)"),
                           ps[:, 2:4, :].rearrange("p a b -> p (a b)")).then_inc(l_pt, 1)
                for _ in due(s, POOLED + 9):
                    act.wait_ge(l_back, 1)
                    A.copy(lat_ot, ps[0:32, 1, :]).then_inc(l_ot, 1)
                for _ in due(s, LOCAL + 29):
                    act.wait_ge(g_sum, 1)
                    A.activation(small[:, 1, :], small[:, 0, :], ACT.Tanh, scale=0.5).then_inc(g_gate, 1)
                for _ in due(s, LOCAL + 31):
                    act.wait_ge(mixed_made, 1)
                    A.copy(xt[:], ps[:, 0, :]).then_inc(mixed_t, 1)
                for _ in due(s, LOCAL + 35):
                    xt_copy(1, 2)
                for _ in due(s, MOE + 2):
                    act.wait_ge(m_shifted, 1)
                    A.activation(small[:, 2, 0:32], small[:, 1, 0:32], ACT.Exp).then_inc(m_exp, 1)
                for c in due(s, MOE, NCH):
                    n = E_CHUNKS[c % 3][1]
                    act.wait_ge(m_gate, c + 1)
                    if c >= 2:
                        act.wait_ge(m_hid, c - 1)
                    A.activation(sil[0:n, c % 2, :], ps[0:n, 0, :], ACT.Silu).then_inc(m_silu, 1)

            def square(l, u):
                act.wait_ge(d["qk_made"], at(l, "qk_made", u + 1))
                if u >= 2:
                    act.wait_ge(d["parts"], at(l, "parts", u - 1))
                A.activation(quad[:, u % 2, :], ps[:, 4 + u % 3, :], ACT.Square).then_inc(d["sq"], 1)

            def window_turned(l, w):
                act.wait_ge(d["pturn"], at(l, "pturn", w + 1))
                if w >= 2:
                    act.wait_ge(d["pv"], at(l, "pv", w - 1))
                A.copy(ptw[:, w % 2], ps[:, 6, :].rearrange("p (n q) -> p n q", n=NP)).then_inc(d["ptw"], 1)

            def window_out(l, w):
                act.wait_ge(d["pv"], at(l, "pv", w + 1))
                A.copy(ot[:, :, w * W:(w + 1) * W],
                       ps[:, 7, 0:NP * W].rearrange("p (n q) -> p n q", n=NP)).then_inc(d["ot"], 1)

            def rear(s):
                for _ in due(s, SSM + 2):
                    act.wait_ge(xt_made[2], 1)
                    A.copy(ht[:], ps[:, 4, :]).then_inc(xt_ready[2], 1)
                for l in range(2):
                    q = s - LAYER[l]
                    for _ in due(q, PROJ - 1):
                        act.wait_ge(d["h_made"], at(l, "h_made", 1))
                        A.copy(ht[:], ps[:, 7, :]).then_inc(d["h_ready"], 1)
                    for t in due(q, PROJ, NT):
                        act.wait_ge(d["v_made"], at(l, "v_made", t + 1))
                        A.copy(vt[:, t, :], ps[:, 7, :]).then_inc(d["v_ready"], 1)
                    for u in due(q, PROJ, 8):
                        square(l, u)
                    for u in due(q, PROJ + 6, 8):
                        act.wait_ge(d["turned"], at(l, "turned", u + 1))
                        A.copy(qt[:, u // 4, :, (u % 4) * P:(u % 4 + 1) * P],
                               ps[:, 7, :].rearrange("p (n q) -> p n q", n=NP)).then_inc(d["qt_ready"], 1)
                    for w in due(q, WINDOWS + 2, NW):
                        act.wait_ge(d["shifted"], at(l, "shifted", w + 1))
                        for n in range(NP):
                            q_ = quad[:, w % 4, n * P:(n + 1) * P]
                            last = A.activation(q_, q_, ACT.Exp, scale=QK_SCALE, bias=wmax[:, w % 4, 4 + n:5 + n],
                                                accum_out=wmax[:, w % 4, 8 + n:9 + n])
                        last.then_inc(d["probs"], 1)
                    for w in due(q, WINDOWS + 4, NW):
                        window_turned(l, w)
                    for w in due(q, WINDOWS + 5, NW):
                        window_out(l, w)
                    for _ in due(q, FF + 5):
                        act.wait_ge(xt_made[3 + l], 1)
                        A.activation(hn[:], ps[:, 5, :], ACT.Identity, scale=ln_g[l][:],
                                     bias=ln_b[l][:]).then_inc(xt_ready[3 + l], 1)
                    for c in due(q, FF + 6, 3):
                        n = H_CHUNKS[c][1]
                        act.wait_ge(d["ga"], at(l, "ga", c + 1))
                        A.activation(gel[0:n, c, :], ps[0:n, GA_BANKS[c][1], :], ACT.Gelu,
                                     bias=b1g[l][0:n, c:c + 1]).then_inc(d["gelu"], 1)

            run_turns(act, front, rear, lambda s: None, lambda: None)

        @block.tensor
        def _(pe):
            T = nc.tensor
            wait_loaded(pe, "first")

            def prepare(s):
                for _ in due(s, MOE):
                    T.matmul(ps[:, 4, 0:1], omega_w[:], a_col[:], start=True, stop=True).then_inc(setup_pe, 1)
                for _ in due(s, MOE + 12):
                    pe.wait_ge(setup_dve, 2)
                    for t in range(NT):
                        last = T.transpose(ps[:, 5, t * P:(t + 1) * P], turn_t[:, t * P:(t + 1) * P], ident[:])
                    last.then_inc(setup_pe, 1)

            def turn_tiles(src, bank_):
                for t in range(NT):
                    last = T.transpose(ps[:, bank_, t * P:(t + 1) * P], src[:, t, :], ident[:])
                return last

            def project(bank_, rows_, w_):
                for t in range(NT):
                    last = T.matmul(b4(bank_)[:, t, :], rows_[:, t * P:(t + 1) * P], w_, start=True, stop=True)
                return last

            def scores0(u):
                qb, g = u // NG0, u % NG0
                if u == 0:
                    pe.wait_ge(qk_split, 8)
                    pe.wait_ge(v0_ready, 1)
                    pe.wait_ge(lat_split, 1)
                else:
                    pe.wait_ge(a_shifted, u)
                r = slice(SLOT * g, SLOT * (g + 1))
                first = max(qb - 1, 0) * P
                for h in range(4):
                    o = (h % 2) * 256 + (0 if qb else P)
                    last = T.matmul(ps[:, h // 2, o:(h % 2 + 1) * 256], qk[r, h, qb * P:(qb + 1) * P].bitcast(F32R),
                                    qk[r, 4 + h, first:(qb + 1) * P].bitcast(F32R), start=True, stop=True)
                last.then_inc(a_scores, 1)

            def turned0(u):
                pe.wait_ge(a_probs, u + 1)
                if u:
                    pe.wait_ge(a_pt, u)
                for h in range(4):
                    last = T.transpose(ps[:, 2, h * P:(h + 1) * P], prob[:, u % 3, h, :], ident[:])
                last.then_inc(a_turned, 1)

            def values0(u):
                qb, g = u // NG0, u % NG0
                wait_cur(pe, u)
                if qb:
                    pe.wait_ge(a_prev, u + 1 - NG0)
                if u:
                    pe.wait_ge(a_ot, u)
                for h in range(4):
                    o = ps[32 * h:32 * h + HD0 + 1, 3, 0:P]
                    last = T.matmul(o, v0[:, qb, 4 * g + h, :], p_cur[:, u % 2, h, :], start=True, stop=(qb == 0))
                    if qb:
                        last = T.matmul(o, v0[:, qb - 1, 4 * g + h, :], p_prev[:, u % 2, h, :],
                                        start=False, stop=True)
                last.then_inc(a_pv, 1)

            def front(s):
                for _ in due(s, NORM0 + 2):
                    pe.wait_ge(xn_ready[0], 1)
                    turn_tiles(xn, 3).then_inc(xt_made[0], 1)
                for u in due(s, QK, 8):
                    if u == 0:
                        pe.wait_ge(xt_ready[0], 1)
                    if u >= 3:
                        pe.wait_ge(qk_split, u - 2)
                    T.matmul(ps[:, u % 3, :], wqk[:, u, :], xt[:], start=True, stop=True).then_inc(qk_made, 1)
                for _ in due(s, QK + 8):
                    project(3, xt, wv0[:]).then_inc(v0_made, 1)
                    pe.wait_ge(pooled, 1)
                    pe.wait_ge(qk_split, 6)
                    T.matmul(ps[0:32, 2, 0:NLAT], rk_w[:], pool_t[:, 0, :], start=True, stop=True)
                    T.matmul(ps[:, 2, NLAT:NLAT + 32], pool_t[:].rearrange("p a l -> p (a l)"), rv_w[:],
                             start=True, stop=True).then_inc(lat_made, 1)
                for u in due(s, LOCAL + 3, N_UNITS):
                    turned0(u)
                for u in due(s, LOCAL + 5, N_UNITS):
                    values0(u)
                for u in due(s, LOCAL, N_UNITS):
                    scores0(u)
                for _ in due(s, POOLED):
                    pe.wait_ge(a_shifted, N_UNITS)
                    T.matmul(ps[0:32, 0, :], rq_w[:], xt[:], start=True, stop=True).then_inc(rq_made, 1)
                for _ in due(s, POOLED + 2):
                    pe.wait_ge(rqt_ready, 1)
                    for t in range(NT):
                        last = T.matmul(ps[:, t // 2, (t % 2) * 256:(t % 2 + 1) * 256], rqt[:, t * P:(t + 1) * P],
                                        rk_bd[:].rearrange("p h l -> p (h l)"), start=True, stop=True)
                    last.then_inc(l_scores, 1)
                for _ in due(s, LOCAL + 22):
                    pe.wait_ge(a_ot, N_UNITS)
                    pe.wait_ge(l_shifted, 1)
                    for u in range(N_UNITS):
                        last = T.transpose(ps[:, u // NG0, (u % NG0) * P:(u % NG0 + 1) * P],
                                           o_t(u), ident[:])
                    last.then_inc(a_back, 1)
                for _ in due(s, POOLED + 7):
                    pe.wait_ge(l_probs, 1)
                    pe.wait_ge(a_loc, 1)
                    for i in range(8):
                        last = T.transpose(ps[:, 2 + i // 4, (i % 4) * P:(i % 4 + 1) * P],
                                           lat_p[:, i * P:(i + 1) * P], ident[:])
                    last.then_inc(l_turned, 1)
                for _ in due(s, POOLED + 8):
                    pe.wait_ge(l_pt, 1)
                    for t in range(NT):
                        for c in range(2):
                            last = T.matmul(ps[:, 0, t * 32 + c * 16:t * 32 + c * 16 + 16], lat_t[:, 2 * t + c, :],
                                            rv_bd[:, c].rearrange("p a d -> p (a d)"), start=True, stop=True)
                    last.then_inc(l_out, 1)
                for _ in due(s, POOLED + 9):
                    pe.wait_ge(l_norm, 1)
                    for t in range(NT):
                        last = T.transpose(ps[0:32, 1, t * P:(t + 1) * P], lat_o[:, t, :], ident[:])
                    last.then_inc(l_back, 1)
                for _ in due(s, POOLED + 10):
                    pe.wait_ge(l_ot, 1)
                    for t in range(NT):
                        last = T.matmul(b4(2)[:, t, :], lat_ot[:, t * P:(t + 1) * P], rout_w[:],
                                        start=True, stop=True)
                    last.then_inc(l_remote, 1)
                for _ in due(s, LOCAL + 31):
                    pe.wait_ge(mixed_ready, 1)
                    turn_tiles(tiles(tmp[3]), 0).then_inc(mixed_made, 1)
                for _ in due(s, LOCAL + 32):
                    pe.wait_ge(mixed_t, 1)
                    project(1, xt, out_w[:]).then_inc(a_proj, 1)
                for _ in due(s, LOCAL + 35):
                    pe.wait_ge(xn_ready[1], 1)
                    turn_tiles(xn, 2).then_inc(xt_made[1], 1)
                for _ in due(s, MOE):
                    pe.wait_ge(xt_ready[1], 1)
                    for t in range(NT):
                        last = T.matmul(ps[:, 3, t * NE:(t + 1) * NE], xt[:, t * P:(t + 1) * P], router[:],
                                        start=True, stop=True)
                    last.then_inc(m_logits, 1)
                for c in due(s, MOE, NCH):
                    lo, n = E_CHUNKS[c % 3]
                    lo += (c // 3) * FI
                    if c:
                        pe.wait_ge(m_silu, c)
                    T.matmul(ps[0:n, 0, :], gate_w[:, lo:lo + n], xt[:], start=True, stop=True).then_inc(m_gate, 1)
                for c in due(s, MOE + 2, NCH):
                    e, n = c // 3, E_CHUNKS[c % 3][1]
                    pe.wait_ge(m_hid, c + 1)
                    if c == 3:
                        pe.wait_ge(m_shifted, 1)
                    if c % 3 == 0 and e >= 2:
                        pe.wait_ge(m_added, NT * (e - 1))
                    for t in range(NT):
                        last = T.matmul(b4(2 + e % 2)[:, t, :], hid[0:n, c % 2, t * P:(t + 1) * P],
                                        down_w[0:n, c, :], start=(c % 3 == 0 and t == 0), stop=(c % 3 == 2),
                                        skip_group_check=True)
                    last.then_inc(m_down, 1)
                for c in due(s, MOE, NCH):
                    lo, n = E_CHUNKS[c % 3]
                    lo += (c // 3) * FI
                    if c:
                        pe.wait_ge(m_hid, c)
                    T.matmul(ps[0:n, 1, :], up_w[:, lo:lo + n], xt[:], start=True, stop=True).then_inc(m_up, 1)

            def scores(l, w):
                if w >= 2:
                    pe.wait_ge(d["shifted"], at(l, "shifted", w - 1))
                qw = slice(w * W, (w + 1) * W)
                bank_ = 4 + w % 2
                for n in range(NP):
                    for h in range(2):
                        r = slice(W * h, W * h + W)
                        if w % 2:
                            last = T.matmul(ps[r, bank_, n * P:(n + 1) * P], qt[r, 0, n, qw],
                                            qt[r, 1, n, (w - 1) * W:(w + 1) * W], start=True, stop=True)
                        else:
                            before = max(w - 1, 0)
                            T.matmul(ps[r, bank_, n * P:n * P + W], qt[r, 0, n, qw], qt[r, 1, n, qw],
                                     start=True, stop=True)
                            last = T.matmul(ps[r, bank_, n * P + W:(n + 1) * P], qt[r, 0, n, qw],
                                            qt[r, 1, n, before * W:(before + 1) * W], start=True, stop=True)
                last.then_inc(d["scores"], 1)

            def turned(l, w):
                pe.wait_ge(d["pnorm"], at(l, "pnorm", w + 1))
                if w:
                    pe.wait_ge(d["ptw"], at(l, "ptw", w))
                for n in range(NP):
                    last = T.transpose(ps[:, 6, n * P:(n + 1) * P], quad[:, w % 4, n * P:(n + 1) * P], ident[:])
                last.then_inc(d["pturn"], 1)

            def values(l, w):
                pe.wait_ge(d["ptw"], at(l, "ptw", w + 1))
                if w == 2:
                    pe.wait_ge(d["vte"], at(l, "vte", 32))
                if w:
                    pe.wait_ge(d["ot"], at(l, "ot", w))
                t = w // 2
                for n in range(NP):
                    for h in range(2):
                        f = slice((2 * n + h) * W, (2 * n + h + 1) * W)
                        o = ps[W * h:W * h + W, 7, n * W:(n + 1) * W]
                        pcols = slice(h * W, h * W + W)
                        if w:
                            v_ = vt[:, t, f] if w % 2 else vte[:, t - 1, f]
                            last = T.matmul(o, v_, ptw[:, w % 2, n, pcols], start=True, stop=True)
                        else:
                            last = T.matmul(o, vt[0:W, t, f], ptw[0:W, w % 2, n, pcols], start=True, stop=True)
                last.then_inc(d["pv"], 1)

            def rear(s):
                for _ in due(s, SSM + 2):
                    pe.wait_ge(xn_ready[2], 1)
                    turn_tiles(tiles(rtmp[0][:]), 4).then_inc(xt_made[2], 1)
                for _ in due(s, SSM + 3):
                    pe.wait_ge(xt_ready[2], 1)
                    project(5, ht, bw2[:]).then_inc(s_in, 1)
                for _ in due(s, SSM + 5):
                    pe.wait_ge(s_turned, 1)
                    for t in range(NT):
                        last = T.matmul(ps[:, 6, t * P:S], quad[:, 0, t * P:(t + 1) * P], up_to[:, 0:S - t * P],
                                        start=(t == 0), stop=(t == NT - 1), skip_group_check=True)
                    last.then_inc(s_sum, 1)
                for _ in due(s, SSM + 7):
                    pe.wait_ge(s_state, 1)
                    project(7, quad[:, 1], cw2[:]).then_inc(s_out, 1)
                for l in range(2):
                    q = s - LAYER[l]
                    for _ in due(q, PROJ - 1):
                        pe.wait_ge(d["shift"], at(l, "shift", 32))
                        pe.wait_ge(d["left"], at(l, "left", 1))
                        turn_tiles(shifted, 7).then_inc(d["h_made"], 1)
                    for t in due(q, PROJ, NT):
                        pe.wait_ge(d["h_ready"], at(l, "h_ready", 1))
                        if t:
                            pe.wait_ge(d["v_ready"], at(l, "v_ready", t))
                        T.matmul(ps[:, 7, :], ht[:, t * P:(t + 1) * P], wqkv[l][:, 2, :],
                                 start=True, stop=True).then_inc(d["v_made"], 1)
                    for u in due(q, PROJ, 8):
                        if u >= 3:
                            pe.wait_ge(d["parts"], at(l, "parts", u - 2))
                        T.matmul(ps[:, 4 + u % 3, :], ht[:, (u % 4) * P:(u % 4 + 1) * P], wqkv[l][:, u // 4, :],
                                 start=True, stop=True).then_inc(d["qk_made"], 1)
                    for u in due(q, PROJ + 6, 8):
                        pe.wait_ge(d["normed"], at(l, "normed", u + 1))
                        if u:
                            pe.wait_ge(d["qt_ready"], at(l, "qt_ready", u))
                        else:
                            pe.wait_ge(d["v_ready"], at(l, "v_ready", NT))
                        for n in range(NP):
                            last = T.transpose(ps[:, 7, n * P:(n + 1) * P], qr[:, u % 4, n * P:(n + 1) * P],
                                               ident[:])
                        last.then_inc(d["turned"], 1)
                    for w in due(q, WINDOWS + 4, NW):
                        turned(l, w)
                    for w in due(q, WINDOWS + 5, NW):
                        values(l, w)
                    for w in due(q, WINDOWS, NW):
                        if w == 0:
                            pe.wait_ge(d["qt_ready"], at(l, "qt_ready", 8))
                        scores(l, w)
                    for _ in due(q, FF):
                        pe.wait_ge(d["ot"], at(l, "ot", NW))
                        for t in range(NT):
                            for n in range(NP):
                                last = T.matmul(b4(4)[:, t, :], ot[:, n, t * P:(t + 1) * P], wo[l][:, n, :],
                                                start=(n == 0), stop=(n == NP - 1))
                        last.then_inc(d["wo"], 1)
                    for _ in due(q, FF + 5):
                        pe.wait_ge(xn_ready[3 + l], 1)
                        turn_tiles(tiles(rtmp[0][:]), 5).then_inc(xt_made[3 + l], 1)
                    for c in due(q, FF + 6, 3):
                        lo, n = H_CHUNKS[c]
                        value_bank, gate_bank = GA_BANKS[c]
                        if c == 0:
                            pe.wait_ge(xt_ready[3 + l], 1)
                        if c == 2:
                            pe.wait_ge(d["mlp"], at(l, "mlp", 1))
                        T.matmul(ps[0:n, value_bank, :], w1[l][:, lo:lo + n], hn[:], start=True, stop=True)
                        T.matmul(ps[0:n, gate_bank, :], w1[l][:, HID + lo:HID + lo + n], hn[:],
                                 start=True, stop=True).then_inc(d["ga"], 1)
                    for _ in due(q, FF + 10):
                        pe.wait_ge(d["mlp"], at(l, "mlp", 3))
                        for t in range(NT):
                            for c, (lo, n) in enumerate(H_CHUNKS):
                                last = T.matmul(b4(4)[:, t, :], quad[0:n, c, t * P:(t + 1) * P], w2[l][0:n, c, :],
                                                start=(c == 0), stop=(c == 2))
                        last.then_inc(d["w2"], 1)

            run_turns(pe, front, rear, prepare, lambda: None)

        @block.vector
        def _(dve):
            V = nc.vector
            steps = [0]

            def start_turn():
                steps[0] = 0

            def mark(ins):
                steps[0] += 1
                ins.then_inc(dve_step, 1)
                return steps[0]

            def need(n):
                dve.wait_ge(dve_step, n)

            wait_loaded(dve, "first")
            V.tensor_tensor(low_bias[:], low_rows[:], bqk[:], ALU.mult).then_inc(setup_dve, 1)
            dve.wait_ge(setup_done, 1)

            def prepare(s):
                for i in due(s, MOE + 14, 4):
                    l, i = i // 2, i % 2
                    scale = qk_s[l][i]
                    V.tensor_tensor(rope_c[l][i][:], rope[2 * i], scale[:].unsqueeze(1).to_broadcast([P, NT, W]),
                                    ALU.mult)
                    for a, c in ((0, 32), (32, 0)):
                        V.tensor_tensor(rope_s[l][i][:, :, a:a + 32], rope[2 * i + 1][:, :, a:a + 32],
                                        scale[:, c:c + 32].unsqueeze(1).to_broadcast([P, NT, 32]), ALU.mult)
                for _ in due(s, MOE + 1):
                    dve.wait_ge(setup_pe, 1)
                    need(mark(V.tensor_copy(omega[:], ps[:, 4, 0:1])))
                    need(mark(V.tensor_tensor(pw[:, 0:1], omega[:], omega[:], ALU.mult)))
                    V.tensor_scalar(pw[:, 1:2], pw[:, 0:1], 1.0, None, ALU.add)
                    need(mark(V.tensor_scalar(pw[:, 2:3], pw[:, 0:1], -1.0, 1.0, ALU.mult, ALU.add)))
                    need(mark(V.reciprocal(pw[:, 3:4], pw[:, 1:2])))
                    V.tensor_tensor(pw[:, 4:5], pw[:, 2:3], pw[:, 3:4], ALU.mult)
                    need(mark(V.scalar_tensor_tensor(pw[:, 5:6], omega[:], 2.0, pw[:, 3:4], ALU.mult, ALU.mult)))
                    V.memset(cos_t[:, 0:1], 1.0)
                    need(mark(V.memset(sin_t[:, 0:1], 0.0)))
                for k in due(s, MOE + 2, 9):
                    m, c0, n0 = 2 ** k, 4 + 2 * (k % 2), 6 - 2 * (k % 2)
                    c_, s_ = pw[:, c0:c0 + 1], pw[:, c0 + 1:c0 + 2]
                    V.tensor_scalar(turn_t[:, 0:m], sin_t[:, 0:m], s_, None, ALU.mult)
                    need(mark(V.tensor_scalar(rtmp[0][:, 0:m], sin_t[:, 0:m], c_, None, ALU.mult)))
                    V.scalar_tensor_tensor(cos_t[:, m:2 * m], cos_t[:, 0:m], c_, turn_t[:, 0:m],
                                           ALU.mult, ALU.subtract)
                    V.scalar_tensor_tensor(sin_t[:, m:2 * m], cos_t[:, 0:m], s_, rtmp[0][:, 0:m], ALU.mult, ALU.add)
                    need(mark(V.tensor_tensor(pw[:, 8:9], s_, s_, ALU.mult)))
                    V.scalar_tensor_tensor(pw[:, n0:n0 + 1], c_, c_, pw[:, 8:9], ALU.mult, ALU.subtract)
                    need(mark(V.scalar_tensor_tensor(pw[:, n0 + 1:n0 + 2], c_, 2.0, s_, ALU.mult, ALU.mult)))
                for _ in due(s, MOE + 11):
                    V.tensor_copy(turn_t[0:64, :], cos_t[0:64, :])
                    V.tensor_copy(turn_t[64:P, :], sin_t[64:P, :]).then_inc(setup_dve, 1)
                for _ in due(s, MOE + 13):
                    dve.wait_ge(setup_pe, 2)
                    V.tensor_copy(turn[:], b4(5))

            def moments(k, src):
                i = int(k >= 2)
                for t in range(NT):
                    n = mark(V.bn_stats(stats[i][:, t, :], src[:, t, :]))
                need(n)
                for t in range(NT):
                    last = V.bn_aggr(mv[i][:, t, :], stats[i][:, t, :])
                last.then_inc(var_ready[k], 1)

            def normalise(k, src, dst):
                i = int(k >= 2)
                dve.wait_ge(rstd_ready[k], 1)
                for t in range(NT):
                    last = V.tensor_scalar(dst[:, t, :], src[:, t, :], mv[i][:, t, 0:1], rstd[i][:, t:t + 1],
                                           ALU.subtract, ALU.mult)
                last.then_inc(xn_ready[k], 1)

            def pooled_tokens():
                dve.wait_ge(xt_ready[0], 1)
                need(mark(V.tensor_reduce(pool_t[:, 0, :], xt[:].rearrange("p (l c) -> p l c", c=8), AX_X, ALU.add)))
                V.tensor_copy(pool_t[:, 1, :], pool_t[:, 0, :]).then_inc(pooled, 1)

            def pooled_keys_values():
                dve.wait_ge(lat_made, 1)
                V.tensor_scalar(rk_row[:], ps[0:32, 2, 0:NLAT], 0.125, rk_b[:], ALU.mult, ALU.add)
                need(mark(V.scalar_tensor_tensor(rv_row[:], ps[:, 2, NLAT:NLAT + 32], 0.125, rv_b[:],
                                                 ALU.mult, ALU.add)))
                V.tensor_tensor(rk_bd[:], rk_row[:].unsqueeze(1).to_broadcast([32, LH, NLAT]),
                                own_head[:].unsqueeze(2).to_broadcast([32, LH, NLAT]), ALU.mult)
                V.tensor_tensor(rv_bd[:], rv_row[:].rearrange("p (c a d) -> p c a d", c=2, a=2),
                                own_half[:].unsqueeze(1).unsqueeze(3).to_broadcast([P, 2, 2, HD0]),
                                ALU.mult).then_inc(lat_split, 1)

            def shift0(u):
                qb = u // NG0
                dve.wait_ge(a_scores, u + 1)
                both = ps[:, 0:2, :].rearrange("p a (h k) -> p (a h) k", h=2)
                cur = both[:, :, P:2 * P]
                prev = both[:, :, 0:P] if qb else never[:].unsqueeze(1).to_broadcast([P, 4, P])
                need(mark(V.copy_predicated(cur, take_prev[:].unsqueeze(1).to_broadcast([P, 4, P]), prev)))
                if qb:
                    need(mark(V.memset(cur[0:1, :, 0:1], NEG)))
                need(mark(V.tensor_reduce(negmax[:, u % 2, :], cur, AX_X, ALU.max)))
                if u >= 3:
                    dve.wait_ge(a_turned, u - 2)
                V.tensor_tensor(prob[:, u % 3], cur, negmax[:, u % 2, :].unsqueeze(2).to_broadcast([P, 4, P]),
                                ALU.subtract).then_inc(a_shifted, 1)

            def keys_of_block(u):
                if u % 2:
                    return
                dve.wait_ge(a_pt, u + 1)
                if u >= 2:
                    dve.wait_ge(a_pv, u - 1)
                V.tensor_tensor(p_cur[:, u % 2], pt[:, u % 2], key_before[:].unsqueeze(1).to_broadcast([P, 4, P]),
                                ALU.mult).then_inc(a_cur, 1)

            lat3 = lat_p.rearrange("p (t h l) -> p t h l", t=NT, h=LH)
            lat2 = lat_p.rearrange("p (n l) -> p n l", l=NLAT)
            t0 = tmp[0].rearrange("p (n d) -> p n d", d=HD0)
            t3 = tmp[3].rearrange("p (n d) -> p n d", d=HD0)

            def pooled_shift():
                dve.wait_ge(l_scores, 1)
                dve.wait_ge(a_pv, N_UNITS)
                for a in range(2):
                    n = mark(V.tensor_tensor(lat3[:, 2 * a:2 * a + 2],
                                             ps[:, a, :].rearrange("p (t h l) -> p t h l", t=2, h=LH),
                                             lat_mask[:, 2 * a:2 * a + 2].unsqueeze(2).to_broadcast([P, 2, LH, NLAT]),
                                             ALU.add))
                need(n)
                need(mark(V.tensor_reduce(small[:, 2, 0:16], lat2, AX_X, ALU.max)))
                V.tensor_tensor(lat2, lat2, small[:, 2, 0:16].unsqueeze(2).to_broadcast([P, 16, NLAT]),
                                ALU.subtract).then_inc(l_shifted, 1)

            def pooled_sums():
                dve.wait_ge(l_probs, 1)
                need(mark(V.tensor_reduce(small[:, 3, 0:16], lat2, AX_X, ALU.add)))
                need(mark(V.reciprocal(small[:, 4, 0:16], small[:, 3, 0:16])))
                need(mark(V.tensor_tensor(small[:, 5, 0:16].rearrange("p (t h) -> p t h", t=NT),
                                          small[:, 4, 0:16].rearrange("p (t h) -> p t h", t=NT),
                                          lat_valid[:].unsqueeze(2).to_broadcast([P, NT, LH]), ALU.mult)))

            def local_normalised():
                locf = loc[:].rearrange("p t h d -> p (t h) d")
                dve.wait_ge(a_loc, 1)
                need(mark(V.tensor_scalar(loc_r[:], locf[:, :, HD0], 1e-30, None, ALU.max)))
                need(mark(V.reciprocal(small[:, 6, :], loc_r[:])))
                need(mark(V.tensor_tensor(t0, locf[:, :, 0:HD0], small[:, 6, :].unsqueeze(2)
                                          .to_broadcast([P, 64, HD0]), ALU.mult)))
                need(mark(V.tensor_tensor(t3, t0, gl[:].unsqueeze(1).to_broadcast([P, 64, HD0]), ALU.mult)))

            def gate_sum():
                dve.wait_ge(g_rem, 2)
                need(mark(V.tensor_tensor(tmp[3], tmp[3], tmp[1], ALU.add)))
                V.tensor_reduce(small[:, 0, :], t3, AX_X, ALU.add).then_inc(g_sum, 1)
                dve.wait_ge(rem_ready, 1)
                need(mark(V.tensor_tensor(tmp[4], tmp[0], remote, ALU.subtract)))

            def gated():
                dve.wait_ge(g_gate, 1)
                need(mark(V.tensor_scalar(small[:, 7, :], small[:, 1, :], 0.5, 0.5, ALU.mult, ALU.add)))
                need(mark(V.tensor_tensor(tmp[5].rearrange("p (n d) -> p n d", d=HD0),
                                          tmp[4].rearrange("p (n d) -> p n d", d=HD0),
                                          small[:, 7, :].unsqueeze(2).to_broadcast([P, 64, HD0]), ALU.mult)))
                V.tensor_tensor(tmp[3], tmp[5], remote, ALU.add).then_inc(mixed_ready, 1)

            logits = small[:, 0, 0:32].rearrange("p (t e) -> p t e", e=NE)

            def router_shift():
                dve.wait_ge(m_logits, 1)
                need(mark(V.tensor_copy(small[:, 0, 0:32], ps[:, 3, 0:NT * NE])))
                need(mark(V.tensor_reduce(small[:, 3, 0:NT], logits, AX_X, ALU.max)))
                V.tensor_tensor(small[:, 1, 0:32].rearrange("p (t e) -> p t e", e=NE), logits,
                                small[:, 3, 0:NT].unsqueeze(2).to_broadcast([P, NT, NE]),
                                ALU.subtract).then_inc(m_shifted, 1)

            def ranks():
                sh = [P, NT, NE, NE]
                pair = [t_[:, 0:256].rearrange("p (t e f) -> p t e f", t=NT, e=NE) for t_ in tmp[0:2]]
                other, own = logits.unsqueeze(2).to_broadcast(sh), logits.unsqueeze(3).to_broadcast(sh)
                V.tensor_tensor(pair[0], other, own, ALU.is_gt)
                need(mark(V.tensor_tensor(pair[1], other, own, ALU.is_equal)))
                need(mark(V.tensor_tensor(tmp[2][:, 0:256].rearrange("p (t e) -> p t e", t=NT),
                                          tmp[1][:, 0:256].rearrange("p (t e) -> p t e", t=NT),
                                          lower_index[:].unsqueeze(1).to_broadcast([P, NT, 64]), ALU.mult)))
                need(mark(V.tensor_tensor(tmp[3][:, 0:256], tmp[0][:, 0:256], tmp[2][:, 0:256], ALU.add)))
                need(mark(V.tensor_reduce(small[:, 4, 0:32], tmp[3][:, 0:256].rearrange("p (n f) -> p n f", f=NE),
                                          AX_X, ALU.add)))
                need(mark(V.tensor_scalar(small[:, 5, 0:32], small[:, 4, 0:32], 2.0, None, ALU.is_lt)))

            def router_weights():
                dve.wait_ge(m_exp, 1)
                ex = small[:, 2, 0:32].rearrange("p (t e) -> p t e", e=NE)
                need(mark(V.tensor_reduce(small[:, 3, 8:8 + NT], ex, AX_X, ALU.add)))
                n = mark(V.tensor_tensor(small[:, 6, 0:32], small[:, 2, 0:32], small[:, 5, 0:32], ALU.mult))
                need(mark(V.reciprocal(small[:, 3, 16:16 + NT], small[:, 3, 8:8 + NT])))
                need(mark(V.tensor_tensor(w_te[:], small[:, 6, 0:32].rearrange("p (t e) -> p t e", e=NE),
                                          small[:, 3, 16:16 + NT].unsqueeze(2).to_broadcast([P, NT, NE]), ALU.mult)))

            def product(c):
                n_ = E_CHUNKS[c % 3][1]
                dve.wait_ge(m_silu, c + 1)
                dve.wait_ge(m_up, c + 1)
                if c >= 2:
                    dve.wait_ge(m_down, c - 1)
                V.tensor_tensor(hid[0:n_, c % 2, :], sil[0:n_, c % 2, :], ps[0:n_, 1, :], ALU.mult)\
                    .then_inc(m_hid, 1)

            def add_expert(e):
                dve.wait_ge(m_down, 3 * (e + 1))
                if e:
                    dve.wait_ge(m_added, NT * e)
                for t in range(NT):
                    V.scalar_tensor_tensor(x[:, t, :], b4(2 + e % 2)[:, t, :], w_te[:, t, e:e + 1], x[:, t, :],
                                           ALU.mult, ALU.add).then_inc(m_added, 1)

            def front(s):
                for _ in due(s, NORM0):
                    moments(0, x_in)
                for _ in due(s, NORM0 + 1):
                    normalise(0, x_in, xn)
                for u in due(s, QK + 2, 8):
                    dve.wait_ge(low_ready, u + 1)
                    V.scalar_tensor_tensor(qk[:, u, :].bitcast(F32R), ps[:, u % 3, :], bqk[:, u:u + 1],
                                           low[:, u % 2, :], ALU.add, ALU.subtract).then_inc(qk_split, 1)
                for _ in due(s, QK):
                    pooled_tokens()
                for _ in due(s, QK + 9):
                    dve.wait_ge(v0_made, 1)
                    V.tensor_tensor(v0[:, :, :, 0:HD0], b4(3).rearrange("p t (h d) -> p t h d", d=HD0),
                                    v_b[:].rearrange("p (h d) -> p h d", d=HD0).unsqueeze(1)
                                    .to_broadcast([P, NT, NH0, HD0]), ALU.add).then_inc(v0_ready, 1)
                    pooled_keys_values()
                for u in due(s, LOCAL + 1, N_UNITS):
                    shift0(u)
                for u in due(s, LOCAL + 4, N_UNITS):
                    keys_of_block(u)
                for _ in due(s, POOLED + 4):
                    pooled_shift()
                for _ in due(s, LOCAL + 23):
                    dve.wait_ge(a_back, 1)
                    V.tensor_copy(loc[:], ps[:, 0:4, :].rearrange("p t (n s) -> p t n s", s=SLOT)
                                  [:, :, :, 0:HD0 + 1]).then_inc(a_loc, 1)
                for _ in due(s, POOLED + 6):
                    pooled_sums()
                for _ in due(s, LOCAL + 24):
                    local_normalised()
                for _ in due(s, POOLED + 8):
                    dve.wait_ge(l_out, 1)
                    V.tensor_tensor(lat_o[:].rearrange("p t (h d) -> p (t h) d", h=LH),
                                    ps[:, 0, 0:P].rearrange("p (n d) -> p n d", d=HD0),
                                    small[:, 5, 0:16].unsqueeze(2).to_broadcast([P, 16, HD0]), ALU.mult)\
                        .then_inc(l_norm, 1)
                for _ in due(s, LOCAL + 28):
                    dve.wait_ge(l_remote, 1)
                    V.tensor_tensor(tiles(remote), b4(2), rout_b[:].unsqueeze(1).to_broadcast([P, NT, P]),
                                    ALU.add).then_inc(rem_ready, 1)
                for _ in due(s, LOCAL + 29):
                    gate_sum()
                for _ in due(s, LOCAL + 30):
                    gated()
                for _ in due(s, LOCAL + 33):
                    dve.wait_ge(a_proj, 1)
                    V.tensor_tensor(x[:], b4(1), tiles(tmp[2]), ALU.add).then_inc(x1_ready, 1)
                    dve.wait_ge(x1_ready, 1)
                    moments(1, x)
                for _ in due(s, LOCAL + 34):
                    normalise(1, x, xn)
                for c in due(s, MOE + 1, NCH):
                    product(c)
                for _ in due(s, MOE + 1):
                    router_shift()
                for _ in due(s, MOE + 2):
                    ranks()
                for _ in due(s, MOE + 3):
                    router_weights()
                for e in range(NE):
                    for _ in due(s, MOE + 3 * e + 5):
                        add_expert(e)

            def h8(ap):
                return ap.rearrange("p (h k) -> p h k", h=8)

            def parts(l, u):
                i, t = u // 4, u % 4
                src = ps[:, 4 + u % 3, :]
                c_part, s_part = rtmp[u % 2][:], quad[:, 2 + u % 2, :]
                dve.wait_ge(d["sq"], at(l, "sq", u + 1))
                if u >= 2:
                    dve.wait_ge(d["rot"], at(l, "rot", u - 1))
                V.tensor_tensor(h8(c_part), h8(src), rope_c[l][i][:, t, :].unsqueeze(1)
                                .to_broadcast([P, 8, W]), ALU.mult)
                for a, c in ((0, 32), (32, 0)):
                    V.tensor_tensor(h8(s_part)[:, :, a:a + 32], h8(src)[:, :, c:c + 32],
                                    rope_s[l][i][:, t, a:a + 32].unsqueeze(1).to_broadcast([P, 8, 32]), ALU.mult)
                V.tensor_reduce(ss[:, 8 * u:8 * u + 8], h8(quad[:, u % 2, :]), AX_X, ALU.add)\
                    .then_inc(d["parts"], 1)

            def inverse_norms(l, i):
                c = slice(32 * i, 32 * i + 32)
                dve.wait_ge(d["parts"], at(l, "parts", 4 * i + 4))
                need(mark(V.tensor_scalar(nw[:, 0, c], ss[:, c], 1e-24, None, ALU.max)))
                need(mark(V.tensor_scalar(nw[:, 1, c].bitcast(I32), nw[:, 0, c].bitcast(I32), 1, None,
                                          ALU.logical_shift_right)))
                need(mark(V.tensor_scalar(nw[:, 2, c].bitcast(I32), nw[:, 1, c].bitcast(I32), -1.0,
                                          float(0x5f3759df), ALU.mult, ALU.add)))
                for k in range(3):
                    old, new = nw[:, 2 - k % 2, c], nw[:, 1 + k % 2, c]
                    need(mark(V.tensor_tensor(nw[:, 3, c], old, old, ALU.mult)))
                    need(mark(V.scalar_tensor_tensor(nw[:, 4, c], nw[:, 3, c], -0.5, nw[:, 0, c],
                                                     ALU.mult, ALU.mult)))
                    need(mark(V.scalar_tensor_tensor(new, nw[:, 4, c], 1.5, old, ALU.add, ALU.mult)))

            def normed(l, u):
                dve.wait_ge(d["rot"], at(l, "rot", u + 1))
                q = h8(qr[:, u % 4, :])
                V.tensor_tensor(q, q, nw[:, 1, 8 * u:8 * u + 8].unsqueeze(2).to_broadcast([P, 8, W]),
                                ALU.mult).then_inc(d["normed"], 1)

            def n4(ap):
                return ap.rearrange("p (n k) -> p n k", n=NP)

            def shift(l, w):
                kind = 0 if w % 2 else (1 if w else 2)
                dve.wait_ge(d["scores"], at(l, "scores", w + 1))
                if w >= 4:
                    dve.wait_ge(d["pturn"], at(l, "pturn", w - 3))
                need(mark(V.tensor_tensor(n4(quad[:, w % 4, :]), n4(ps[:, 4 + w % 2, :]),
                                          win_mask[:, kind, :].unsqueeze(1).to_broadcast([P, NP, P]), ALU.add)))
                need(mark(V.tensor_reduce(wmax[:, w % 4, 0:4], n4(quad[:, w % 4, :]), AX_X, ALU.max)))
                V.tensor_scalar(wmax[:, w % 4, 4:8], wmax[:, w % 4, 0:4], -QK_SCALE, None,
                                ALU.mult).then_inc(d["shifted"], 1)

            def sums(l, w):
                dve.wait_ge(d["probs"], at(l, "probs", w + 1))
                V.reciprocal(wmax[:, w % 4, 12:16], wmax[:, w % 4, 8:12]).then_inc(d["wsum"], 1)

            def rear(s):
                for _ in due(s, SSM):
                    moments(2, x)
                for _ in due(s, SSM + 1):
                    normalise(2, x, tiles(rtmp[0][:]))
                for _ in due(s, SSM + 4):
                    dve.wait_ge(s_in, 1)
                    V.tensor_tensor(tiles(quad[:, 0]), b4(5), turn[:], ALU.mult).then_inc(s_turned, 1)
                for _ in due(s, SSM + 6):
                    dve.wait_ge(s_sum, 1)
                    V.tensor_tensor(quad[:, 1], ps[:, 6, :], turn_t[:], ALU.mult).then_inc(s_state, 1)
                for _ in due(s, SSM + 8):
                    dve.wait_ge(s_skip, 1)
                    dve.wait_ge(s_out, 1)
                    V.tensor_tensor(xr[:], b4(7), tiles(quad[:, 3]), ALU.add).then_inc(x3_ready, 1)
                    dve.wait_ge(x3_ready, 1)
                    moments(5, xr)
                for _ in due(s, SSM + 9):
                    dve.wait_ge(y_free, 1)
                    normalise(5, xr, y)
                for l in range(2):
                    q = s - LAYER[l]
                    for i in due(q, PROJ + 5) or due(q, PROJ + 9):
                        inverse_norms(l, int(q == PROJ + 9))
                    for u in due(q, PROJ + 5, 8):
                        normed(l, u)
                    for u in due(q, PROJ + 1, 8):
                        parts(l, u)
                    for w in due(q, WINDOWS + 1, NW):
                        shift(l, w)
                    for w in due(q, WINDOWS + 3, NW):
                        sums(l, w)
                    for _ in due(q, FF + 1):
                        dve.wait_ge(d["wo"], at(l, "wo", 1))
                        if l == 0:
                            dve.wait_ge(xn_ready[5], 1)
                        else:
                            dve.wait_ge(d["y_out"], 1)
                        V.tensor_tensor(y[:], y[:], b4(4), ALU.add).then_inc(d["y_mid"], 1)
                    for _ in due(q, FF + 3):
                        dve.wait_ge(d["shift2"], at(l, "shift2", 32))
                        dve.wait_ge(d["left2"], at(l, "left2", 1))
                        moments(3 + l, shifted)
                    for _ in due(q, FF + 4):
                        normalise(3 + l, shifted, tiles(rtmp[0][:]))
                    for c in due(q, FF + 7, 3):
                        n = H_CHUNKS[c][1]
                        dve.wait_ge(d["gelu"], at(l, "gelu", c + 1))
                        V.scalar_tensor_tensor(quad[0:n, c, :], ps[0:n, GA_BANKS[c][0], :], b1a[l][0:n, c:c + 1],
                                               gel[0:n, c, :], ALU.add, ALU.mult).then_inc(d["mlp"], 1)
                    for _ in due(q, FF + 10):
                        need(mark(V.tensor_tensor(tiles(ht[:]), y[:],
                                                  b2[l][:].unsqueeze(1).to_broadcast([P, NT, P]), ALU.add)))
                    for _ in due(q, LAYER_STEPS):
                        dve.wait_ge(d["w2"], at(l, "w2", 1))
                        V.tensor_tensor(y[:], tiles(ht[:]), b4(4), ALU.add).then_inc(d["y_out"], 1)
                        if l == 1:
                            dve.wait_ge(d["y_out"], 2)
                            V.tensor_tensor(y[:], xr[:], y[:], ALU.add).then_inc(x4_ready, 1)

            run_turns(dve, front, rear, prepare, start_turn)


def constants():
    f = np.float32
    p = np.arange(P)
    c = {"ident": np.eye(P, dtype=f)}
    c["take_prev"] = (p[None, :] >= p[:, None]).astype(np.int32)
    c["key_before"] = (p[:, None] < p[None, :]).astype(f)
    c["key_after"] = (p[:, None] >= p[None, :]).astype(f)
    tok = np.arange(S).reshape(NT, P)
    lat = np.where(np.arange(NLAT)[None, None, :] < (tok // 8)[:, :, None], 0.0, NEG).astype(f)
    c["lat_mask"] = np.ascontiguousarray(lat.transpose(1, 0, 2))
    c["lat_valid"] = np.ascontiguousarray((tok >= 8).astype(f).T)
    c["own_head"] = (np.arange(32)[:, None] // 8 == np.arange(LH)[None, :]).astype(f)
    c["own_half"] = (p[:, None] // 64 == np.arange(2)[None, :]).astype(f)
    low = np.zeros((P, 8), f)
    row = p % SLOT
    low[(row >= 16) & (row < 24), 0:4] = 1.0
    low[(row >= 8) & (row < 16), 4:8] = 1.0
    c["low_rows"] = low
    e = np.arange(NE)
    c["lower_index"] = np.ascontiguousarray(np.broadcast_to((e[None, :] < e[:, None]).astype(f).reshape(1, -1), (P, 64)))
    j, k = np.arange(32)[:, None].astype(np.float64), (np.arange(P) % 64)[None, :]
    c["omega_w"] = (-(np.sin(2 * np.pi * (j + 1) * k / 64) + (j >= 1) * np.sin(2 * np.pi * j * k / 64))).astype(f)
    c["up_to"] = (p[:, None] <= np.arange(S)[None, :]).astype(f)
    half = np.arange(0, W, 2, dtype=f)
    inv = f(1.0) / f(10000.0) ** (half / f(W))
    t = np.arange(S, dtype=f)
    fr = (t[:, None] * inv[None, :]).astype(f)
    fr = np.concatenate([fr, fr], -1)
    base = (half + f(0.4) * W) / f(1.4 * W)
    power = (t - S // 2) / f(32)
    scale = base[None, :].astype(f) ** power[:, None].astype(f)
    scale = np.concatenate([scale, scale], -1)
    sign = np.where(np.arange(W) < 32, -1.0, 1.0)
    tabs = [np.cos(fr) * scale, np.sin(fr) * scale * sign, np.cos(fr) / scale, np.sin(fr) / scale * sign]
    for i, a in enumerate(tabs):
        c[f"rope{i}"] = np.ascontiguousarray(a.astype(f).reshape(NT, P, W).transpose(1, 0, 2))
    q, kk = (p % W)[:, None], np.arange(W)[None, :]
    cur, prev = kk <= q, kk >= q
    no = np.zeros_like(cur)
    m = np.stack([np.concatenate([prev, cur], 1), np.concatenate([cur, prev], 1), np.concatenate([cur, no], 1)], 1)
    c["win_mask"] = np.where(m, 0.0, NEG).astype(f)
    return c


def layout(a):
    g = {n: np.asarray(v) for n, v in a.items()}
    o = {"x": np.concatenate([g["L0_attn_x"], np.zeros_like(g["L0_attn_x"][:1])])}
    qkv_w, qkv_b = g["L0_attn_qkv_w"], g["L0_attn_qkv_b"]
    wqk = np.zeros((P, 8, P), np.float32)
    bqk = np.zeros((P, 8), np.float32)
    for i in range(2):
        for h in range(NH0):
            grp, t = h // 4, h % 4
            for r in range(3):
                cols = slice(SLOT * grp + 8 * r, SLOT * grp + 8 * r + 8)
                src = slice(i * P + 8 * h, i * P + 8 * h + 8)
                wqk[:, 4 * i + t, cols] = qkv_w[:, src]
                bqk[cols, 4 * i + t] = qkv_b[src]
    o["wqk"], o["bqk"] = wqk, bqk
    o["wv0"], o["v_b"] = qkv_w[:, 2 * P:], qkv_b[2 * P:]
    o["rq_w"], o["rq_b"] = g["L0_attn_rq_w"], g["L0_attn_rq_b"][:, None]
    o["rk_w"], o["rv_w"] = g["L0_attn_rkv_w"][:, :32], g["L0_attn_rkv_w"][:, 32:]
    o["rk_b"], o["rv_b"] = g["L0_attn_rkv_b"][:32, None], g["L0_attn_rkv_b"][32:]
    o["rout_w"], o["rout_b"] = g["L0_attn_rout_w"], g["L0_attn_rout_b"]
    o["out_w"], o["out_b"] = g["L0_attn_out_w"], g["L0_attn_out_b"]
    o["gl"], o["gr"] = g["L0_attn_gl_w"][:, 0], g["L0_attn_gr_w"][:, 0]
    o["router"] = g["L0_ffn_router_w"].T
    o["gate_w"] = g["L0_ffn_gate_w"].reshape(NE * FI, P).T
    o["up_w"] = g["L0_ffn_up_w"].reshape(NE * FI, P).T
    down = np.zeros((P, NCH, P), np.float32)
    for e in range(NE):
        for i, (lo, n) in enumerate(E_CHUNKS):
            down[0:n, 3 * e + i, :] = g["L0_ffn_down_w"][e, :, lo:lo + n].T
    o["down_w"] = down
    o["bw2"] = np.concatenate([g["L1_attn_B_w"].T] * 2, 1)
    o["cw2"] = np.concatenate([g["L1_attn_C_w"].T] * 2, 0)
    o["a_col"], o["d_row"] = g["L1_attn_a_params"][:, None], g["L1_attn_D"]
    for l in range(2):
        o[f"wqkv{l}"] = g["L1_ffn_wqkv"][l].reshape(P, 3, INNER)
        o[f"wo{l}"] = g["L1_ffn_wo"][l].reshape(NP, P, P).transpose(1, 0, 2)
        o[f"qk_s{l}0"], o[f"qk_s{l}1"] = g["L1_ffn_q_scale"][l], g["L1_ffn_k_scale"][l]
        o[f"w1_{l}"] = g["L1_ffn_w1"][l]
        w2, b1 = np.zeros((P, 3, P), np.float32), np.zeros((2, P, 3), np.float32)
        for i, (lo, n) in enumerate(H_CHUNKS):
            w2[0:n, i, :] = g["L1_ffn_w2"][l, lo:lo + n, :]
            for j in range(2):
                b1[j, 0:n, i] = g["L1_ffn_b1"][l, j * HID + lo:j * HID + lo + n]
        o[f"w2_{l}"], o[f"b1a{l}"], o[f"b1g{l}"] = w2, b1[0], b1[1]
        o[f"ln_g{l}"], o[f"ln_b{l}"] = g["L1_ffn_ln_g"][l][:, None], g["L1_ffn_ln_b"][l][:, None]
        o[f"b2_{l}"] = g["L1_ffn_b2"][l]
    return o


def kernel(**inputs):
    import concourse.bacc as _bacc
    from concourse.bass_utils import run_bass_kernel_spmd as _run

    nc = _bacc.Bacc("TRN2", target_bir_lowering=False, num_devices=1)
    arrays = {f"in_{n}": np.ascontiguousarray(v) for n, v in {**layout(inputs), **constants()}.items()}
    io = {n[3:]: nc.dram_tensor(n, v.shape, mybir.dt.from_np(v.dtype), kind="ExternalInput").ap()
          for n, v in arrays.items()}
    shape = np.shape(inputs["L0_attn_x"])
    out = nc.dram_tensor("out", shape, F32, kind="ExternalOutput").ap()
    build(nc, io, shape[0], out)
    r = _run(nc, [arrays], core_ids=[0])
    return r.results[0]["out"]
```
